# Optimizing a Trainium2 kernel written in Bass

```python
import numpy as np
import jax
import jax.numpy as jnp

def _softmax(x, axis=-1):
    return jax.nn.softmax(x, axis=axis)

def _gelu(x):
    return jax.nn.gelu(x, approximate=True)

def _silu(x):
    return jax.nn.silu(x)

def _sigmoid(x):
    return jax.nn.sigmoid(x)

def _layernorm(x, axis=-1, eps=1e-05):
    m = jnp.mean(x, axis=axis, keepdims=True)
    v = jnp.var(x, axis=axis, keepdims=True)
    return (x - m) / jnp.sqrt(v + eps)

def _scatter_add(tgt, idx, src, axis=0):
    return tgt.at[idx].add(src)

def _segment_sum(src, seg, n):
    return jax.ops.segment_sum(src, seg, n)
kernel_name = 'mk_early_fusion_d1_tok_img1024_r4_90e978'

def setup_inputs(seed: int=0):
    np.random.seed(seed)
    _w = jnp.asarray

    def _rec_inputs():
        import jax
        import jax.numpy as jnp
        _rk = jax.random.key(seed)
        x = -0.00016672 + 0.999947 * jax.random.normal(jax.random.fold_in(_rk, 1), (64, 3, 96, 96), jnp.float32)
        txt = 0.434251 + 1.14597 * jax.random.normal(jax.random.fold_in(_rk, 2), (64, 128, 256), jnp.float32)
        return (x, txt)
    x, txt = _rec_inputs()

    def _L0_tok_setup():
        import jax, jax.numpy as jnp
        import numpy as np
        DIM = 256
        IMG = 96
        P = 16
        C = 3
        TEMP = 10000.0
        EPS = 1e-05
        PATCH_DIM = C * P * P
        HP = IMG // P

        def layernorm(x, gamma, beta):
            mu = jnp.mean(x, axis=-1, keepdims=True)
            var = jnp.var(x, axis=-1, keepdims=True)
            return (x - mu) * jax.lax.rsqrt(var + EPS) * gamma + beta

        def posemb_sincos_2d(h, w, dim, dtype):
            y, x = jnp.meshgrid(jnp.arange(h), jnp.arange(w), indexing='ij')
            omega = jnp.arange(dim // 4, dtype=jnp.float32) / (dim // 4 - 1)
            omega = 1.0 / TEMP ** omega
            y = y.reshape(-1)[:, None] * omega[None, :]
            x = x.reshape(-1)[:, None] * omega[None, :]
            pe = jnp.concatenate((jnp.sin(x), jnp.cos(x), jnp.sin(y), jnp.cos(y)), axis=1)
            return pe.astype(dtype)
        key = jax.random.key(seed)
        ks = jax.random.split(key, 8)
        B = 64
        img = jax.random.normal(ks[0], (B, C, IMG, IMG), dtype=jnp.float32)
        cls_token = jax.random.normal(ks[1], (1, 1, DIM), dtype=jnp.float32)
        cls_pos_embedding = jax.random.normal(ks[2], (1, 1, DIM), dtype=jnp.float32)
        ln1_g = jnp.ones((PATCH_DIM,), jnp.float32)
        ln1_b = jnp.zeros((PATCH_DIM,), jnp.float32)
        W = jax.random.normal(ks[3], (PATCH_DIM, DIM), dtype=jnp.float32) / np.sqrt(PATCH_DIM)
        bias = jnp.zeros((DIM,), jnp.float32)
        ln2_g = jnp.ones((DIM,), jnp.float32)
        ln2_b = jnp.zeros((DIM,), jnp.float32)
        return {'img': img, 'cls_token': cls_token, 'cls_pos_embedding': cls_pos_embedding, 'ln1_g': ln1_g, 'ln1_b': ln1_b, 'W': W, 'bias': bias, 'ln2_g': ln2_g, 'ln2_b': ln2_b}
    _L0_tok_all = _L0_tok_setup()
    _L0_tok_in = {k: v for k, v in _L0_tok_all.items() if k in ('cls_token', 'cls_pos_embedding', 'ln1_g', 'ln1_b', 'W', 'bias', 'ln2_g', 'ln2_b')}
    del _L0_tok_all

    def _L0_attn_setup():
        import jax, jax.numpy as jnp
        import numpy as np
        import math
        B, S, D = (4, 512, 256)
        H = 16
        HD = D // H
        DL = 64
        LAMBDA_DECAY = 0.01
        key = jax.random.key(seed)
        ks = jax.random.split(key, 8)
        sc = lambda fan_in: 1.0 / math.sqrt(fan_in)
        return {'x': jax.random.normal(ks[0], (B, S, D), dtype=jnp.float32), 'W_q': jax.random.normal(ks[1], (D, D), dtype=jnp.float32) * sc(D), 'W_k': jax.random.normal(ks[2], (D, D), dtype=jnp.float32) * sc(D), 'W_v': jax.random.normal(ks[3], (D, D), dtype=jnp.float32) * sc(D), 'W_o': jax.random.normal(ks[4], (D, D), dtype=jnp.float32) * sc(D), 'W_down_kv': jax.random.normal(ks[5], (D, DL), dtype=jnp.float32) * sc(D), 'W_up_k': jax.random.normal(ks[6], (DL, D), dtype=jnp.float32) * sc(DL), 'W_up_v': jax.random.normal(ks[7], (DL, D), dtype=jnp.float32) * sc(DL)}
    _L0_attn_all = _L0_attn_setup()
    _L0_attn_in = {k: v for k, v in _L0_attn_all.items() if k in ('W_q', 'W_k', 'W_v', 'W_o', 'W_down_kv', 'W_up_k', 'W_up_v')}
    del _L0_attn_all

    def _L0_ffn_setup():
        import jax, jax.numpy as jnp
        import numpy as np
        D = 256
        HD = 128
        EA = 8
        KA = 2
        EF = 16
        KF = 2
        FH = 128
        MAXP = 64
        B, S = (4, 256)
        EPS = 1e-05

        def _layer_norm(x, w, b):
            mu = x.mean(-1, keepdims=True)
            var = ((x - mu) ** 2).mean(-1, keepdims=True)
            return (x - mu) * jax.lax.rsqrt(var + EPS) * w + b

        def _topk_gates(logits, k):
            top_vals, top_idx = jax.lax.top_k(logits, k)
            g = jax.nn.softmax(top_vals, axis=-1)
            onehot = jax.nn.one_hot(top_idx, logits.shape[-1], dtype=logits.dtype)
            return jnp.einsum('...k,...ke->...e', g, onehot)

        def _moa(x, gate_w, q_w, q_b, k_w, k_b, v_w, v_b, o_w, o_b, rel_table):
            S_ = x.shape[1]
            gates = _topk_gates(x @ gate_w, KA)
            q = (jnp.einsum('bsd,edh->bseh', x, q_w) + q_b) * HD ** (-0.5)
            k = x @ k_w + k_b
            v = x @ v_w + v_b
            scores = jnp.einsum('bqeh,bkh->beqk', q, k)
            rel_s = jnp.einsum('bqeh,rh->beqr', q, rel_table)
            pos = jnp.arange(S_)
            rel_idx = jnp.clip(pos[None, :] - pos[:, None], -MAXP, MAXP) + MAXP
            scores = scores + jnp.take_along_axis(rel_s, rel_idx[None, None], axis=-1)
            p = jax.nn.softmax(scores, axis=-1)
            ctx = jnp.einsum('beqk,bkh->bqeh', p, v)
            out = jnp.einsum('bqeh,ehd,bqe->bqd', ctx, o_w, gates)
            return out + jnp.einsum('bqe,ed->bqd', gates, o_b)

        def _moe_ffn(x, gate_w, w1, b1, w2, b2):
            gates = _topk_gates(x @ gate_w, KF)
            h = jax.nn.relu(jnp.einsum('bsd,edh->bseh', x, w1) + b1)
            out = jnp.einsum('bseh,ehd,bse->bsd', h, w2, gates)
            return out + jnp.einsum('bse,ed->bsd', gates, b2)
        key = jax.random.key(seed)
        ks = jax.random.split(key, 12)
        r = lambda i, shape, scale=0.02: jax.random.normal(ks[i], shape, jnp.float32) * scale
        return {'src': jax.random.normal(ks[0], (B, S, D), jnp.float32), 'ln1_w': jnp.ones((D,), jnp.float32), 'ln1_b': jnp.zeros((D,), jnp.float32), 'ln2_w': jnp.ones((D,), jnp.float32), 'ln2_b': jnp.zeros((D,), jnp.float32), 'attn_gate_w': r(1, (D, EA)), 'q_w': r(2, (EA, D, HD)), 'q_b': jnp.zeros((EA, HD), jnp.float32), 'k_w': r(3, (D, HD)), 'k_b': jnp.zeros((HD,), jnp.float32), 'v_w': r(4, (D, HD)), 'v_b': jnp.zeros((HD,), jnp.float32), 'o_w': r(5, (EA, HD, D)), 'o_b': jnp.zeros((EA, D), jnp.float32), 'rel_table': r(6, (2 * MAXP + 1, HD)), 'ff_gate_w': r(7, (D, EF)), 'ff_w1': r(8, (EF, D, FH)), 'ff_b1': jnp.zeros((EF, FH), jnp.float32), 'ff_w2': r(9, (EF, FH, D)), 'ff_b2': jnp.zeros((EF, D), jnp.float32)}
    _L0_ffn_all = _L0_ffn_setup()
    _L0_ffn_in = {k: v for k, v in _L0_ffn_all.items() if k in ('ln1_w', 'ln1_b', 'ln2_w', 'ln2_b', 'attn_gate_w', 'q_w', 'q_b', 'k_w', 'k_b', 'v_w', 'v_b', 'o_w', 'o_b', 'rel_table', 'ff_gate_w', 'ff_w1', 'ff_b1', 'ff_w2', 'ff_b2')}
    del _L0_ffn_all
    return {'x': x, 'txt': txt, 'L0_tok_cls_token': _L0_tok_in['cls_token'], 'L0_tok_cls_pos_embedding': _L0_tok_in['cls_pos_embedding'], 'L0_tok_ln1_g': _L0_tok_in['ln1_g'], 'L0_tok_ln1_b': _L0_tok_in['ln1_b'], 'L0_tok_W': _L0_tok_in['W'], 'L0_tok_bias': _L0_tok_in['bias'], 'L0_tok_ln2_g': _L0_tok_in['ln2_g'], 'L0_tok_ln2_b': _L0_tok_in['ln2_b'], 'L0_attn_W_q': _L0_attn_in['W_q'], 'L0_attn_W_k': _L0_attn_in['W_k'], 'L0_attn_W_v': _L0_attn_in['W_v'], 'L0_attn_W_o': _L0_attn_in['W_o'], 'L0_attn_W_down_kv': _L0_attn_in['W_down_kv'], 'L0_attn_W_up_k': _L0_attn_in['W_up_k'], 'L0_attn_W_up_v': _L0_attn_in['W_up_v'], 'L0_ffn_ln1_w': _L0_ffn_in['ln1_w'], 'L0_ffn_ln1_b': _L0_ffn_in['ln1_b'], 'L0_ffn_ln2_w': _L0_ffn_in['ln2_w'], 'L0_ffn_ln2_b': _L0_ffn_in['ln2_b'], 'L0_ffn_attn_gate_w': _L0_ffn_in['attn_gate_w'], 'L0_ffn_q_w': _L0_ffn_in['q_w'], 'L0_ffn_q_b': _L0_ffn_in['q_b'], 'L0_ffn_k_w': _L0_ffn_in['k_w'], 'L0_ffn_k_b': _L0_ffn_in['k_b'], 'L0_ffn_v_w': _L0_ffn_in['v_w'], 'L0_ffn_v_b': _L0_ffn_in['v_b'], 'L0_ffn_o_w': _L0_ffn_in['o_w'], 'L0_ffn_o_b': _L0_ffn_in['o_b'], 'L0_ffn_rel_table': _L0_ffn_in['rel_table'], 'L0_ffn_ff_gate_w': _L0_ffn_in['ff_gate_w'], 'L0_ffn_ff_w1': _L0_ffn_in['ff_w1'], 'L0_ffn_ff_b1': _L0_ffn_in['ff_b1'], 'L0_ffn_ff_w2': _L0_ffn_in['ff_w2'], 'L0_ffn_ff_b2': _L0_ffn_in['ff_b2']}

def reference(x, txt, L0_tok_cls_token, L0_tok_cls_pos_embedding, L0_tok_ln1_g, L0_tok_ln1_b, L0_tok_W, L0_tok_bias, L0_tok_ln2_g, L0_tok_ln2_b, L0_attn_W_q, L0_attn_W_k, L0_attn_W_v, L0_attn_W_o, L0_attn_W_down_kv, L0_attn_W_up_k, L0_attn_W_up_v, L0_ffn_ln1_w, L0_ffn_ln1_b, L0_ffn_ln2_w, L0_ffn_ln2_b, L0_ffn_attn_gate_w, L0_ffn_q_w, L0_ffn_q_b, L0_ffn_k_w, L0_ffn_k_b, L0_ffn_v_w, L0_ffn_v_b, L0_ffn_o_w, L0_ffn_o_b, L0_ffn_rel_table, L0_ffn_ff_gate_w, L0_ffn_ff_w1, L0_ffn_ff_b1, L0_ffn_ff_w2, L0_ffn_ff_b2):
    import jax
    import jax.numpy as jnp

    def _L0_tok_ref(img, cls_token, cls_pos_embedding, ln1_g, ln1_b, W, bias, ln2_g, ln2_b):
        import jax, jax.numpy as jnp
        import numpy as np
        DIM = 256
        IMG = 96
        P = 16
        C = 3
        TEMP = 10000.0
        EPS = 1e-05
        PATCH_DIM = C * P * P
        HP = IMG // P

        def layernorm(x, gamma, beta):
            mu = jnp.mean(x, axis=-1, keepdims=True)
            var = jnp.var(x, axis=-1, keepdims=True)
            return (x - mu) * jax.lax.rsqrt(var + EPS) * gamma + beta

        def posemb_sincos_2d(h, w, dim, dtype):
            y, x = jnp.meshgrid(jnp.arange(h), jnp.arange(w), indexing='ij')
            omega = jnp.arange(dim // 4, dtype=jnp.float32) / (dim // 4 - 1)
            omega = 1.0 / TEMP ** omega
            y = y.reshape(-1)[:, None] * omega[None, :]
            x = x.reshape(-1)[:, None] * omega[None, :]
            pe = jnp.concatenate((jnp.sin(x), jnp.cos(x), jnp.sin(y), jnp.cos(y)), axis=1)
            return pe.astype(dtype)
        b = img.shape[0]
        x = img.reshape(b, C, HP, P, HP, P)
        x = jnp.transpose(x, (0, 2, 4, 3, 5, 1))
        x = x.reshape(b, HP, HP, PATCH_DIM)
        x = layernorm(x, ln1_g, ln1_b)
        x = jnp.einsum('bhwp,pd->bhwd', x, W) + bias
        x = layernorm(x, ln2_g, ln2_b)
        pe = posemb_sincos_2d(HP, HP, DIM, x.dtype)
        x = x.reshape(b, HP * HP, DIM) + pe[None]
        cls_tokens = jnp.broadcast_to(cls_token + cls_pos_embedding, (b, 1, DIM))
        return jnp.concatenate((cls_tokens, x), axis=1)

    def _L0_attn_ref(x, W_q, W_k, W_v, W_o, W_down_kv, W_up_k, W_up_v):
        import jax, jax.numpy as jnp
        import numpy as np
        import math
        B, S, D = (4, 512, 256)
        H = 16
        HD = D // H
        DL = 64
        LAMBDA_DECAY = 0.01
        b, s, d = x.shape
        q = x @ W_q
        k = x @ W_k
        v = x @ W_v
        latent_kv = (k + v) @ W_down_kv
        k_rec = (latent_kv @ W_up_k).reshape(b, s, H, HD).transpose(0, 2, 1, 3)
        v_rec = (latent_kv @ W_up_v).reshape(b, s, H, HD).transpose(0, 2, 1, 3)
        qh = q.reshape(b, s, H, HD).transpose(0, 2, 1, 3)
        scores = jnp.einsum('bhqd,bhkd->bhqk', qh, k_rec) / math.sqrt(d)
        t = jnp.arange(s, dtype=jnp.float32)
        decay = jnp.exp(-LAMBDA_DECAY * jnp.abs(t[:, None] - t[None, :]))
        scores = scores * decay[None, None, :, :]
        attn = jax.nn.softmax(scores, axis=-1)
        out = jnp.einsum('bhqk,bhkd->bhqd', attn, v_rec)
        out = out.transpose(0, 2, 1, 3).reshape(b, s, d)
        return out @ W_o

    def _L0_ffn_ref(src, ln1_w, ln1_b, ln2_w, ln2_b, attn_gate_w, q_w, q_b, k_w, k_b, v_w, v_b, o_w, o_b, rel_table, ff_gate_w, ff_w1, ff_b1, ff_w2, ff_b2):
        import jax, jax.numpy as jnp
        import numpy as np
        D = 256
        HD = 128
        EA = 8
        KA = 2
        EF = 16
        KF = 2
        FH = 128
        MAXP = 64
        B, S = (4, 256)
        EPS = 1e-05

        def _layer_norm(x, w, b):
            mu = x.mean(-1, keepdims=True)
            var = ((x - mu) ** 2).mean(-1, keepdims=True)
            return (x - mu) * jax.lax.rsqrt(var + EPS) * w + b

        def _topk_gates(logits, k):
            top_vals, top_idx = jax.lax.top_k(logits, k)
            g = jax.nn.softmax(top_vals, axis=-1)
            onehot = jax.nn.one_hot(top_idx, logits.shape[-1], dtype=logits.dtype)
            return jnp.einsum('...k,...ke->...e', g, onehot)

        def _moa(x, gate_w, q_w, q_b, k_w, k_b, v_w, v_b, o_w, o_b, rel_table):
            S_ = x.shape[1]
            gates = _topk_gates(x @ gate_w, KA)
            q = (jnp.einsum('bsd,edh->bseh', x, q_w) + q_b) * HD ** (-0.5)
            k = x @ k_w + k_b
            v = x @ v_w + v_b
            scores = jnp.einsum('bqeh,bkh->beqk', q, k)
            rel_s = jnp.einsum('bqeh,rh->beqr', q, rel_table)
            pos = jnp.arange(S_)
            rel_idx = jnp.clip(pos[None, :] - pos[:, None], -MAXP, MAXP) + MAXP
            scores = scores + jnp.take_along_axis(rel_s, rel_idx[None, None], axis=-1)
            p = jax.nn.softmax(scores, axis=-1)
            ctx = jnp.einsum('beqk,bkh->bqeh', p, v)
            out = jnp.einsum('bqeh,ehd,bqe->bqd', ctx, o_w, gates)
            return out + jnp.einsum('bqe,ed->bqd', gates, o_b)

        def _moe_ffn(x, gate_w, w1, b1, w2, b2):
            gates = _topk_gates(x @ gate_w, KF)
            h = jax.nn.relu(jnp.einsum('bsd,edh->bseh', x, w1) + b1)
            out = jnp.einsum('bseh,ehd,bse->bsd', h, w2, gates)
            return out + jnp.einsum('bse,ed->bsd', gates, b2)
        res = src
        xn = _layer_norm(src, ln1_w, ln1_b)
        x = res + _moa(xn, attn_gate_w, q_w, q_b, k_w, k_b, v_w, v_b, o_w, o_b, rel_table)
        res = x
        xn = _layer_norm(x, ln2_w, ln2_b)
        return res + _moe_ffn(xn, ff_gate_w, ff_w1, ff_b1, ff_w2, ff_b2)
    h = _L0_tok_ref(x, L0_tok_cls_token, L0_tok_cls_pos_embedding, L0_tok_ln1_g, L0_tok_ln1_b, L0_tok_W, L0_tok_bias, L0_tok_ln2_g, L0_tok_ln2_b)
    h = jnp.concatenate([h, txt], axis=1)
    h = h + _L0_attn_ref(_layernorm(h, axis=-1), L0_attn_W_q, L0_attn_W_k, L0_attn_W_v, L0_attn_W_o, L0_attn_W_down_kv, L0_attn_W_up_k, L0_attn_W_up_v)
    h = h + _L0_ffn_ref(_layernorm(h, axis=-1), L0_ffn_ln1_w, L0_ffn_ln1_b, L0_ffn_ln2_w, L0_ffn_ln2_b, L0_ffn_attn_gate_w, L0_ffn_q_w, L0_ffn_q_b, L0_ffn_k_w, L0_ffn_k_b, L0_ffn_v_w, L0_ffn_v_b, L0_ffn_o_w, L0_ffn_o_b, L0_ffn_rel_table, L0_ffn_ff_gate_w, L0_ffn_ff_w1, L0_ffn_ff_b1, L0_ffn_ff_w2, L0_ffn_ff_b2)
    return h

_drawn_inputs = setup_inputs


def setup_inputs(seed=0):
    import zlib

    import numpy as np

    out = dict(_drawn_inputs(seed))
    spreads = {'L0_tok_ln1_g': (1.0, 0.2),
     'L0_tok_ln1_b': (0.0, 0.1),
     'L0_tok_bias': (0.0, 0.1),
     'L0_tok_ln2_g': (1.0, 0.2),
     'L0_tok_ln2_b': (0.0, 0.1),
     'L0_ffn_ln1_w': (1.0, 0.6),
     'L0_ffn_ln1_b': (0.0, 0.736),
     'L0_ffn_ln2_w': (1.0, 0.6),
     'L0_ffn_ln2_b': (0.0, 0.619),
     'L0_ffn_q_b': (0.0, 0.8),
     'L0_ffn_k_b': (0.0, 2.0),
     'L0_ffn_v_b': (0.0, 0.8),
     'L0_ffn_o_b': (0.0, 0.289),
     'L0_ffn_ff_b1': (0.0, 0.8),
     'L0_ffn_ff_b2': (0.0, 0.519)}
    factors = {'L0_ffn_q_w': 8.0,
     'L0_ffn_k_w': 8.0,
     'L0_ffn_v_w': 8.0,
     'L0_ffn_o_w': 5.682,
     'L0_ffn_rel_table': 8.0,
     'L0_ffn_ff_w1': 3.862,
     'L0_ffn_ff_w2': 3.086}
    for name, (base, spread) in spreads.items():
        noise = np.random.default_rng([zlib.crc32(name.encode()), seed]).standard_normal(out[name].shape)
        drawn = base * np.exp(spread * noise) if base else spread * noise
        out[name] = jnp.asarray(drawn.astype(out[name].dtype))
    for name, factor in factors.items():
        out[name] = (out[name] * factor).astype(out[name].dtype)
    return out
```

```python
import concourse.bass as bass
from concourse import mybir
from concourse.alu_op_type import AluOpType as ALU
from contextlib import ExitStack

F32 = mybir.dt.float32
BF16 = mybir.dt.bfloat16
U32 = mybir.dt.uint32
ACT = mybir.ActivationFunctionType
AX = mybir.AxisListType

D = 256
HALF = D // 128
PATCH, CH, GRID = 16, 3, 6
NPATCH = GRID * GRID
TXT = 128
SEQ = 1 + NPATCH + TXT
PAIR = 2 * SEQ
TT = PAIR // 3
PF = CH * PATCH * PATCH
PC = PF // 128
HEADS, HD, GROUPS = 16, 16, 4
LAT = 64
EA, EF = 8, 16
MAXP = 64
REL = 2 * MAXP + 1
REM = SEQ - 128
WIDE = 384
IMG1 = WIDE - SEQ
SPAN = 2 * SEQ - 1
EPS = 1e-5
ARENA = 26200
SLOTS = [(0, 0, 0, 128, 0), (1, 0, 128, 64, 0), (1, 64, 138, 64, 1), (2, 0, 202, 128, 1)]

EXPERTS_BEFORE, EXPERTS_AFTER = 2, 2


def spread(ap, n):
    return bass.AP(ap.tensor, ap.offset, [list(ap.ap[0]), [0, n], list(ap.ap[-1])])


def columns(ap, n):
    return bass.AP(ap.tensor, ap.offset, [list(x) for x in ap.ap] + [[0, n]])


def ends_of(ap):
    return bass.AP(ap.tensor, ap.offset + 128, [list(ap.ap[0]), [SEQ, 2], [-128, 2], [1, REM]])


def at(eng, value):
    return value if isinstance(value, int) else eng.to_reg(value)


def wait_all(eng, *pairs):
    found = [(sem, at(eng, value)) for sem, value in pairs]
    for sem, value in found:
        eng.wait_ge(sem, value)


def early_fusion(nc, t, out):
    images = t["x"].shape[0]
    pairs = images // 2
    PI = min(16, images)
    PR = PI * GRID
    patch_steps = images // PI
    SCALE_Q = 128.0 ** -0.5

    ctx = ExitStack()
    with ctx:
        def sb(name, shape, dt=F32):
            return ctx.enter_context(nc.sbuf_tensor(name, shape, dt))

        arena = sb("arena", [128, ARENA])
        ends = {"early": 0, "late": 0}

        def within(when, shape):
            size = 1
            for x in shape[1:]:
                size *= x
            at = ends[when]
            ends[when] = at + size
            assert ends[when] <= ARENA, ends
            v = arena[0:shape[0], at:at + size]
            names = ["a", "b", "c", "d"][:len(shape) - 1]
            if len(names) == 1:
                return v
            return v.rearrange(f"p ({' '.join(names)}) -> p {' '.join(names)}", **dict(zip(names, shape[1:])))

        def sem(name):
            return ctx.enter_context(nc.semaphore(name))

        banks = [ctx.enter_context(nc.psum_tensor(f"bank{b}", [128, 512], F32)) for b in range(8)]
        S_BANKS = banks[0:2]
        PT, CT, HB, GB = banks[2], banks[3], banks[4], banks[5]
        ACC = banks[6:8]

        tokens_dram = nc.dram_tensor("patch_tokens", [images * NPATCH, D], F32)
        cls_dram = nc.dram_tensor("cls_rows", [2, D], F32)
        span_dram = nc.dram_tensor("rel_span", [EA, 3 * 128, SPAN], F32)

        ident = sb("ident", [128, 128])
        wt = within("early", [128, PC, D])
        ln1g = sb("ln1g", [128, PC])
        ln1b = sb("ln1b", [128, PC])
        tbias = within("early", [128, D])
        ln2g = within("early", [128, D])
        peb = within("early", [PR, GRID, D])
        tln2b = within("early", [128, D])
        wq = sb("wq", [128, HALF, HEADS, 32])
        wk_v = within("early", [128, 2, HALF, D])
        wkvT = within("early", [128, HALF, D])
        wdown = sb("wdown", [128, HALF, LAT])
        wlat = sb("wlat", [128, HALF, LAT])
        wupk = sb("wupk", [LAT, HEADS, 32])
        wupv = sb("wupv", [LAT, D])
        wo = sb("wo", [128, GROUPS, D])
        decay = sb("decay", [128, 3, SEQ])
        maskr = sb("maskr", [2 * REM, HEADS, HD])
        maskc = sb("maskc", [2 * REM, 2])
        iota = sb("iota", [128, EF])
        lnw = sb("lnw", [128, 4, HALF])
        gatew = sb("gatew", [128, HALF, EA])
        qw = sb("qw", [128, EA, HALF, 128])
        qb = sb("qb", [128, EA])
        kw = sb("kw", [128, HALF, 128])
        kb = sb("kb", [128, 1])
        vw = sb("vw", [128, HALF, 128])
        vb = sb("vb", [128, 128])
        vbm = sb("vbm", [2 * REM, 2, 128])
        ow = sb("ow", [128, EA, D])
        ob = sb("ob", [EA, D])
        reltab = within("early", [128, 128])
        relT = sb("relT", [128, REL])
        fgatew = sb("fgatew", [128, HALF, EF])
        w1 = sb("w1", [128, EF, HALF, 128])
        b1 = sb("b1", [128, EF])
        w2 = sb("w2", [128, EF, D])
        b2 = sb("b2", [EF, D])
        pick_f = within("early", [3 * EF, EF, 128])
        pick = sb("pick", [3 * EF, EF, 128], BF16)
        neghalf = sb("neghalf", [128, GRID])
        clsr = within("early", [2, D])
        clsp = within("early", [2, D])

        xin = within("early", [PR, CH * PATCH, GRID * PATCH])
        xpn = within("early", [PR, 2, PF])
        xpT = within("early", [128, 2, PC, PR])
        ytok = within("early", [PR, GRID, D])
        pst = sb("pst", [PR, GRID, 2, 6])
        pmv = sb("pmv", [PR, GRID, 2])
        pve = sb("pve", [PR, GRID])
        prs = sb("prs", [PR, GRID])

        h_in = sb("h_in", [TT, 3, D])
        h1 = sb("h1", [TT, 3, D])
        src = sb("src", [TT, 3, D])
        x2 = src
        resid = sb("resid", [TT, 3, D])
        xn = sb("xn", [TT, 3, D])
        st = sb("st", [TT, 3, 6])
        mv = sb("mv", [TT, 3, 2])
        ve = sb("ve", [TT, 3])
        rs = sb("rs", [TT, 3])
        xaT = within("late", [128, HALF, PAIR])
        x1T = within("late", [128, HALF, PAIR])
        x2T = within("late", [128, HALF, PAIR])
        qT = within("late", [128, GROUPS, PAIR])
        kT = within("late", [128, GROUPS, PAIR])
        latT = within("late", [LAT, PAIR])
        latR = within("late", [LAT, 2, 2 * REM])
        x1R = within("late", [128, HALF, 2, 2 * REM])
        rsx = within("late", [128, 3, 128])
        v_main = sb("v_main", [128, 2, HEADS, 32])
        v_rem = sb("v_rem", [2 * REM, 2, HEADS, 32])
        sc = within("late", [128, 2, 3, SEQ])
        nmax = sb("nmax", [128, 2, 3])
        prob = within("late", [128, 2, 3, 2 * SEQ])
        ptm = within("late", [128, 4, WIDE])
        ptr = within("late", [2 * REM, 2, WIDE])
        sums = sb("sums", [128, 3, HEADS])
        rsum = sb("rsum", [128, 3, HEADS])
        cts = within("late", [128, PAIR])
        ctn = within("late", [128, GROUPS, PAIR])
        kmT = within("late", [128, PAIR])
        vm = within("late", [128, 2, 2, 128])
        vmr = within("late", [2 * REM, 2, 2, 128])
        qm = within("late", [128, EA, PAIR])
        span = within("late", [128, 2, 3, SPAN])
        bias = within("late", [128, EA, 3, SEQ])
        glog = sb("glog", [128, 3, EF])
        gtop = sb("gtop", [128, 3, 8])
        gidx = sb("gidx", [128, 3, 8], U32)
        gidf = sb("gidf", [128, 3, 2])
        gd = sb("gd", [128, 3])
        ge = sb("ge", [128, 3])
        gs = sb("gs", [128, 3])
        g1 = sb("g1", [128, 3])
        g2 = sb("g2", [128, 3])
        ga = sb("ga", [128, 3, EF])
        gb = sb("gb", [128, 3, EF])
        gates_a = sb("gates_a", [128, 3, EA])
        gatesT_a = sb("gatesT_a", [EA, PAIR])
        msum = sb("msum", [128, EA, 3])
        mrs = sb("mrs", [128, EA, 3])
        mw = sb("mw", [128, EA, 3])
        cm = within("late", [128, 2, PAIR])
        gates_f = sb("gates_f", [TT, 3, EF])
        gparts = sb("gparts", [TT, 3, 3, EF])
        gpb = sb("gpb", [TT, 3, 3, EF], BF16)
        grest = sb("grest", [TT, 3, EF])
        gatesT_f = sb("gatesT_f", [EF, PAIR])
        partsT = sb("partsT", [3 * EF, PAIR], BF16)
        hr = within("late", [128, PAIR])
        hg = within("late", [128, 2, PAIR])

        w_in = sem("w_in")
        bias_zero = sem("bias_zero")
        pool_turn = sem("pool_turn")
        zeroed = sem("zeroed")
        wpad_in = sem("wpad_in")
        x_in = sem("x_in")
        pvar = sem("pvar")
        prstd = sem("prstd")
        pnorm = sem("pnorm")
        ptran = sem("ptran")
        pfeat = sem("pfeat")
        pmm = sem("pmm")
        padd = sem("padd")
        ptok = sem("ptok")
        pst_out = sem("pst_out")
        dve_step = sem("dve_step")
        cls_sum = sem("cls_sum")
        cls_out = sem("cls_out")
        setup_pe = sem("setup_pe")
        setup_dve = sem("setup_dve")

        h_loaded = sem("h_loaded")
        h_free = sem("h_free")
        var_ready = sem("var_ready")
        rstd_ready = sem("rstd_ready")
        xn_ready = sem("xn_ready")
        xn_tran = sem("xn_tran")
        feat_ready = sem("feat_ready")
        proj_done = sem("proj_done")
        proj_act = sem("proj_act")
        proj_dve = sem("proj_dve")
        sc_done = sem("sc_done")
        sc_taken = sem("sc_taken")
        max_ready = sem("max_ready")
        prob_ready = sem("prob_ready")
        pt_done = sem("pt_done")
        pt_taken = sem("pt_taken")
        pv_done = sem("pv_done")
        cts_ready = sem("cts_ready")
        rsum_ready = sem("rsum_ready")
        rsx_ready = sem("rsx_ready")
        x1r_ready = sem("x1r_ready")
        rb_done = sem("rb_done")
        ctn_ready = sem("ctn_ready")
        oproj_done = sem("oproj_done")
        oproj_taken = sem("oproj_taken")
        mk_done = sem("mk_done")
        mk_act = sem("mk_act")
        mk_dve = sem("mk_dve")
        top_diff = sem("top_diff")
        top_exp = sem("top_exp")
        gates_ready = sem("gates_ready")
        gates_tran = sem("gates_tran")
        gatesT_ready = sem("gatesT_ready")
        q_done = sem("q_done")
        q_ready = sem("q_ready")
        rel_done = sem("rel_done")
        rel_mid = sem("rel_mid")
        span_ready = sem("span_ready")
        span_out = [sem(f"span_out{b}") for b in range(2)]
        bias_in = [sem(f"bias_in{e}") for e in range(EA)]
        mw_ready = sem("mw_ready")
        moa_done = sem("moa_done")
        fg_done = sem("fg_done")
        fgates_ready = sem("fgates_ready")
        fg_tran = sem("fg_tran")
        fgT_ready = sem("fgT_ready")
        up_done = sem("up_done")
        relu_ready = sem("relu_ready")
        gated_ready = sem("gated_ready")
        down_done = sem("down_done")
        y_ready = sem("y_ready")
        stored = sem("stored")
        smax_free = sem("smax_free")

        WLOADS = 0

        block = ctx.enter_context(nc.Block())

        XN, TRAN, FEAT = 3, 6, 6
        UNITS = HEADS + EA
        PROJ, PACT = 11, 11

        @block.sync
        def _(sp):
            for step in range(patch_steps):
                if step:
                    sp.wait_ge(pvar, 2 * step)
                for c in range(CH):
                    sp.dma_start(xin[:, c * PATCH:(c + 1) * PATCH, :].rearrange("r p w -> r (p w)"),
                                 t["x"][step * PI:(step + 1) * PI, c].rearrange("b (g p) w -> b g (p w)", g=GRID)
                                 ).then_inc(x_in, 16)
                if step:
                    sp.wait_ge(ptok, step)
                    sp.dma_start(tokens_dram[(step - 1) * PI * NPATCH:step * PI * NPATCH, :].rearrange("(r w) d -> r (w d)", w=GRID),
                                 ytok[:, :, :].rearrange("r w d -> r (w d)")).then_inc(pst_out, 16)
            sp.wait_ge(ptok, patch_steps)
            sp.dma_start(tokens_dram[(patch_steps - 1) * PI * NPATCH:patch_steps * PI * NPATCH, :].rearrange("(r w) d -> r (w d)", w=GRID),
                         ytok[:, :, :].rearrange("r w d -> r (w d)")).then_inc(pst_out, 16)
            sp.wait_ge(cls_sum, 1)
            sp.dma_start(cls_dram[:, :], clsr[:, :]).then_inc(cls_out, 16)
            sp.wait_ge(cls_out, 16)
            sp.wait_ge(pst_out, 16 * patch_steps)

            def load(n):
                if not (isinstance(n, int) and n == 0):
                    sp.wait_ge(h_free, at(sp, n * 1))
                pieces = []
                for a in range(2):
                    pieces += [("c", a, 0, a * SEQ, 1), ("p", a, 0, a * SEQ + 1, NPATCH), ("t", a, 0, a * SEQ + 1 + NPATCH, TXT)]
                for kind, a, first, row, count in pieces:
                    while count:
                        tile, r = divmod(row, TT)
                        m = min(count, TT - r)
                        if kind == "c":
                            s = cls_dram[a:a + 1, :]
                        elif kind == "p":
                            s = tokens_dram[bass.ds(n * 2 * NPATCH + a * NPATCH + first, m), :]
                        else:
                            s = t["txt"].rearrange("b s d -> (b s) d")[bass.ds(n * 2 * TXT + a * TXT + first, m), :]
                        sp.dma_start(h_in[r:r + m, tile, :], s).then_inc(h_loaded, 16)
                        first, row, count = first + m, row + m, count - m

            def spans(n):
                for e in range(EA):
                    wait_all(sp, (span_ready, n * EA + e + 1))
                    sp.dma_start(span_dram[e].rearrange("(s p) w -> p s w", p=128), span[:, e % 2, :, :]).then_inc(span_out[e % 2], 16)
                    if e >= 1:
                        skew(n, e - 1)
                skew(n, EA - 1)

            def skew(n, e):
                r = at(sp, n * (EA // 2 * 16) + (e // 2 + 1) * 16)
                sp.wait_ge(span_out[e % 2], r)
                base = e * 3 * 128 * SPAN
                T = span_dram[:, :, :].tensor
                for slot, row, rows, q0 in ((0, 0, 128, 0), (2, 0, 128, REM), (1, 0, REM, 128), (1, 128 - REM, REM, 0)):
                    s = bass.AP(T, base + (slot * 128 + row) * SPAN + SEQ - 1 - q0, [[SPAN - 1, rows], [1, SEQ]])
                    sp.dma_start(bias[row:row + rows, e, slot, :], s).then_inc(bias_in[e], 16)

            def store(n):
                rows = out.rearrange("b s d -> (b s) d")
                r = at(sp, n * 1 + 1)
                sp.wait_ge(y_ready, r)
                sp.dma_start(rows[bass.ds(n * PAIR, PAIR), :].rearrange("(c p) d -> p c d", p=TT), resid[:, :, :]).then_inc(stored, 16)

            load(0)
            sp.wait_ge(bias_zero, 1)
            spans(0)
            with sp.Fori(0, pairs - 1) as n:
                load(n + 1)
                store(n)
                spans(n + 1)
            store(pairs - 1)
            sp.wait_ge(stored, 16 * pairs)

        @block.gpsimd
        def _(pool):
            for z in (wq, wupk, wo, v_main, v_rem):
                pool.memset(z[:], 0.0).then_inc(zeroed, 1)
            pool.memset(neghalf[:], -0.5).then_inc(zeroed, 1)
            pool.wait_ge(zeroed, 6)
            for step in range(patch_steps):
                for k in range(2):
                    pool.wait_ge(pvar, 2 * step + k + 1)
                    nc.gpsimd.tensor_tensor(prs[:, :], pve[:, :], neghalf[0:PR, :], ALU.pow).then_inc(prstd, 1)

            pool.wait_ge(ptok, patch_steps)
            pool.memset(bias[:, :, :, :], 0.0).then_inc(bias_zero, 1)

            def inverse_root(n, k):
                pool.wait_ge(var_ready, at(pool, n * 4 + k + 1))
                nc.gpsimd.tensor_tensor(rs[:, :], ve[:, :], neghalf[0:TT, 0:3], ALU.pow).then_inc(rstd_ready, 1)

            def pair(n):
                inverse_root(n, 0)
                for g in range(GROUPS):
                    if g:
                        wait_all(pool, (rsum_ready, n * GROUPS + g + 1), (rb_done, n * GROUPS + g))
                    else:
                        pool.wait_ge(rsum_ready, at(pool, n * GROUPS + 1))
                    pool.sem_inc(pool_turn, 1)
                    nc.gpsimd.tensor_copy(rsx[:, :, :].rearrange("p s (h d) -> p s h d", d=32), columns(rsum[:, :, 4 * g:4 * g + 4], 32)).then_inc(rsx_ready, 1)
                inverse_root(n, 1)
                inverse_root(n, 2)
                for k in range(HALF):
                    pool.wait_ge(feat_ready, at(pool, n * FEAT + 3 + k))
                    pool.sem_inc(pool_turn, 1)
                    nc.gpsimd.tensor_copy(x1R[:, k].rearrange("p a (b r) -> p a b r", b=2), ends_of(x1T[:, k, :])).then_inc(x1r_ready, 1)
                for e in range(EA):
                    pool.wait_ge(rel_mid, at(pool, n * EA + e + 1))
                    pool.sem_inc(pool_turn, 1)
                    mid = span[:, e % 2, :, SEQ - 1 - MAXP:SEQ + MAXP]
                    side = SEQ - 1 - MAXP
                    nc.gpsimd.tensor_copy(span[:, e % 2, :, 0:side], columns(mid[:, :, 0], side))
                    nc.gpsimd.tensor_copy(span[:, e % 2, :, SEQ + MAXP:SPAN], columns(mid[:, :, REL - 1], side)).then_inc(span_ready, 1)
                inverse_root(n, 3)

            pair(0)
            with pool.Fori(0, pairs - 1) as n:
                pair(n + 1)

        @block.scalar
        def _(act):
            def load(dst, source):
                nonlocal WLOADS
                act.dma_start(dst, source, allow_slow_non_contiguous=True).then_inc(w_in, 16)
                WLOADS += 16

            load(ident[:], t["ident"])
            tw = t["L0_tok_W"].rearrange("(h p c) d -> p c h d", p=128, c=CH)
            for c in range(CH):
                load(wt[:, 2 * c:2 * c + 2, :], tw[:, c])
            for dst, name in ((ln1g, "L0_tok_ln1_g"), (ln1b, "L0_tok_ln1_b")):
                v = t[name].rearrange("(h p c) -> p c h", p=128, c=CH)
                for c in range(CH):
                    load(dst[:, 2 * c:2 * c + 2], v[:, c])
            for dst, name in ((tbias, "L0_tok_bias"), (ln2g, "L0_tok_ln2_g"), (tln2b, "L0_tok_ln2_b")):
                load(dst[:], t[name].partition_broadcast(128))
            load(peb[:], t["pe"][0:PR])
            for r in range(2):
                load(clsr[r:r + 1, :], t["L0_tok_cls_token"].rearrange("a b d -> (a b) d"))
                load(clsp[r:r + 1, :], t["L0_tok_cls_pos_embedding"].rearrange("a b d -> (a b) d"))
            load(wk_v[:, 0], t["L0_attn_W_k"].rearrange("(k p) d -> p k d", p=128))
            load(wk_v[:, 1], t["L0_attn_W_v"].rearrange("(k p) d -> p k d", p=128))
            load(wdown[:], t["L0_attn_W_down_kv"].rearrange("(k p) d -> p k d", p=128))
            load(wupv[:], t["L0_attn_W_up_v"])
            load(decay[:], t["decay"])
            load(maskr[:], t["mask_rows"])
            load(maskc[:], t["mask_cols"])
            load(iota[:], t["iota"])
            for k, name in enumerate(("ln1_w", "ln1_b", "ln2_w", "ln2_b")):
                load(lnw[:, k, :], t["L0_ffn_" + name].rearrange("(k p) -> p k", p=128))
            load(gatew[:], t["L0_ffn_attn_gate_w"].rearrange("(k p) e -> p k e", p=128))
            for k in range(HALF):
                load(qw[:, :, k, :], t["L0_ffn_q_w"][:, k * 128:(k + 1) * 128, :].rearrange("e p h -> p e h"))
                load(w1[:, :, k, :], t["L0_ffn_ff_w1"][:, k * 128:(k + 1) * 128, :].rearrange("e p h -> p e h"))
            load(qb[:], t["L0_ffn_q_b"].rearrange("e h -> h e"))
            load(kw[:], t["L0_ffn_k_w"].rearrange("(k p) d -> p k d", p=128))
            load(kb[:], t["L0_ffn_k_b"].rearrange("(p o) -> p o", o=1))
            load(vw[:], t["L0_ffn_v_w"].rearrange("(k p) d -> p k d", p=128))
            load(vb[:], t["L0_ffn_v_b"].partition_broadcast(128))
            load(ow[:], t["L0_ffn_o_w"].rearrange("e h d -> h e d"))
            load(ob[:], t["L0_ffn_o_b"])
            load(reltab[:], t["L0_ffn_rel_table"][0:128])
            load(relT[:, 128:REL], t["L0_ffn_rel_table"][128:REL].rearrange("r h -> h r"))
            load(fgatew[:], t["L0_ffn_ff_gate_w"].rearrange("(k p) e -> p k e", p=128))
            load(b1[:], t["L0_ffn_ff_b1"].rearrange("e h -> h e"))
            load(w2[:], t["L0_ffn_ff_w2"].rearrange("e h d -> h e d"))
            load(b2[:], t["L0_ffn_ff_b2"])
            load(pick_f[:], t["pick"])
            act.wait_ge(zeroed, 6)
            for k in range(HALF):
                act.dma_start(wq[:, k, :, 0:HD], t["L0_attn_W_q"][k * 128:(k + 1) * 128, :].rearrange("p (h d) -> p h d", d=HD)).then_inc(wpad_in, 16)
            act.dma_start(wupk[:, :, 0:HD], t["L0_attn_W_up_k"].rearrange("l (h d) -> l h d", d=HD)).then_inc(wpad_in, 16)
            for j in range(4):
                act.dma_start(wo[32 * j:32 * j + HD, :, :],
                              t["L0_attn_W_o"].rearrange("(g j d) n -> j d g n", g=GROUPS, j=4)[j]).then_inc(wpad_in, 16)

            act.wait_ge(w_in, WLOADS)
            for step in range(patch_steps):
                for w in range(GRID):
                    u = step * GRID + w
                    if u >= 2:
                        act.wait_ge(pmm, u - 1)
                    for half in range(2):
                        act.wait_ge(ptran, 2 * u + half + 1)
                        for c in range(3):
                            k = 3 * half + c
                            last = nc.scalar.activation(xpT[:, u % 2, k, :], S_BANKS[half][:, c * PR:(c + 1) * PR], ACT.Identity,
                                                        bias=ln1b[:, k:k + 1], scale=ln1g[:, k:k + 1])
                        last.then_inc(pfeat, 1)

            def features(n, k, dst, gain):
                for c in range(HALF):
                    act.wait_ge(xn_tran, at(act, n * TRAN + 2 * k + c + 1))
                    if gain is None:
                        i = nc.scalar.copy(dst[:, c, :], S_BANKS[c][:, 0:PAIR])
                    else:
                        i = nc.scalar.activation(dst[:, c, :], S_BANKS[c][:, 0:PAIR], ACT.Identity,
                                                 bias=lnw[:, gain + 1, c:c + 1], scale=lnw[:, gain, c:c + 1])
                    i.then_inc(feat_ready, 1)

            def softmax_row(n, u, parity):
                act.wait_ge(max_ready, at(act, n * UNITS + u + 1))
                for s in range(3):
                    acc = sums[:, s, u:u + 1] if u < HEADS else msum[:, u - HEADS, s:s + 1]
                    last = nc.scalar.activation(prob[:, parity, s, u % 2 * SEQ:(u % 2 + 1) * SEQ], sc[:, u % 2, s, :], ACT.Exp,
                                                bias=nmax[:, u % 2, s:s + 1], scale=1.0, accum_out=acc)
                last.then_inc(prob_ready, 1)

            def take_main(n, u):
                p, h = divmod(u, 2)
                act.wait_ge(pt_done, at(act, n * 3 * UNITS // 2 + 3 * p + h + 1) if isinstance(n, int) else at(act, n * (3 * UNITS // 2) + 3 * p + h + 1))
                nc.scalar.copy(ptm[:, u % 4, :], PT[:, 0:WIDE]).then_inc(pt_taken, 1)

            def take_rem(n, p):
                act.wait_ge(pt_done, at(act, n * (3 * UNITS // 2) + 3 * p + 3))
                nc.scalar.copy(ptr[:, p % 2, :], PT[0:2 * REM, 0:WIDE]).then_inc(pt_taken, 1)

            def relu(m, e):
                if e == 0:
                    act.wait_ge(up_done, at(act, m * EF + 1))
                else:
                    wait_all(act, (up_done, m * EF + e + 1), (gated_ready, m * EF + e))
                nc.scalar.activation(hr[:, :], HB[:, 0:PAIR], ACT.Relu, bias=b1[:, e:e + 1], scale=1.0).then_inc(relu_ready, 1)

            def top_exp_step(n, k):
                act.wait_ge(top_diff, at(act, n * 2 + k + 1))
                rows = 128 if k == 0 else TT
                nc.scalar.activation(ge[0:rows, :], gd[0:rows, :], ACT.Exp).then_inc(top_exp, 1)

            def latent_attention(n, m):
                features(n, 0, xaT, None)
                for g in range(GROUPS):
                    act.wait_ge(proj_done, at(act, n * PROJ + g + 1))
                    nc.scalar.copy(qT[:, g, :], (CT, PT)[g % 2][:, 0:PAIR]).then_inc(proj_act, 1)
                act.wait_ge(proj_done, at(act, n * PROJ + 5))
                nc.scalar.copy(latT[:, :], CT[0:LAT, 0:PAIR]).then_inc(proj_act, 1)
                nc.scalar.copy(latR[:, :, :].rearrange("p a (b r) -> p a b r", b=2), ends_of(CT[0:LAT, 0:PAIR])).then_inc(proj_act, 1)
                for g in range(GROUPS):
                    act.wait_ge(proj_done, at(act, n * PROJ + 6 + g))
                    nc.scalar.copy(kT[:, g, :], (PT, CT)[g % 2][:, 0:PAIR]).then_inc(proj_act, 1)
                act.wait_ge(proj_done, at(act, n * PROJ + 10))
                nc.scalar.copy(v_main[:, :, :, 0:HD].rearrange("p a h d -> p (a h) d"), PT[:, :].rearrange("p (h d) -> p h d", d=HD)).then_inc(proj_act, 1)
                if m is not None:
                    for e in range(EXPERTS_BEFORE):
                        relu(m, e)
                e = EXPERTS_BEFORE
                for h in range(HEADS + 3):
                    if m is not None and e < EF - EXPERTS_AFTER:
                        relu(m, e)
                        e += 1
                    if h < HEADS:
                        softmax_row(n, h, (h // 2) % 2)
                    if 2 <= h < HEADS + 2:
                        take_main(n, h - 2)
                    if h >= 3 and h % 2 == 1:
                        take_rem(n, (h - 3) // 2)
                        if (h - 3) // 2 % 2 == 1:
                            g = (h - 3) // 4
                            act.wait_ge(pv_done, at(act, n * (GROUPS + EA) + g + 1))
                            nc.scalar.copy(cts[:, :], CT[:, 0:PAIR]).then_inc(cts_ready, 1)
                if m is not None:
                    for e in range(EF - EXPERTS_AFTER, EF):
                        relu(m, e)

            def mixture_of_attention(n):
                features(n, 1, x1T, 0)
                act.wait_ge(mk_done, at(act, n * 4 + 1))
                nc.scalar.activation(kmT[:, :], HB[:, 0:PAIR], ACT.Identity, bias=kb[:, 0:1], scale=1.0).then_inc(mk_act, 1)
                for e in range(EA):
                    act.wait_ge(rel_done, at(act, n * EA + e + 1))
                    if e == 0:
                        top_exp_step(n, 0)
                    wb = e - 2
                    if wb >= 0:
                        act.wait_ge(span_out[e % 2], at(act, n * (EA // 2 * 16) + (wb // 2 + 1) * 16))
                    nc.scalar.copy(span[:, e % 2, :, SEQ - 1 - MAXP:SEQ + MAXP],
                                   S_BANKS[e % 2][:, 0:3 * REL].rearrange("p (s r) -> p s r", s=3)).then_inc(rel_mid, 1)
                for x in range(EA + 3):
                    if x < EA:
                        softmax_row(n, HEADS + x, x // 2 % 2)
                    if 2 <= x < EA + 2:
                        take_main(n, HEADS + x - 2)
                    if x >= 3 and x % 2 == 1:
                        take_rem(n, (HEADS + x - 3) // 2)
                        for e in (x - 3, x - 2):
                            act.wait_ge(pv_done, at(act, n * (GROUPS + EA) + GROUPS + e + 1))
                            nc.scalar.copy(cm[:, e % 2, :], (CT, HB)[e % 2][:, 0:PAIR]).then_inc(cts_ready, 1)
                features(n, 2, x2T, 2)
                top_exp_step(n, 1)
                act.wait_ge(fg_tran, at(act, n * 2 + 1))
                nc.scalar.copy(gatesT_f[:, :], CT[0:EF, 0:PAIR]).then_inc(fgT_ready, 1)
                act.wait_ge(fg_tran, at(act, n * 2 + 2))
                nc.scalar.copy(partsT[:, :], PT[0:3 * EF, 0:PAIR]).then_inc(fgT_ready, 1)

            latent_attention(0, None)
            mixture_of_attention(0)
            with act.Fori(0, pairs - 1) as n:
                latent_attention(n + 1, n)
                mixture_of_attention(n + 1)
            for e in range(EF):
                relu(pairs - 1, e)

        @block.vector
        def _(dve):
            count = [0]

            def link(i):
                count[0] += 1
                return i.then_inc(dve_step, 1)

            def linked():
                dve.wait_ge(dve_step, count[0])

            def restart():
                linked()
                dve.sem_clear(dve_step)
                count[0] = 0

            dve.wait_ge(w_in, WLOADS)
            nc.vector.tensor_tensor(clsr[:], clsr[:], clsp[:], ALU.add).then_inc(cls_sum, 1)
            link(nc.vector.tensor_tensor(peb[:], peb[:], spread(tln2b[0:PR, :], GRID), ALU.add))
            link(nc.vector.tensor_tensor(wk_v[:, 0], wk_v[:, 0], wk_v[:, 1], ALU.add))
            link(nc.vector.tensor_copy(pick[:], pick_f[:]))
            link(nc.vector.tensor_scalar(vbm[:, 0, :], vb[0:2 * REM, :], maskc[:, 0:1], None, ALU.mult))
            nc.vector.tensor_scalar(vbm[:, 1, :], vb[0:2 * REM, :], maskc[:, 1:2], None, ALU.mult).then_inc(setup_dve, 1)
            dve.wait_ge(setup_pe, 1)
            for k in range(HALF):
                link(nc.vector.tensor_copy(wkvT[:, k, :], S_BANKS[k][:, 0:D]))
            nc.vector.tensor_copy(relT[:, 0:128], PT[:, 0:128]).then_inc(setup_dve, 1)
            dve.wait_ge(setup_pe, 2)
            nc.vector.tensor_copy(wlat[:, :, :], CT[:, 0:HALF * LAT].rearrange("p (k l) -> p k l", k=HALF)).then_inc(setup_dve, 1)

            xw = xin[:, :, :].rearrange("r q (g w) -> r g q w", g=GRID)
            for step in range(patch_steps):
                dve.wait_ge(x_in, 16 * CH * (step + 1))
                for w in range(GRID):
                    for half in range(2):
                        link(nc.vector.bn_stats(pst[:, w, half, :], xw[:, w, 24 * half:24 * half + 24, :]))
                linked()
                for w in range(GRID):
                    link(nc.vector.bn_aggr(pmv[:, w, :], pst[:, w, :, :].rearrange("r h s -> r (h s)")))
                linked()
                nc.vector.tensor_scalar(pve[:, :], pmv[:, :, 1], EPS, None, ALU.add).then_inc(pvar, 1)
                dve.wait_ge(prstd, 2 * step + 1)

                def normalize(w):
                    u = step * GRID + w
                    if u >= 2:
                        dve.wait_ge(ptran, 2 * (u - 1))
                    i = nc.vector.tensor_scalar(xpn[:, u % 2, :].rearrange("r (q w) -> r q w", w=PATCH), xw[:, w],
                                                pmv[:, w, 0:1], prs[:, w:w + 1], ALU.subtract, ALU.mult)
                    i.then_inc(pnorm, 1)

                normalize(0)
                normalize(1)
                if step:
                    dve.wait_ge(pst_out, 16 * step)
                for w in range(GRID):
                    u = step * GRID + w
                    dve.wait_ge(pmm, u + 1)
                    nc.vector.tensor_tensor(ytok[:, w, :], (CT, PT)[u % 2][0:PR, 0:D], tbias[0:PR, :], ALU.add).then_inc(padd, 1)
                    dve.wait_ge(padd, u + 1)
                    link(nc.vector.bn_stats(pst[:, w, 0, :], ytok[:, w, :]))
                    if w + 2 < GRID:
                        normalize(w + 2)
                dve.wait_ge(pnorm, (step + 1) * GRID)
                linked()
                for w in range(GRID):
                    link(nc.vector.bn_aggr(pmv[:, w, :], pst[:, w, 0, :]))
                linked()
                nc.vector.tensor_scalar(pve[:, :], pmv[:, :, 1], EPS, None, ALU.add).then_inc(pvar, 1)
                dve.wait_ge(prstd, 2 * step + 2)
                for w in range(GRID):
                    link(nc.vector.tensor_scalar(ytok[:, w, :], ytok[:, w, :], pmv[:, w, 0:1], prs[:, w:w + 1], ALU.subtract, ALU.mult))
                linked()
                link(nc.vector.tensor_tensor(ytok[:], ytok[:], spread(ln2g[0:PR, :], GRID), ALU.mult))
                linked()
                nc.vector.tensor_tensor(ytok[:], ytok[:], peb[:], ALU.add).then_inc(ptok, 1)

            def layer_norm(n, k, x):
                for j in range(3):
                    link(nc.vector.bn_stats(st[:, j, :], x[:, j, :]))
                linked()
                for j in range(3):
                    link(nc.vector.bn_aggr(mv[:, j, :], st[:, j, :]))
                linked()
                nc.vector.tensor_scalar(ve[:, :], mv[:, :, 1], EPS, None, ALU.add).then_inc(var_ready, 1)

            def normalized(n, k, x, dst):
                dve.wait_ge(rstd_ready, at(dve, n * 4 + k + 1))
                for j in range(3):
                    last = nc.vector.tensor_scalar(dst[:, j, :], x[:, j, :], mv[:, j, 0:1], rs[:, j:j + 1], ALU.subtract, ALU.mult)
                    if j < 2 or dst is not xn:
                        link(last)
                if dst is xn:
                    last.then_inc(xn_ready, 1)

            def gates_of(n, k, rows, slots, experts, dst):
                for s in slots:
                    link(nc.vector.max(gtop[0:rows, s, :], glog[0:rows, s, 0:experts]))
                linked()
                for s in slots:
                    link(nc.vector.max_index(gidx[0:rows, s, :], gtop[0:rows, s, :], glog[0:rows, s, 0:experts]))
                nc.vector.tensor_tensor(gd[0:rows, :], gtop[0:rows, :, 1], gtop[0:rows, :, 0], ALU.subtract).then_inc(top_diff, 1)
                linked()
                link(nc.vector.tensor_copy(gidf[0:rows], gidx[0:rows, :, 0:2]))
                dve.wait_ge(top_exp, at(dve, n * 2 + k + 1))
                link(nc.vector.tensor_scalar(gs[0:rows], ge[0:rows], 1.0, None, ALU.add))
                linked()
                link(nc.vector.reciprocal(g1[0:rows], gs[0:rows]))
                linked()
                link(nc.vector.tensor_tensor(g2[0:rows], ge[0:rows], g1[0:rows], ALU.mult))
                linked()
                for s in slots:
                    link(nc.vector.tensor_scalar(ga[0:rows, s, 0:experts], iota[0:rows, 0:experts], gidf[0:rows, s, 0:1], g1[0:rows, s:s + 1], ALU.is_equal, ALU.mult))
                    link(nc.vector.tensor_scalar(gb[0:rows, s, 0:experts], iota[0:rows, 0:experts], gidf[0:rows, s, 1:2], g2[0:rows, s:s + 1], ALU.is_equal, ALU.mult))
                linked()
                return nc.vector.tensor_tensor(dst[0:rows], ga[0:rows, :, 0:experts], gb[0:rows, :, 0:experts], ALU.add)

            def scores(n, u):
                if u < 2:
                    dve.wait_ge(sc_done, at(dve, n * UNITS + u + 1))
                    if not (isinstance(n, int) and n == 0):
                        dve.wait_ge(prob_ready, at(dve, n * UNITS + u - 1))
                else:
                    wait_all(dve, (sc_done, n * UNITS + u + 1), (prob_ready, n * UNITS + u - 1))
                s = S_BANKS[u % 2][:, 0:3 * SEQ].rearrange("p (s k) -> p s k", s=3)
                if u < HEADS:
                    i = nc.vector.tensor_tensor(sc[:, u % 2], s, decay[:], ALU.mult)
                else:
                    e = u - HEADS
                    dve.wait_ge(bias_in[e], at(dve, n * 64 + 64))
                    i = nc.vector.tensor_tensor(sc[:, u % 2], s, bias[:, e], ALU.add)
                i.then_inc(sc_taken, 1)
                dve.wait_ge(sc_taken, at(dve, n * UNITS + u + 1))
                nc.vector.tensor_reduce(nmax[:, u % 2, :], sc[:, u % 2], AX.X, ALU.max, negate=True).then_inc(max_ready, 1)

            def gate_hidden(m, e):
                if e >= 2:
                    wait_all(dve, (relu_ready, m * EF + e + 1), (down_done, m * EF + e - 1))
                else:
                    dve.wait_ge(relu_ready, at(dve, m * EF + e + 1))
                nc.vector.tensor_tensor(hg[:, e % 2, :], GB[:, 0:PAIR], hr[:, :], ALU.mult).then_inc(gated_ready, 1)

            def finish(m):
                dve.wait_ge(down_done, at(dve, m * EF + EF))
                link(nc.vector.tensor_tensor(resid[:, 0:2, :], ACC[0][0:TT, :].rearrange("p (c d) -> p c d", c=2), resid[:, 0:2, :], ALU.add))
                nc.vector.tensor_tensor(resid[:, 2, :], ACC[1][0:TT, 0:D], resid[:, 2, :], ALU.add).then_inc(y_ready, 1)

            def latent_attention(n, m):
                dve.wait_ge(h_loaded, at(dve, n * LOADS + LOADS))
                layer_norm(n, 0, h_in)
                normalized(n, 0, h_in, xn)
                if m is not None:
                    for e in range(EXPERTS_BEFORE):
                        gate_hidden(m, e)
                dve.wait_ge(proj_done, at(dve, n * PROJ + 11))
                link(nc.vector.tensor_tensor(v_rem[:, 0, :, 0:HD], CT[0:2 * REM, 0:D].rearrange("p (h d) -> p h d", d=HD), maskr[:], ALU.mult))
                nc.vector.tensor_tensor(v_rem[:, 1, :, 0:HD], CT[0:2 * REM, D:2 * D].rearrange("p (h d) -> p h d", d=HD), maskr[:], ALU.mult).then_inc(proj_dve, 1)
                e = EXPERTS_BEFORE
                for h in range(HEADS + 3):
                    if h < HEADS:
                        scores(n, h)
                    if m is not None and e < EF - EXPERTS_AFTER:
                        gate_hidden(m, e)
                        e += 1
                    if h >= 3 and h % 4 == 3 and h < HEADS + 3:
                        g = h // 4
                        if h < HEADS:
                            dve.wait_ge(prob_ready, at(dve, n * UNITS + h + 1))
                            nc.vector.reciprocal(rsum[:, :, 4 * g:4 * g + 4], sums[:, :, 4 * g:4 * g + 4]).then_inc(rsum_ready, 1)
                    if h >= 5 and (h - 3) // 2 % 2 == 1 and h % 2 == 1:
                        g = (h - 3) // 4
                        wait_all(dve, (rb_done, n * GROUPS + g + 1), (cts_ready, n * (GROUPS + EA) + g + 1))
                        rb = bass.AP(CT[:, :].tensor, 0, [list(CT[:, :].ap[0]), [IMG1, 2], [1, SEQ]])
                        nc.vector.tensor_tensor(ctn[:, g, :].rearrange("p (a q) -> p a q", a=2), rb,
                                                cts[:, :].rearrange("p (a q) -> p a q", a=2), ALU.mult).then_inc(ctn_ready, 1)
                if m is not None:
                    for e in range(EF - EXPERTS_AFTER, EF):
                        gate_hidden(m, e)
                dve.wait_ge(oproj_done, at(dve, n * 1 + 1))
                link(nc.vector.tensor_tensor(h1[:, 0:2, :], S_BANKS[0][0:TT, :].rearrange("p (c d) -> p c d", c=2), h_in[:, 0:2, :], ALU.add))
                nc.vector.tensor_tensor(h1[:, 2, :], S_BANKS[1][0:TT, 0:D], h_in[:, 2, :], ALU.add).then_inc(h_free, 1)
                dve.wait_ge(h_free, at(dve, n * 1 + 1))

            def mixture_of_attention(n, m):
                layer_norm(n, 1, h1)
                if m is not None:
                    finish(m)
                normalized(n, 1, h1, src)
                linked()
                layer_norm(n, 2, src)
                normalized(n, 2, src, xn)
                dve.wait_ge(mk_done, at(dve, n * 4 + 2))
                nc.vector.tensor_tensor(vm[:, :, :, :].rearrange("p b a d -> p (b a) d"), GB[:, :].rearrange("p (c d) -> p c d", c=4), spread(vb[:, :], 4), ALU.add).then_inc(mk_dve, 1)
                dve.wait_ge(mk_done, at(dve, n * 4 + 3))
                for par in range(2):
                    for a in range(2):
                        last = nc.vector.scalar_tensor_tensor(out=vmr[:, par, a, :], in0=CT[0:2 * REM, a * 128:(a + 1) * 128],
                                                              scalar=maskc[:, par:par + 1], in1=vbm[:, par, :],
                                                              op0=ALU.mult, op1=ALU.add)
                        if par + a < 2:
                            link(last)
                last.then_inc(mk_dve, 1)
                dve.wait_ge(mk_done, at(dve, n * 4 + 4))
                nc.vector.tensor_copy(glog[:, :, 0:EA], PT[:, 0:3 * EA].rearrange("p (s e) -> p s e", s=3)).then_inc(mk_dve, 1)
                dve.wait_ge(mk_dve, at(dve, n * 3 + 3))
                for e in range(2):
                    queries(n, e)
                gates_of(n, 0, 128, range(3), EA, gates_a).then_inc(gates_ready, 1)
                for e in range(2, EA):
                    queries(n, e)
                dve.wait_ge(gates_tran, at(dve, n * 1 + 1))
                nc.vector.tensor_copy(gatesT_a[:, :].rearrange("e (a q) -> e a q", a=2),
                                      bass.AP(CT[:, :].tensor, 0, [[CT[:, :].ap[0][0], EA], [IMG1, 2], [1, SEQ]])).then_inc(gatesT_ready, 1)
                for x in range(EA + 1):
                    if x < EA:
                        scores(n, HEADS + x)
                    if x >= 1:
                        e = x - 1
                        dve.wait_ge(prob_ready, at(dve, n * UNITS + HEADS + e + 1))
                        link(nc.vector.reciprocal(mrs[:, e, :], msum[:, e, :]))
                        linked()
                        link(nc.vector.tensor_tensor(mw[:, e, :], mrs[:, e, :], gates_a[:, :, e], ALU.mult))
                        linked()
                        for s in range(3):
                            p = prob[:, e // 2 % 2, s, e % 2 * SEQ:(e % 2 + 1) * SEQ]
                            last = nc.vector.tensor_scalar(p, p, mw[:, e, s:s + 1], None, ALU.mult)
                            if s < 2:
                                link(last)
                        last.then_inc(mw_ready, 1)
                dve.wait_ge(moa_done, at(dve, n * 1 + 1))
                link(nc.vector.tensor_tensor(x2[:, 0:2, :], ACC[0][0:TT, :].rearrange("p (c d) -> p c d", c=2), src[:, 0:2, :], ALU.add))
                link(nc.vector.tensor_tensor(x2[:, 2, :], ACC[1][0:TT, 0:D], src[:, 2, :], ALU.add))
                linked()
                layer_norm(n, 3, x2)
                if m is not None:
                    dve.wait_ge(stored, at(dve, m * 16 + 16))
                link(nc.vector.tensor_tensor(resid[:], x2[:], h1[:], ALU.add))
                normalized(n, 3, x2, xn)
                dve.wait_ge(fg_done, at(dve, n * 1 + 1))
                link(nc.vector.tensor_copy(glog[0:TT], PT[0:TT, 0:3 * EF].rearrange("p (s e) -> p s e", s=3)))
                linked()
                link(gates_of(n, 1, TT, range(3), EF, gates_f))
                linked()
                link(nc.vector.tensor_copy(gpb[:, :, 0, :], gates_f[:]))
                linked()
                link(nc.vector.tensor_tensor(grest[:], gates_f[:], gpb[:, :, 0, :], ALU.subtract))
                linked()
                link(nc.vector.tensor_copy(gpb[:, :, 1, :], grest[:]))
                linked()
                link(nc.vector.tensor_tensor(gparts[:, :, 2, :], grest[:], gpb[:, :, 1, :], ALU.subtract))
                nc.vector.tensor_copy(gparts[:, :, 0:2, :].rearrange("p s a e -> p s (a e)"), gpb[:, :, 0:2, :].rearrange("p s a e -> p s (a e)")).then_inc(fgates_ready, 1)

            def queries(n, e):
                dve.wait_ge(q_done, at(dve, n * EA + e + 1))
                nc.vector.tensor_scalar(qm[:, e, :], (HB, GB)[e % 2][:, 0:PAIR], qb[:, e:e + 1], SCALE_Q, ALU.add, ALU.mult).then_inc(q_ready, 1)

            latent_attention(0, None)
            mixture_of_attention(0, None)
            restart()
            with dve.Fori(0, pairs - 1) as n:
                latent_attention(n + 1, n)
                mixture_of_attention(n + 1, n)
                restart()
            for e in range(EF):
                gate_hidden(pairs - 1, e)
            finish(pairs - 1)

        @block.tensor
        def _(pe):
            mm = nc.tensor.matmul
            I = ident

            pe.wait_ge(setup_dve, 1)
            for c in range(HALF):
                for k in range(HALF):
                    nc.tensor.transpose(S_BANKS[c][:, k * 128:(k + 1) * 128], wk_v[:, 0, k, c * 128:(c + 1) * 128], I[:])
            nc.tensor.transpose(PT[:, 0:128], reltab[:], I[:]).then_inc(setup_pe, 1)
            pe.wait_ge(setup_dve, 2)
            for k in range(HALF):
                for c in range(HALF):
                    last = mm(CT[:, k * LAT:(k + 1) * LAT], wkvT[:, c, k * 128:(k + 1) * 128], wdown[:, c, :], start=c == 0, stop=c == HALF - 1)
            last.then_inc(setup_pe, 1)
            pe.wait_ge(setup_dve, 3)
            pe.wait_ge(wpad_in, 16 * (HALF + 1 + 4))

            columns_ = patch_steps * GRID

            def embed(u):
                pe.wait_ge(pfeat, 2 * u + 2)
                if u >= 2:
                    pe.wait_ge(padd, u - 1)
                for k in range(PC):
                    last = mm((CT, PT)[u % 2][0:PR, 0:D], xpT[:, u % 2, k, :], wt[:, k, :], start=k == 0, stop=k == PC - 1)
                last.then_inc(pmm, 1)

            for u in range(columns_):
                if u and u % GRID == 0:
                    embed(u - 1)
                pe.wait_ge(pnorm, u + 1)
                for half in range(2):
                    if u:
                        pe.wait_ge(pfeat, 2 * (u - 1) + half + 1)
                    for c in range(3):
                        k = 3 * half + c
                        last = nc.tensor.transpose(S_BANKS[half][:, c * PR:(c + 1) * PR], xpn[:, u % 2, k * 128:(k + 1) * 128], I[0:PR, 0:PR])
                    last.then_inc(ptran, 1)
                if u % GRID:
                    embed(u - 1)
            embed(columns_ - 1)

            def transposes(n, k):
                pe.wait_ge(xn_ready, at(pe, n * XN + k + 1))
                for c in range(HALF):
                    for j in range(3):
                        last = nc.tensor.transpose(S_BANKS[c][:, j * TT:(j + 1) * TT], xn[:, j, c * 128:(c + 1) * 128], I[0:TT, 0:TT])
                    last.then_inc(xn_tran, 1)

            def project(n):
                pe.wait_ge(feat_ready, at(pe, n * FEAT + 2))
                def taken(k):
                    pe.wait_ge(proj_act, at(pe, n * PACT + k))

                for g in range(GROUPS):
                    if g >= 2:
                        taken(g - 1)
                    for k in range(HALF):
                        last = mm((CT, PT)[g % 2][:, 0:PAIR], wq[:, k, 4 * g:4 * g + 4, :].rearrange("p h d -> p (h d)"), xaT[:, k, :], start=k == 0, stop=k == 1)
                    last.then_inc(proj_done, 1)
                taken(3)
                for k in range(HALF):
                    last = mm(CT[0:LAT, 0:PAIR], wlat[:, k, :], xaT[:, k, :], start=k == 0, stop=k == 1)
                last.then_inc(proj_done, 1)
                taken(6)
                for g in range(GROUPS):
                    if g >= 2:
                        taken(5 + g)
                    mm((PT, CT)[g % 2][:, 0:PAIR], wupk[:, 4 * g:4 * g + 4, :].rearrange("p h d -> p (h d)"), latT[:, :], start=True, stop=True).then_inc(proj_done, 1)
                taken(9)
                halves = wupv[:, :].rearrange("l (h b d) -> l b h d", b=2, d=HD)
                places = PT[:, :].rearrange("p (a h b d) -> p a b h d", a=2, b=2, d=HD)
                for a in range(2):
                    for b in range(2):
                        k0 = a * SEQ + b * REM
                        last = mm(places[:, a, b], latT[:, k0:k0 + 128], halves[:, b], start=True, stop=True, skip_group_check=True)
                last.then_inc(proj_done, 1)
                taken(10)
                for a in range(2):
                    last = mm(CT[0:2 * REM, a * D:(a + 1) * D], latR[:, a, :], wupv[:, :], start=True, stop=True)
                last.then_inc(proj_done, 1)

            def head_scores(n, h):
                g, j = divmod(h, 4)
                if h == 0:
                    wait_all(pe, (proj_act, n * PACT + 11), (proj_dve, n + 1))
                if h >= 2:
                    pe.wait_ge(sc_taken, at(pe, n * UNITS + h - 1))
                for s, row, col, rows, a in SLOTS:
                    last = mm(S_BANKS[h % 2][row:row + rows, s * SEQ:(s + 1) * SEQ], qT[32 * j:32 * j + HD, g, col:col + rows],
                              kT[32 * j:32 * j + HD, g, a * SEQ:(a + 1) * SEQ], start=True, stop=True, tile_position=(32 * j, row))
                last.then_inc(sc_done, 1)

            def tran_main(n, u):
                p, h = divmod(u, 2)
                k = n * (3 * UNITS // 2) + 3 * p + h
                ready = prob_ready if u < HEADS else mw_ready
                value = n * UNITS + u + 1 if u < HEADS else n * EA + (u - HEADS) + 1
                if u == 0:
                    pe.wait_ge(ready, at(pe, value))
                else:
                    wait_all(pe, (ready, value), (pt_taken, k))
                for s in range(3):
                    last = nc.tensor.transpose(PT[:, s * 128:(s + 1) * 128], prob[:, p % 2, s, (SEQ + REM) * h:(SEQ + REM) * h + 128], I[:])
                last.then_inc(pt_done, 1)

            def tran_rem(n, p):
                pe.wait_ge(pt_taken, at(pe, n * (3 * UNITS // 2) + 3 * p + 2))
                for s in range(3):
                    last = nc.tensor.transpose(PT[0:2 * REM, s * 128:(s + 1) * 128], prob[:, p % 2, s, 128:128 + 2 * REM], I[:])
                last.then_inc(pt_done, 1)

            def group_values(n, g):
                value = n * (3 * UNITS // 2) + 6 * g + 6
                if g:
                    wait_all(pe, (pt_taken, value), (ctn_ready, n * GROUPS + g))
                else:
                    pe.wait_ge(pt_taken, at(pe, value))
                for a in range(2):
                    q0 = a * IMG1
                    for j in range(4):
                        mm(CT[32 * j:32 * j + 32, a * SEQ:(a + 1) * SEQ], v_main[:, a, 4 * g + j, :], ptm[:, j, q0:q0 + SEQ],
                           start=True, stop=False, tile_position=(0, 32 * j))
                    for j in range(4):
                        last = mm(CT[32 * j:32 * j + 32, a * SEQ:(a + 1) * SEQ], v_rem[:, a, 4 * g + j, :], ptr[:, j // 2, q0:q0 + SEQ],
                                  start=False, stop=True, tile_position=(0, 32 * j))
                last.then_inc(pv_done, 1)

            def group_divisors(n, g):
                wait_all(pe, (rsx_ready, n * GROUPS + g + 1), (cts_ready, n * (GROUPS + EA) + g + 1))
                for s in range(3):
                    last = mm(CT[:, s * 128:(s + 1) * 128], rsx[:, s, :], I[:], start=True, stop=True)
                last.then_inc(rb_done, 1)

            def out_project(n):
                pe.wait_ge(ctn_ready, at(pe, n * GROUPS + GROUPS))
                pe.wait_ge(sc_taken, at(pe, n * UNITS + HEADS))
                for j in range(3):
                    for g in range(GROUPS):
                        last = mm(S_BANKS[j // 2][0:TT, (j % 2) * D:(j % 2 + 1) * D], ctn[:, g, j * TT:(j + 1) * TT], wo[:, g, :],
                                  start=g == 0, stop=g == GROUPS - 1)
                last.then_inc(oproj_done, 1)

            def expert_up(m, e):
                if e == 0:
                    wait_all(pe, (fgT_ready, m * 2 + 2))
                else:
                    wait_all(pe, (gated_ready, m * EF + e))
                for k in range(HALF):
                    mm(HB[:, 0:PAIR], w1[:, e, k, :], x2T[:, k, :], start=k == 0, stop=k == 1)
                mm(GB[:, 0:PAIR], pick[:, e, :], partsT[:, :], start=True, stop=True).then_inc(up_done, 1)

            def into_tiles(first, last_, lhs, rhs, seq_start):
                for j in range(3):
                    i = mm(ACC[j // 2][0:TT, (j % 2) * D:(j % 2 + 1) * D], lhs(j), rhs,
                           start=seq_start and j != 1, stop=last_, skip_group_check=True)
                return i

            def expert_down(m, e):
                if e == 0:
                    into_tiles(True, False, lambda j: gatesT_f[:, j * TT:(j + 1) * TT], b2[:, :], True)
                pe.wait_ge(gated_ready, at(pe, m * EF + e + 1))
                into_tiles(False, e == EF - 1, lambda j: hg[:, e % 2, j * TT:(j + 1) * TT], w2[:, e, :], False).then_inc(down_done, 1)

            def latent_attention(n, m):
                transposes(n, 0)
                done = 0
                if m is not None:
                    expert_up(m, 0)
                    done = 1
                project(n)
                if m is not None:
                    while done < EXPERTS_BEFORE:
                        expert_down(m, done - 1)
                        expert_up(m, done)
                        done += 1
                for h in range(HEADS + 3):
                    if h < HEADS:
                        head_scores(n, h)
                    if m is not None and done < EF - EXPERTS_AFTER:
                        expert_down(m, done - 1)
                        expert_up(m, done)
                        done += 1
                    if 2 <= h < HEADS + 2:
                        tran_main(n, h - 2)
                    if h >= 3 and h % 2 == 1:
                        tran_rem(n, (h - 3) // 2)
                        if (h - 3) // 2 % 2 == 1:
                            g = (h - 3) // 4
                            group_values(n, g)
                            group_divisors(n, g)
                if m is not None:
                    while done < EF:
                        expert_down(m, done - 1)
                        expert_up(m, done)
                        done += 1
                    expert_down(m, EF - 1)
                out_project(n)

            def mixture_of_attention(n, m):
                pe.wait_ge(h_free, at(pe, n * 1 + 1))
                transposes(n, 1)
                pe.wait_ge(feat_ready, at(pe, n * FEAT + 4))
                for k in range(HALF):
                    last = mm(HB[:, 0:PAIR], kw[:, k, :], x1T[:, k, :], start=k == 0, stop=k == 1)
                last.then_inc(mk_done, 1)
                for b in range(2):
                    for a in range(2):
                        k0 = a * SEQ + b * REM
                        for k in range(HALF):
                            last = mm(GB[:, (2 * b + a) * 128:(2 * b + a + 1) * 128], x1T[:, k, k0:k0 + 128], vw[:, k, :], start=k == 0, stop=k == 1)
                last.then_inc(mk_done, 1)
                pe.wait_ge(x1r_ready, at(pe, n * HALF + 2))
                for a in range(2):
                    for k in range(HALF):
                        last = mm(CT[0:2 * REM, a * 128:(a + 1) * 128], x1R[:, k, a, :], vw[:, k, :], start=k == 0, stop=k == 1)
                last.then_inc(mk_done, 1)
                for s, row, col, rows, a in SLOTS:
                    for k in range(HALF):
                        last = mm(PT[row:row + rows, s * EA:(s + 1) * EA], x1T[:, k, col:col + rows], gatew[:, k, :], start=k == 0, stop=k == 1, tile_position=(0, row))
                last.then_inc(mk_done, 1)
                for e in range(EA + 1):
                    if e < EA:
                        if e == 0:
                            pe.wait_ge(mk_act, at(pe, n * 1 + 1))
                        elif e == 1:
                            pe.wait_ge(mk_dve, at(pe, n * 3 + 1))
                        else:
                            pe.wait_ge(q_ready, at(pe, n * EA + e - 1))
                        for k in range(HALF):
                            last = mm((HB, GB)[e % 2][:, 0:PAIR], qw[:, e, k, :], x1T[:, k, :], start=k == 0, stop=k == 1)
                        last.then_inc(q_done, 1)
                    if e >= 1:
                        x = e - 1
                        if x >= 2:
                            wait_all(pe, (q_ready, n * EA + x + 1), (rel_mid, n * EA + x - 1))
                        else:
                            pe.wait_ge(q_ready, at(pe, n * EA + x + 1))
                        for s, row, col, rows, a in SLOTS:
                            last = mm(S_BANKS[x % 2][row:row + rows, s * REL:(s + 1) * REL], qm[:, x, col:col + rows], relT[:, :],
                                      start=True, stop=True, tile_position=(0, row))
                        last.then_inc(rel_done, 1)
                wait_all(pe, (gates_ready, n + 1), (mk_dve, n * 3 + 3))
                for s in range(3):
                    last = nc.tensor.transpose(CT[0:EA, s * 128:(s + 1) * 128], gates_a[:, s, :], I[:])
                last.then_inc(gates_tran, 1)
                for x in range(EA + 4):
                    if x < EA:
                        if x < 2:
                            pe.wait_ge(rel_mid, at(pe, n * EA + EA - 1 + x))
                        else:
                            pe.wait_ge(sc_taken, at(pe, n * UNITS + HEADS + x - 1))
                        for s, row, col, rows, a in SLOTS:
                            last = mm(S_BANKS[x % 2][row:row + rows, s * SEQ:(s + 1) * SEQ], qm[:, x, col:col + rows], kmT[:, a * SEQ:(a + 1) * SEQ],
                                      start=True, stop=True, tile_position=(0, row))
                        last.then_inc(sc_done, 1)
                    if x == 1:
                        wait_all(pe, (gatesT_ready, n + 1))
                        if m is not None:
                            pe.wait_ge(y_ready, at(pe, m + 1))
                        into_tiles(True, False, lambda j: gatesT_a[:, j * TT:(j + 1) * TT], ob[:, :], True)
                    if 2 <= x < EA + 2:
                        tran_main(n, HEADS + x - 2)
                    if x >= 3 and x % 2 == 1 and x < EA + 3:
                        tran_rem(n, (HEADS + x - 3) // 2)
                        for e in (x - 3, x - 2):
                            base = n * (GROUPS + EA) + GROUPS
                            p = (HEADS + e) // 2
                            if e >= 2:
                                wait_all(pe, (pt_taken, n * (3 * UNITS // 2) + 3 * p + 3), (cts_ready, base + e - 1))
                            else:
                                wait_all(pe, (pt_taken, n * (3 * UNITS // 2) + 3 * p + 3))
                            for a in range(2):
                                q0 = a * IMG1
                                bank = (CT, HB)[e % 2]
                                mm(bank[:, a * SEQ:(a + 1) * SEQ], vm[:, e % 2, a, :], ptm[:, e % 4, q0:q0 + SEQ], start=True, stop=False)
                                last = mm(bank[:, a * SEQ:(a + 1) * SEQ], vmr[:, e % 2, a, :], ptr[:, p % 2, q0:q0 + SEQ], start=False, stop=True)
                            last.then_inc(pv_done, 1)
                        for e in (x - 3, x - 2):
                            pe.wait_ge(cts_ready, at(pe, base + e + 1))
                            last = into_tiles(False, e == EA - 1, lambda j: cm[:, e % 2, j * TT:(j + 1) * TT], ow[:, e, :], False)
                last.then_inc(moa_done, 1)
                transposes(n, 2)
                pe.wait_ge(feat_ready, at(pe, n * FEAT + 6))
                for j in range(3):
                    for k in range(HALF):
                        last = mm(PT[0:TT, j * EF:(j + 1) * EF], x2T[:, k, j * TT:(j + 1) * TT], fgatew[:, k, :], start=k == 0, stop=k == 1)
                last.then_inc(fg_done, 1)
                pe.wait_ge(fgates_ready, at(pe, n * 1 + 1))
                for j in range(3):
                    last = nc.tensor.transpose(CT[0:EF, j * TT:(j + 1) * TT], gates_f[:, j, :], I[0:TT, 0:TT])
                last.then_inc(fg_tran, 1)
                for j in range(3):
                    last = nc.tensor.transpose(PT[0:3 * EF, j * TT:(j + 1) * TT], gparts[:, j, :, :].rearrange("p a e -> p (a e)"), I[0:TT, 0:TT])
                last.then_inc(fg_tran, 1)

            latent_attention(0, None)
            mixture_of_attention(0, None)
            with pe.Fori(0, pairs - 1) as n:
                latent_attention(n + 1, n)
                mixture_of_attention(n + 1, n)
            expert_up(pairs - 1, 0)
            for e in range(1, EF):
                expert_down(pairs - 1, e - 1)
                expert_up(pairs - 1, e)
            expert_down(pairs - 1, EF - 1)


LOADS = 16 * 8


def constants():
    import numpy as np
    f = np.float32
    c = {"ident": np.eye(128, dtype=f)}
    y, x = np.meshgrid(np.arange(GRID), np.arange(GRID), indexing="ij")
    omega = np.arange(D // 4, dtype=f) / f(D // 4 - 1)
    omega = (f(1.0) / np.power(f(10000.0), omega)).astype(f)
    y = y.reshape(-1)[:, None].astype(f) * omega[None]
    x = x.reshape(-1)[:, None].astype(f) * omega[None]
    pe = np.concatenate((np.sin(x), np.cos(x), np.sin(y), np.cos(y)), axis=1).astype(f)
    c["pe"] = np.ascontiguousarray(np.tile(pe.reshape(GRID, GRID, D), (16, 1, 1)))
    k = np.arange(SEQ, dtype=f)
    dec = np.ones((128, 3, SEQ), f)
    for s, row, col, rows, a in SLOTS:
        q = np.arange(rows) + col - a * SEQ
        q = np.clip(q, 0, SEQ - 1).astype(f)
        dec[row:row + rows, s] = np.exp(f(-0.01) * np.abs(q[:, None] - k[None])) / f(16.0)
    c["decay"] = dec
    top = (np.arange(2 * REM) < REM)
    even = (np.arange(HEADS) % 2 == 0)
    c["mask_rows"] = np.ascontiguousarray(np.repeat((top[:, None] == even[None])[:, :, None], HD, 2).astype(f))
    c["mask_cols"] = np.stack([top, ~top], 1).astype(f)
    c["iota"] = np.tile(np.arange(EF, dtype=f), (128, 1))
    pick = np.zeros((3, EF, EF, 128), f)
    for e in range(EF):
        pick[:, e, e] = 1
    c["pick"] = pick.reshape(3 * EF, EF, 128)
    return c


def kernel(**inputs):
    import numpy as np
    import concourse.bacc as bacc
    from concourse.bass_utils import run_bass_kernel_spmd

    nc = bacc.Bacc("TRN2", target_bir_lowering=False, num_devices=1)
    arrays, aps = {}, {}
    for name, a in {**inputs, **constants()}.items():
        a = np.ascontiguousarray(a)
        arrays[f"in_{name}"] = a
        aps[name] = nc.dram_tensor(f"in_{name}", a.shape, mybir.dt.from_np(a.dtype), kind="ExternalInput").ap()
    shape = (inputs["x"].shape[0], SEQ, D)
    out = nc.dram_tensor("out", shape, F32, kind="ExternalOutput").ap()
    early_fusion(nc, aps, out)
    r = run_bass_kernel_spmd(nc, [arrays], core_ids=[0])
    return r.results[0]["out"]
```

```python
import concourse.bass as bass
from concourse import mybir
from concourse.alu_op_type import AluOpType as ALU
from contextlib import ExitStack

F32 = mybir.dt.float32
BF16 = mybir.dt.bfloat16
U32 = mybir.dt.uint32
ACT = mybir.ActivationFunctionType
AX = mybir.AxisListType

D = 256
HALF = D // 128
PATCH, CH, GRID = 16, 3, 6
NPATCH = GRID * GRID
TXT = 128
SEQ = 1 + NPATCH + TXT
PAIR = 2 * SEQ
TT = PAIR // 3
PF = CH * PATCH * PATCH
PC = PF // 128
HEADS, HD, GROUPS = 16, 16, 4
LAT = 64
EA, EF = 8, 16
MAXP = 64
REL = 2 * MAXP + 1
SIDE = SEQ - 1 - MAXP
REM = SEQ - 128
WIDE = 384
IMG1 = WIDE - SEQ
SPAN = 2 * SEQ - 1
EPS = 1e-5
ARENA = 26200
SLOTS = [(0, 0, 0, 128, 0), (1, 0, 128, 64, 0), (1, 64, 138, 64, 1), (2, 0, 202, 128, 1)]

HEAD_STEPS = HEADS + 4
GATE_STEP = 3
EXPERT_STEPS = (4, 5, 7, 9, 11, 13, 14, 15, 16, 17, 18, 19)


FIRST_SCORES = 6


def spread(ap, n):
    return bass.AP(ap.tensor, ap.offset, [list(ap.ap[0]), [0, n], list(ap.ap[-1])])


def columns(ap, n):
    return bass.AP(ap.tensor, ap.offset, [list(x) for x in ap.ap] + [[0, n]])


def ends_of(ap):
    return bass.AP(ap.tensor, ap.offset + 128, [list(ap.ap[0]), [SEQ, 2], [-128, 2], [1, REM]])


def at(eng, value):
    return value if isinstance(value, int) else eng.to_reg(value)


def wait_all(eng, *pairs):
    found = [(sem, at(eng, value)) for sem, value in pairs]
    for sem, value in found:
        eng.wait_ge(sem, value)


def early_fusion(nc, t, out):
    images = t["x"].shape[0]
    pairs = images // 2
    PI = min(16, images)
    PR = PI * GRID
    patch_steps = images // PI
    SCALE_Q = 128.0 ** -0.5

    ctx = ExitStack()
    with ctx:
        def sb(name, shape, dt=F32):
            return ctx.enter_context(nc.sbuf_tensor(name, shape, dt))

        arena = sb("arena", [128, ARENA])
        ends = {"early": 0, "late": 0}

        def within(when, shape):
            size = 1
            for x in shape[1:]:
                size *= x
            at = ends[when]
            ends[when] = at + size
            assert ends[when] <= ARENA, ends
            v = arena[0:shape[0], at:at + size]
            names = ["a", "b", "c", "d"][:len(shape) - 1]
            if len(names) == 1:
                return v
            return v.rearrange(f"p ({' '.join(names)}) -> p {' '.join(names)}", **dict(zip(names, shape[1:])))

        def sem(name):
            return ctx.enter_context(nc.semaphore(name))

        banks = [ctx.enter_context(nc.psum_tensor(f"bank{b}", [128, 512], F32)) for b in range(8)]
        S_BANKS = banks[0:2]
        PT, CT, HB, GB = banks[2], banks[3], banks[4], banks[5]
        ACC = banks[6:8]

        tokens_dram = nc.dram_tensor("patch_tokens", [images * NPATCH, D], F32)
        cls_dram = nc.dram_tensor("cls_rows", [2, D], F32)
        span_dram = nc.dram_tensor("rel_span", [EA, 3 * 128, SPAN], F32)

        ident = sb("ident", [128, 128])
        wt = within("early", [128, PC, D])
        ln1g = sb("ln1g", [128, PC])
        ln1b = sb("ln1b", [128, PC])
        tbias = within("early", [128, D])
        ln2g = within("early", [128, D])
        peb = within("early", [PR, GRID, D])
        tln2b = within("early", [128, D])
        wq = sb("wq", [128, HALF, HEADS, 32])
        wk_v = within("early", [128, 2, HALF, D])
        wkvT = within("early", [128, HALF, D])
        wdown = sb("wdown", [128, HALF, LAT])
        wlat = sb("wlat", [128, HALF, LAT])
        wupk = sb("wupk", [LAT, HEADS, 32])
        wupv = sb("wupv", [LAT, D])
        wo = sb("wo", [128, GROUPS, D])
        decay = sb("decay", [128, 3, SEQ])
        maskr = sb("maskr", [2 * REM, HEADS, HD])
        maskc = sb("maskc", [2 * REM, 2])
        iota = sb("iota", [128, EF])
        lnw = sb("lnw", [128, 4, HALF])
        gatew = sb("gatew", [128, HALF, EA])
        qw = sb("qw", [128, EA, HALF, 128])
        qb = sb("qb", [128, EA])
        qbs = sb("qbs", [128, EA])
        kw = sb("kw", [128, HALF, 128])
        kb = sb("kb", [128, 1])
        vw = sb("vw", [128, HALF, 128])
        vb = sb("vb", [128, 128])
        vbm = sb("vbm", [2 * REM, 2, 128])
        ow = sb("ow", [128, EA, D])
        ob = sb("ob", [EA, D])
        reltab = within("early", [128, 128])
        relT = sb("relT", [128, REL])
        fgatew = sb("fgatew", [128, HALF, EF])
        w1 = sb("w1", [128, EF, HALF, 128])
        b1 = sb("b1", [128, EF])
        w2 = sb("w2", [128, EF, D])
        b2 = sb("b2", [EF, D])
        pick_f = within("early", [3 * EF, EF, 128])
        pick = sb("pick", [3 * EF, EF, 128], BF16)
        neghalf = sb("neghalf", [128, GRID])
        clsr = within("early", [2, D])
        clsp = within("early", [2, D])

        xin = within("early", [PR, CH * PATCH, GRID * PATCH])
        xpn = within("early", [PR, 2, PF])
        xpT = within("early", [128, 2, PC, PR])
        ytok = within("early", [PR, GRID, D])
        pst = sb("pst", [PR, GRID, 2, 6])
        pmv = sb("pmv", [PR, GRID, 2])
        pve = sb("pve", [PR, GRID])
        prs = sb("prs", [PR, GRID])

        h_in = sb("h_in", [TT, 3, D])
        h1 = sb("h1", [TT, 3, D])
        src = sb("src", [TT, 3, D])
        x2 = src
        resid = sb("resid", [TT, 3, D])
        xn = sb("xn", [TT, 3, D])
        st = sb("st", [TT, 3, 6])
        mv = sb("mv", [TT, 3, 2])
        ve = sb("ve", [TT, 3])
        rs = sb("rs", [TT, 3])
        xaT = within("late", [128, HALF, PAIR])
        x1T = within("late", [128, HALF, PAIR])
        x2T = within("late", [128, HALF, PAIR])
        qT = within("late", [128, GROUPS, PAIR])
        kT = within("late", [128, GROUPS, PAIR])
        latT = within("late", [LAT, PAIR])
        latR = within("late", [LAT, 2, 2 * REM])
        x1R = within("late", [128, HALF, 2, 2 * REM])
        rsx = within("late", [128, 3, 128])
        v_main = sb("v_main", [128, 2, HEADS, 32])
        v_rem = sb("v_rem", [2 * REM, 2, HEADS, 32])
        sc = within("late", [128, 2, 3, SEQ])
        nmax = sb("nmax", [128, 2, 3])
        prob = within("late", [128, 2, 3, 2 * SEQ])
        pt_area = within("late", [128, 6 * WIDE])
        ptm = pt_area[:, 0:4 * WIDE].rearrange("p (u q) -> p u q", u=4)
        ptr = pt_area[0:2 * REM, 4 * WIDE:6 * WIDE].rearrange("p (u q) -> p u q", u=2)
        sums = sb("sums", [128, 3, HEADS])
        rsum = sb("rsum", [128, 3, HEADS])
        cts = within("late", [128, PAIR])
        ctn = within("late", [128, GROUPS, PAIR])
        kmT = within("late", [128, PAIR])
        vm = within("late", [128, 2, 2, 128])
        vmr = within("late", [2 * REM, 2, 2, 128])
        qm = within("late", [128, EA, PAIR])
        span_own = within("late", [128, 2, 3, SPAN])
        span_lent = pt_area[:, 0:6 * SPAN].rearrange("p (u s w) -> p u s w", u=2, s=3)
        spans_of = [span_lent[:, 0], span_lent[:, 1], span_own[:, 0], span_own[:, 1]]
        bias = within("late", [128, EA, 3, SEQ])
        glog = sb("glog", [128, 3, EF])
        gtop = sb("gtop", [128, 3, 8])
        gidx = sb("gidx", [128, 3, 8], U32)
        gidf = sb("gidf", [128, 3, 2])
        gd = sb("gd", [128, 3])
        ge = sb("ge", [128, 3])
        gs = sb("gs", [128, 3])
        g1 = sb("g1", [128, 3])
        g2 = sb("g2", [128, 3])
        ga = sb("ga", [128, 3, EF])
        gb = sb("gb", [128, 3, EF])
        gates_a = sb("gates_a", [128, 3, EA])
        gatesT_a = sb("gatesT_a", [EA, PAIR])
        msum = sb("msum", [128, EA, 3])
        mrs = sb("mrs", [128, EA, 3])
        mw = sb("mw", [128, EA, 3])
        cm = within("late", [128, 2, PAIR])
        gates_f = sb("gates_f", [TT, 3, EF])
        gparts = sb("gparts", [TT, 3, 3, EF])
        gpb = sb("gpb", [TT, 3, 3, EF], BF16)
        grest = sb("grest", [TT, 3, EF])
        gatesT_f = sb("gatesT_f", [EF, PAIR])
        partsT = sb("partsT", [3 * EF, PAIR], BF16)
        hr = within("late", [128, PAIR])
        hg = within("late", [128, 2, PAIR])

        w_in = sem("w_in")
        bias_zero = sem("bias_zero")
        pool_turn = sem("pool_turn")
        vector_turn = sem("vector_turn")
        zeroed = sem("zeroed")
        wpad_in = sem("wpad_in")
        x_in = sem("x_in")
        pvar = sem("pvar")
        prstd = sem("prstd")
        pnorm = sem("pnorm")
        ptran = sem("ptran")
        pfeat = sem("pfeat")
        pmm = sem("pmm")
        padd = sem("padd")
        ptok = sem("ptok")
        pst_out = sem("pst_out")
        dve_step = sem("dve_step")
        cls_sum = sem("cls_sum")
        cls_out = sem("cls_out")
        setup_pe = sem("setup_pe")
        setup_dve = sem("setup_dve")

        h_loaded = sem("h_loaded")
        h_free = sem("h_free")
        var_ready = sem("var_ready")
        rstd_ready = sem("rstd_ready")
        xn_ready = sem("xn_ready")
        xn_tran = sem("xn_tran")
        feat_ready = sem("feat_ready")
        proj_done = sem("proj_done")
        proj_act = sem("proj_act")
        proj_dve = sem("proj_dve")
        avar_ready = sem("avar_ready")
        arstd_ready = sem("arstd_ready")
        axn_ready = sem("axn_ready")
        axn_tran = sem("axn_tran")
        afeat_ready = sem("afeat_ready")
        sc_done = sem("sc_done")
        sc_taken = sem("sc_taken")
        max_ready = sem("max_ready")
        prob_ready = sem("prob_ready")
        pt_done = sem("pt_done")
        pt_taken = sem("pt_taken")
        pv_done = sem("pv_done")
        cts_ready = sem("cts_ready")
        rsum_ready = sem("rsum_ready")
        rsx_ready = sem("rsx_ready")
        x1r_ready = sem("x1r_ready")
        rb_done = sem("rb_done")
        ctn_ready = sem("ctn_ready")
        oproj_done = sem("oproj_done")
        oproj_taken = sem("oproj_taken")
        mk_done = sem("mk_done")
        mk_act = sem("mk_act")
        mk_dve = sem("mk_dve")
        top_diff = sem("top_diff")
        top_exp = sem("top_exp")
        gates_ready = sem("gates_ready")
        gates_tran = sem("gates_tran")
        gatesT_ready = sem("gatesT_ready")
        q_done = sem("q_done")
        q_ready = sem("q_ready")
        rel_done = sem("rel_done")
        rel_mid = sem("rel_mid")
        rel_ready = sem("rel_ready")
        span_out = [sem(f"span_out{b}") for b in range(4)]
        bias_in = [sem(f"bias_in{e}") for e in range(EA)]
        mw_ready = sem("mw_ready")
        moa_done = sem("moa_done")
        fg_done = sem("fg_done")
        fgates_ready = sem("fgates_ready")
        fg_tran = sem("fg_tran")
        fgT_ready = sem("fgT_ready")
        up_done = sem("up_done")
        relu_ready = sem("relu_ready")
        gated_ready = sem("gated_ready")
        down_done = sem("down_done")
        y_ready = sem("y_ready")
        stored = sem("stored")
        smax_free = sem("smax_free")

        WLOADS = 0

        block = ctx.enter_context(nc.Block())

        XN, TRAN, FEAT = 2, 4, 4
        UNITS = HEADS + EA
        PROJ, PACT = 11, 11

        @block.sync
        def _(sp):
            for step in range(patch_steps):
                if step:
                    sp.wait_ge(pvar, 2 * step)
                for c in range(CH):
                    sp.dma_start(xin[:, c * PATCH:(c + 1) * PATCH, :].rearrange("r p w -> r (p w)"),
                                 t["x"][step * PI:(step + 1) * PI, c].rearrange("b (g p) w -> b g (p w)", g=GRID)
                                 ).then_inc(x_in, 16)
                if step:
                    sp.wait_ge(ptok, step)
                    sp.dma_start(tokens_dram[(step - 1) * PI * NPATCH:step * PI * NPATCH, :].rearrange("(r w) d -> r (w d)", w=GRID),
                                 ytok[:, :, :].rearrange("r w d -> r (w d)")).then_inc(pst_out, 16)
            sp.wait_ge(ptok, patch_steps)
            sp.dma_start(tokens_dram[(patch_steps - 1) * PI * NPATCH:patch_steps * PI * NPATCH, :].rearrange("(r w) d -> r (w d)", w=GRID),
                         ytok[:, :, :].rearrange("r w d -> r (w d)")).then_inc(pst_out, 16)
            sp.wait_ge(cls_sum, 1)
            sp.dma_start(cls_dram[:, :], clsr[:, :]).then_inc(cls_out, 16)
            sp.wait_ge(cls_out, 16)
            sp.wait_ge(pst_out, 16 * patch_steps)

            def load(n):
                if not (isinstance(n, int) and n == 0):
                    sp.wait_ge(h_free, at(sp, n * 1))
                pieces = []
                for a in range(2):
                    pieces += [("c", a, 0, a * SEQ, 1), ("p", a, 0, a * SEQ + 1, NPATCH), ("t", a, 0, a * SEQ + 1 + NPATCH, TXT)]
                for kind, a, first, row, count in pieces:
                    while count:
                        tile, r = divmod(row, TT)
                        m = min(count, TT - r)
                        if kind == "c":
                            s = cls_dram[a:a + 1, :]
                        elif kind == "p":
                            s = tokens_dram[bass.ds(n * 2 * NPATCH + a * NPATCH + first, m), :]
                        else:
                            s = t["txt"].rearrange("b s d -> (b s) d")[bass.ds(n * 2 * TXT + a * TXT + first, m), :]
                        sp.dma_start(h_in[r:r + m, tile, :], s).then_inc(h_loaded, 16)
                        first, row, count = first + m, row + m, count - m

            def spans(n):
                for e in range(EA):
                    sp.wait_ge(rel_ready, at(sp, n * EA + e + 1))
                    sp.dma_start(span_dram[e].rearrange("(s p) w -> p s w", p=128), spans_of[e % 4]).then_inc(span_out[e % 4], 16)
                    if e >= 1:
                        skew(n, e - 1)
                skew(n, EA - 1)

            def skew(n, e):
                r = at(sp, n * (EA // 4 * 16) + (e // 4 + 1) * 16)
                sp.wait_ge(span_out[e % 4], r)
                base = e * 3 * 128 * SPAN
                T = span_dram[:, :, :].tensor
                for slot, row, rows, q0 in ((0, 0, 128, 0), (2, 0, 128, REM), (1, 0, REM, 128), (1, 128 - REM, REM, 0)):
                    s = bass.AP(T, base + (slot * 128 + row) * SPAN + SEQ - 1 - q0, [[SPAN - 1, rows], [1, SEQ]])
                    sp.dma_start(bias[row:row + rows, e, slot, :], s).then_inc(bias_in[e], 16)

            def store(n):
                rows = out.rearrange("b s d -> (b s) d")
                r = at(sp, n * 1 + 1)
                sp.wait_ge(y_ready, r)
                sp.dma_start(rows[bass.ds(n * PAIR, PAIR), :].rearrange("(c p) d -> p c d", p=TT), resid[:, :, :]).then_inc(stored, 16)

            load(0)
            sp.wait_ge(bias_zero, 1)
            load(1)
            spans(0)
            with sp.Fori(0, pairs - 2) as n:
                load(n + 2)
                store(n)
                spans(n + 1)
            store(pairs - 2)
            spans(pairs - 1)
            store(pairs - 1)
            sp.wait_ge(stored, 16 * pairs)

        @block.gpsimd
        def _(pool):
            for z in (wq, wupk, wo, v_main, v_rem):
                pool.memset(z[:], 0.0).then_inc(zeroed, 1)
            pool.memset(neghalf[:], -0.5).then_inc(zeroed, 1)
            pool.wait_ge(zeroed, 6)
            for step in range(patch_steps):
                for k in range(2):
                    pool.wait_ge(pvar, 2 * step + k + 1)
                    nc.gpsimd.tensor_tensor(prs[:, :], pve[:, :], neghalf[0:PR, :], ALU.pow).then_inc(prstd, 1)

            pool.wait_ge(ptok, patch_steps)
            pool.memset(bias[:, :, :, :], 0.0).then_inc(bias_zero, 1)

            def inverse_root(var, rstd, k):
                pool.wait_ge(var, at(pool, k))
                nc.gpsimd.tensor_tensor(rs[:, :], ve[:, :], neghalf[0:TT, 0:3], ALU.pow).then_inc(rstd, 1)

            def pair(n, more):
                for g in range(GROUPS):
                    if g:
                        wait_all(pool, (rsum_ready, n * GROUPS + g + 1), (rb_done, n * GROUPS + g))
                    else:
                        pool.wait_ge(rsum_ready, at(pool, n * GROUPS + 1))
                    pool.sem_inc(pool_turn, 1)
                    nc.gpsimd.tensor_copy(rsx[:, :, :].rearrange("p s (h d) -> p s h d", d=32), columns(rsum[:, :, 4 * g:4 * g + 4], 32)).then_inc(rsx_ready, 1)
                inverse_root(var_ready, rstd_ready, n * 3 + 1)
                inverse_root(var_ready, rstd_ready, n * 3 + 2)
                for k in range(HALF):
                    pool.wait_ge(feat_ready, at(pool, n * FEAT + 1 + k))
                    pool.sem_inc(pool_turn, 1)
                    nc.gpsimd.tensor_copy(x1R[:, k].rearrange("p a (b r) -> p a b r", b=2), ends_of(x1T[:, k, :])).then_inc(x1r_ready, 1)
                if more:
                    inverse_root(avar_ready, arstd_ready, n + 2)
                inverse_root(var_ready, rstd_ready, n * 3 + 3)

            inverse_root(avar_ready, arstd_ready, 1)
            pair(0, True)
            with pool.Fori(0, pairs - 2) as n:
                pair(n + 1, True)
            pair(pairs - 1, False)

        @block.scalar
        def _(act):
            def load(dst, source):
                nonlocal WLOADS
                act.dma_start(dst, source, allow_slow_non_contiguous=True).then_inc(w_in, 16)
                WLOADS += 16

            load(ident[:], t["ident"])
            tw = t["L0_tok_W"].rearrange("(h p c) d -> p c h d", p=128, c=CH)
            for c in range(CH):
                load(wt[:, 2 * c:2 * c + 2, :], tw[:, c])
            for dst, name in ((ln1g, "L0_tok_ln1_g"), (ln1b, "L0_tok_ln1_b")):
                v = t[name].rearrange("(h p c) -> p c h", p=128, c=CH)
                for c in range(CH):
                    load(dst[:, 2 * c:2 * c + 2], v[:, c])
            for dst, name in ((tbias, "L0_tok_bias"), (ln2g, "L0_tok_ln2_g"), (tln2b, "L0_tok_ln2_b")):
                load(dst[:], t[name].partition_broadcast(128))
            load(peb[:], t["pe"][0:PR])
            for r in range(2):
                load(clsr[r:r + 1, :], t["L0_tok_cls_token"].rearrange("a b d -> (a b) d"))
                load(clsp[r:r + 1, :], t["L0_tok_cls_pos_embedding"].rearrange("a b d -> (a b) d"))
            load(wk_v[:, 0], t["L0_attn_W_k"].rearrange("(k p) d -> p k d", p=128))
            load(wk_v[:, 1], t["L0_attn_W_v"].rearrange("(k p) d -> p k d", p=128))
            load(wdown[:], t["L0_attn_W_down_kv"].rearrange("(k p) d -> p k d", p=128))
            load(wupv[:], t["L0_attn_W_up_v"])
            load(decay[:], t["decay"])
            load(maskr[:], t["mask_rows"])
            load(maskc[:], t["mask_cols"])
            load(iota[:], t["iota"])
            for k, name in enumerate(("ln1_w", "ln1_b", "ln2_w", "ln2_b")):
                load(lnw[:, k, :], t["L0_ffn_" + name].rearrange("(k p) -> p k", p=128))
            load(gatew[:], t["L0_ffn_attn_gate_w"].rearrange("(k p) e -> p k e", p=128))
            for k in range(HALF):
                load(qw[:, :, k, :], t["L0_ffn_q_w"][:, k * 128:(k + 1) * 128, :].rearrange("e p h -> p e h"))
                load(w1[:, :, k, :], t["L0_ffn_ff_w1"][:, k * 128:(k + 1) * 128, :].rearrange("e p h -> p e h"))
            load(qb[:], t["L0_ffn_q_b"].rearrange("e h -> h e"))
            load(kw[:], t["L0_ffn_k_w"].rearrange("(k p) d -> p k d", p=128))
            load(kb[:], t["L0_ffn_k_b"].rearrange("(p o) -> p o", o=1))
            load(vw[:], t["L0_ffn_v_w"].rearrange("(k p) d -> p k d", p=128))
            load(vb[:], t["L0_ffn_v_b"].partition_broadcast(128))
            load(ow[:], t["L0_ffn_o_w"].rearrange("e h d -> h e d"))
            load(ob[:], t["L0_ffn_o_b"])
            load(reltab[:], t["L0_ffn_rel_table"][0:128])
            load(relT[:, 128:REL], t["L0_ffn_rel_table"][128:REL].rearrange("r h -> h r"))
            load(fgatew[:], t["L0_ffn_ff_gate_w"].rearrange("(k p) e -> p k e", p=128))
            load(b1[:], t["L0_ffn_ff_b1"].rearrange("e h -> h e"))
            load(w2[:], t["L0_ffn_ff_w2"].rearrange("e h d -> h e d"))
            load(b2[:], t["L0_ffn_ff_b2"])
            load(pick_f[:], t["pick"])
            act.wait_ge(zeroed, 6)
            for k in range(HALF):
                act.dma_start(wq[:, k, :, 0:HD], t["L0_attn_W_q"][k * 128:(k + 1) * 128, :].rearrange("p (h d) -> p h d", d=HD)).then_inc(wpad_in, 16)
            act.dma_start(wupk[:, :, 0:HD], t["L0_attn_W_up_k"].rearrange("l (h d) -> l h d", d=HD)).then_inc(wpad_in, 16)
            for j in range(4):
                act.dma_start(wo[32 * j:32 * j + HD, :, :],
                              t["L0_attn_W_o"].rearrange("(g j d) n -> j d g n", g=GROUPS, j=4)[j]).then_inc(wpad_in, 16)

            act.wait_ge(w_in, WLOADS)
            for step in range(patch_steps):
                for w in range(GRID):
                    u = step * GRID + w
                    if u >= 2:
                        act.wait_ge(pmm, u - 1)
                    for half in range(2):
                        act.wait_ge(ptran, 2 * u + half + 1)
                        for c in range(3):
                            k = 3 * half + c
                            last = nc.scalar.activation(xpT[:, u % 2, k, :], S_BANKS[half][:, c * PR:(c + 1) * PR], ACT.Identity,
                                                        bias=ln1b[:, k:k + 1], scale=ln1g[:, k:k + 1])
                        last.then_inc(pfeat, 1)

            def features(n, k, dst, gain):
                for c in range(HALF):
                    act.wait_ge(xn_tran, at(act, n * TRAN + 2 * k + c + 1))
                    nc.scalar.activation(dst[:, c, :], S_BANKS[c][:, 0:PAIR], ACT.Identity,
                                         bias=lnw[:, gain + 1, c:c + 1], scale=lnw[:, gain, c:c + 1]).then_inc(feat_ready, 1)

            def early_features(p, c):
                act.wait_ge(axn_tran, at(act, p * 2 + c + 1))
                nc.scalar.copy(xaT[:, c, :], GB[:, 0:PAIR]).then_inc(afeat_ready, 1)

            def take_queries(p):
                for g in range(GROUPS):
                    act.wait_ge(proj_done, at(act, p * PROJ + g + 1))
                    nc.scalar.copy(qT[:, g, :], (CT, PT)[g % 2][:, 0:PAIR]).then_inc(proj_act, 1)

            def take_latent(p):
                act.wait_ge(proj_done, at(act, p * PROJ + 5))
                nc.scalar.copy(latT[:, :], CT[0:LAT, 0:PAIR]).then_inc(proj_act, 1)
                nc.scalar.copy(latR[:, :, :].rearrange("p a (b r) -> p a b r", b=2), ends_of(CT[0:LAT, 0:PAIR])).then_inc(proj_act, 1)

            def take_keys(p):
                for g in range(GROUPS):
                    act.wait_ge(proj_done, at(act, p * PROJ + 6 + g))
                    nc.scalar.copy(kT[:, g, :], (PT, CT)[g % 2][:, 0:PAIR]).then_inc(proj_act, 1)

            def take_values(p):
                act.wait_ge(proj_done, at(act, p * PROJ + 10))
                nc.scalar.copy(v_main[:, :, :, 0:HD].rearrange("p a h d -> p (a h) d"), PT[:, :].rearrange("p (h d) -> p h d", d=HD)).then_inc(proj_act, 1)

            def softmax_row(n, u, parity):
                act.wait_ge(max_ready, at(act, n * UNITS + u + 1))
                for s in range(3):
                    acc = sums[:, s, u:u + 1] if u < HEADS else msum[:, u - HEADS, s:s + 1]
                    last = nc.scalar.activation(prob[:, parity, s, u % 2 * SEQ:(u % 2 + 1) * SEQ], sc[:, u % 2, s, :], ACT.Exp,
                                                bias=nmax[:, u % 2, s:s + 1], scale=1.0, accum_out=acc)
                last.then_inc(prob_ready, 1)

            def take_main(n, u):
                p, h = divmod(u, 2)
                act.wait_ge(pt_done, at(act, n * (3 * UNITS // 2) + 3 * p + h + 1))
                nc.scalar.copy(ptm[:, u % 4, :], PT[:, 0:WIDE]).then_inc(pt_taken, 1)

            def take_rem(n, p):
                act.wait_ge(pt_done, at(act, n * (3 * UNITS // 2) + 3 * p + 3))
                nc.scalar.copy(ptr[:, p % 2, :], PT[0:2 * REM, 0:WIDE]).then_inc(pt_taken, 1)

            def relu(m, e):
                if e == 0:
                    act.wait_ge(up_done, at(act, m * EF + 1))
                else:
                    wait_all(act, (up_done, m * EF + e + 1), (gated_ready, m * EF + e))
                nc.scalar.activation(hr[:, :], HB[:, 0:PAIR], ACT.Relu, bias=b1[:, e:e + 1], scale=1.0).then_inc(relu_ready, 1)

            def top_exp_step(n, k):
                act.wait_ge(top_diff, at(act, n * 2 + k + 1))
                rows = 128 if k == 0 else TT
                nc.scalar.activation(ge[0:rows, :], gd[0:rows, :], ACT.Exp).then_inc(top_exp, 1)

            def gate_rows(m):
                act.wait_ge(fg_tran, at(act, m * 2 + 1))
                nc.scalar.copy(gatesT_f[:, :], HB[0:EF, 0:PAIR]).then_inc(fgT_ready, 1)
                act.wait_ge(fg_tran, at(act, m * 2 + 2))
                nc.scalar.copy(partsT[:, :], GB[0:3 * EF, 0:PAIR]).then_inc(fgT_ready, 1)

            def latent_attention(n, m):
                e = 0
                for h in range(HEAD_STEPS):
                    if m is not None and h in EXPERT_STEPS and h >= HEADS:
                        relu(m, e)
                        e += 1
                    if h % 2 == 0 and h >= 4:
                        take_rem(n, (h - 4) // 2)
                    if h >= 6 and h % 4 == 2:
                        g = (h - 6) // 4
                        act.wait_ge(pv_done, at(act, n * (GROUPS + EA) + g + 1))
                        nc.scalar.copy(cts[:, :], CT[:, 0:PAIR]).then_inc(cts_ready, 1)
                    if 2 <= h < HEADS + 2:
                        take_main(n, h - 2)
                    if h == GATE_STEP and m is not None:
                        gate_rows(m)
                    if h == 0:
                        take_values(n)
                    if h < HEADS:
                        softmax_row(n, h, (h // 2) % 2)
                    if m is not None and h in EXPERT_STEPS and h < HEADS:
                        relu(m, e)
                        e += 1
                if m is not None:
                    for e in range(len(EXPERT_STEPS), EF):
                        relu(m, e)

            def mixture_of_attention(n, more):
                features(n, 0, x1T, 0)
                act.wait_ge(mk_done, at(act, n * 4 + 1))
                nc.scalar.activation(kmT[:, :], HB[:, 0:PAIR], ACT.Identity, bias=kb[:, 0:1], scale=1.0).then_inc(mk_act, 1)
                top_exp_step(n, 0)
                for e in range(EA + 1):
                    if e < EA:
                        act.wait_ge(q_done, at(act, n * EA + e + 1))
                        nc.scalar.activation(qm[:, e, :], (HB, GB)[e % 2][:, 0:PAIR], ACT.Identity, bias=qbs[:, e:e + 1], scale=SCALE_Q).then_inc(q_ready, 1)
                    if e >= 1:
                        x = e - 1
                        if x >= 4:
                            wait_all(act, (rel_done, n * EA + x + 1), (span_out[x % 4], n * (EA // 4 * 16) + 16))
                        else:
                            act.wait_ge(rel_done, at(act, n * EA + x + 1))
                        nc.scalar.copy(spans_of[x % 4][:, :, SIDE:SIDE + REL],
                                       (CT, PT)[x % 2][:, 0:3 * REL].rearrange("p (s r) -> p s r", s=3)).then_inc(rel_mid, 1)
                    if e >= FIRST_SCORES + 1:
                        softmax_row(n, HEADS + e - FIRST_SCORES - 1, 0)
                softmax_row(n, HEADS + 2, 1)
                wait_all(act, (span_out[0], n * (EA // 4 * 16) + 32), (span_out[1], n * (EA // 4 * 16) + 32))
                for x in range(2, EA + 5):
                    if x % 2 == 0 and 4 <= x < EA + 4:
                        take_rem(n, (HEADS + x - 4) // 2)
                    if 2 <= x < EA + 2:
                        take_main(n, HEADS + x - 2)
                    if 3 <= x < EA:
                        softmax_row(n, HEADS + x, x // 2 % 2)
                    if 4 <= x < EA + 4:
                        e = x - 4
                        act.wait_ge(pv_done, at(act, n * (GROUPS + EA) + GROUPS + e + 1))
                        nc.scalar.copy(cm[:, e % 2, :], (CT, HB)[e % 2][:, 0:PAIR]).then_inc(cts_ready, 1)
                    if more and x in (6, 7):
                        early_features(n + 1, x - 6)
                if more:
                    take_queries(n + 1)
                    take_latent(n + 1)
                features(n, 1, x2T, 2)
                if more:
                    take_keys(n + 1)
                top_exp_step(n, 1)

            early_features(0, 0)
            early_features(0, 1)
            take_queries(0)
            take_latent(0)
            take_keys(0)
            latent_attention(0, None)
            mixture_of_attention(0, True)
            with act.Fori(0, pairs - 2) as n:
                latent_attention(n + 1, n)
                mixture_of_attention(n + 1, True)
            latent_attention(pairs - 1, pairs - 2)
            mixture_of_attention(pairs - 1, False)
            gate_rows(pairs - 1)
            for e in range(EF):
                relu(pairs - 1, e)

        @block.vector
        def _(dve):
            count = [0]

            def link(i):
                count[0] += 1
                return i.then_inc(dve_step, 1)

            def linked():
                dve.wait_ge(dve_step, count[0])

            def restart():
                linked()
                dve.sem_clear(dve_step)
                count[0] = 0

            dve.wait_ge(w_in, WLOADS)
            nc.vector.tensor_tensor(clsr[:], clsr[:], clsp[:], ALU.add).then_inc(cls_sum, 1)
            link(nc.vector.tensor_tensor(peb[:], peb[:], spread(tln2b[0:PR, :], GRID), ALU.add))
            link(nc.vector.tensor_tensor(wk_v[:, 0], wk_v[:, 0], wk_v[:, 1], ALU.add))
            link(nc.vector.tensor_copy(pick[:], pick_f[:]))
            link(nc.vector.tensor_scalar(qbs[:], qb[:], SCALE_Q, None, ALU.mult))
            link(nc.vector.tensor_scalar(vbm[:, 0, :], vb[0:2 * REM, :], maskc[:, 0:1], None, ALU.mult))
            nc.vector.tensor_scalar(vbm[:, 1, :], vb[0:2 * REM, :], maskc[:, 1:2], None, ALU.mult).then_inc(setup_dve, 1)
            dve.wait_ge(setup_pe, 1)
            for k in range(HALF):
                link(nc.vector.tensor_copy(wkvT[:, k, :], S_BANKS[k][:, 0:D]))
            nc.vector.tensor_copy(relT[:, 0:128], PT[:, 0:128]).then_inc(setup_dve, 1)
            dve.wait_ge(setup_pe, 2)
            nc.vector.tensor_copy(wlat[:, :, :], CT[:, 0:HALF * LAT].rearrange("p (k l) -> p k l", k=HALF)).then_inc(setup_dve, 1)

            xw = xin[:, :, :].rearrange("r q (g w) -> r g q w", g=GRID)
            for step in range(patch_steps):
                dve.wait_ge(x_in, 16 * CH * (step + 1))
                for w in range(GRID):
                    for half in range(2):
                        link(nc.vector.bn_stats(pst[:, w, half, :], xw[:, w, 24 * half:24 * half + 24, :]))
                linked()
                for w in range(GRID):
                    link(nc.vector.bn_aggr(pmv[:, w, :], pst[:, w, :, :].rearrange("r h s -> r (h s)")))
                linked()
                nc.vector.tensor_scalar(pve[:, :], pmv[:, :, 1], EPS, None, ALU.add).then_inc(pvar, 1)
                dve.wait_ge(prstd, 2 * step + 1)

                def normalize(w):
                    u = step * GRID + w
                    if u >= 2:
                        dve.wait_ge(ptran, 2 * (u - 1))
                    i = nc.vector.tensor_scalar(xpn[:, u % 2, :].rearrange("r (q w) -> r q w", w=PATCH), xw[:, w],
                                                pmv[:, w, 0:1], prs[:, w:w + 1], ALU.subtract, ALU.mult)
                    i.then_inc(pnorm, 1)

                normalize(0)
                normalize(1)
                if step:
                    dve.wait_ge(pst_out, 16 * step)
                for w in range(GRID):
                    u = step * GRID + w
                    dve.wait_ge(pmm, u + 1)
                    nc.vector.tensor_tensor(ytok[:, w, :], (CT, PT)[u % 2][0:PR, 0:D], tbias[0:PR, :], ALU.add).then_inc(padd, 1)
                    dve.wait_ge(padd, u + 1)
                    link(nc.vector.bn_stats(pst[:, w, 0, :], ytok[:, w, :]))
                    if w + 2 < GRID:
                        normalize(w + 2)
                dve.wait_ge(pnorm, (step + 1) * GRID)
                linked()
                for w in range(GRID):
                    link(nc.vector.bn_aggr(pmv[:, w, :], pst[:, w, 0, :]))
                linked()
                nc.vector.tensor_scalar(pve[:, :], pmv[:, :, 1], EPS, None, ALU.add).then_inc(pvar, 1)
                dve.wait_ge(prstd, 2 * step + 2)
                for w in range(GRID):
                    link(nc.vector.tensor_scalar(ytok[:, w, :], ytok[:, w, :], pmv[:, w, 0:1], prs[:, w:w + 1], ALU.subtract, ALU.mult))
                linked()
                link(nc.vector.tensor_tensor(ytok[:], ytok[:], spread(ln2g[0:PR, :], GRID), ALU.mult))
                linked()
                nc.vector.tensor_tensor(ytok[:], ytok[:], peb[:], ALU.add).then_inc(ptok, 1)

            def variance(x, var):
                for j in range(3):
                    link(nc.vector.bn_stats(st[:, j, :], x[:, j, :]))
                linked()
                for j in range(3):
                    link(nc.vector.bn_aggr(mv[:, j, :], st[:, j, :]))
                linked()
                nc.vector.tensor_scalar(ve[:, :], mv[:, :, 1], EPS, None, ALU.add).then_inc(var, 1)

            def normalized(rstd, k, x, dst, done):
                dve.wait_ge(rstd, at(dve, k))
                for j in range(3):
                    last = nc.vector.tensor_scalar(dst[:, j, :], x[:, j, :], mv[:, j, 0:1], rs[:, j:j + 1], ALU.subtract, ALU.mult)
                    if j < 2 or done is None:
                        link(last)
                if done is not None:
                    last.then_inc(done, 1)

            def two_largest(rows, experts):
                for s in range(3):
                    link(nc.vector.max(gtop[0:rows, s, :], glog[0:rows, s, 0:experts]))
                linked()
                for s in range(3):
                    link(nc.vector.max_index(gidx[0:rows, s, :], gtop[0:rows, s, :], glog[0:rows, s, 0:experts]))
                nc.vector.tensor_tensor(gd[0:rows, :], gtop[0:rows, :, 1], gtop[0:rows, :, 0], ALU.subtract).then_inc(top_diff, 1)
                linked()
                link(nc.vector.tensor_copy(gidf[0:rows], gidx[0:rows, :, 0:2]))

            def gates_of(n, k, rows, experts, dst):
                dve.wait_ge(top_exp, at(dve, n * 2 + k + 1))
                link(nc.vector.tensor_scalar(gs[0:rows], ge[0:rows], 1.0, None, ALU.add))
                linked()
                link(nc.vector.reciprocal(g1[0:rows], gs[0:rows]))
                linked()
                link(nc.vector.tensor_tensor(g2[0:rows], ge[0:rows], g1[0:rows], ALU.mult))
                linked()
                for s in range(3):
                    link(nc.vector.tensor_scalar(ga[0:rows, s, 0:experts], iota[0:rows, 0:experts], gidf[0:rows, s, 0:1], g1[0:rows, s:s + 1], ALU.is_equal, ALU.mult))
                    link(nc.vector.tensor_scalar(gb[0:rows, s, 0:experts], iota[0:rows, 0:experts], gidf[0:rows, s, 1:2], g2[0:rows, s:s + 1], ALU.is_equal, ALU.mult))
                linked()
                return nc.vector.tensor_tensor(dst[0:rows], ga[0:rows, :, 0:experts], gb[0:rows, :, 0:experts], ALU.add)

            def scores(n, u):
                if u < 2:
                    dve.wait_ge(sc_done, at(dve, n * UNITS + u + 1))
                    if not (isinstance(n, int) and n == 0):
                        dve.wait_ge(prob_ready, at(dve, n * UNITS + u - 1))
                else:
                    wait_all(dve, (sc_done, n * UNITS + u + 1), (prob_ready, n * UNITS + u - 1))
                s = S_BANKS[u % 2][:, 0:3 * SEQ].rearrange("p (s k) -> p s k", s=3)
                if u < HEADS:
                    i = nc.vector.tensor_tensor(sc[:, u % 2], s, decay[:], ALU.mult)
                else:
                    e = u - HEADS
                    dve.wait_ge(bias_in[e], at(dve, n * 64 + 64))
                    i = nc.vector.tensor_tensor(sc[:, u % 2], s, bias[:, e], ALU.add)
                i.then_inc(sc_taken, 1)
                dve.wait_ge(sc_taken, at(dve, n * UNITS + u + 1))
                nc.vector.tensor_reduce(nmax[:, u % 2, :], sc[:, u % 2], AX.X, ALU.max, negate=True).then_inc(max_ready, 1)

            def feed_forward_gates(m):
                link(gates_of(m, 1, TT, EF, gates_f))
                linked()

            def gate_parts():
                link(nc.vector.tensor_copy(gpb[:, :, 0, :], gates_f[:]))
                linked()
                link(nc.vector.tensor_tensor(grest[:], gates_f[:], gpb[:, :, 0, :], ALU.subtract))
                linked()
                link(nc.vector.tensor_copy(gpb[:, :, 1, :], grest[:]))
                linked()
                link(nc.vector.tensor_tensor(gparts[:, :, 2, :], grest[:], gpb[:, :, 1, :], ALU.subtract))
                nc.vector.tensor_copy(gparts[:, :, 0:2, :].rearrange("p s a e -> p s (a e)"), gpb[:, :, 0:2, :].rearrange("p s a e -> p s (a e)")).then_inc(fgates_ready, 1)

            def gate_hidden(m, e):
                if e >= 2:
                    wait_all(dve, (relu_ready, m * EF + e + 1), (down_done, m * EF + e - 1))
                else:
                    dve.wait_ge(relu_ready, at(dve, m * EF + e + 1))
                nc.vector.tensor_tensor(hg[:, e % 2, :], GB[:, 0:PAIR], hr[:, :], ALU.mult).then_inc(gated_ready, 1)

            def finish(m):
                dve.wait_ge(down_done, at(dve, m * EF + EF))
                link(nc.vector.tensor_tensor(resid[:, 0:2, :], ACC[0][0:TT, :].rearrange("p (c d) -> p c d", c=2), resid[:, 0:2, :], ALU.add))
                nc.vector.tensor_tensor(resid[:, 2, :], ACC[1][0:TT, 0:D], resid[:, 2, :], ALU.add).then_inc(y_ready, 1)

            def remainder_values(p):
                dve.wait_ge(proj_done, at(dve, p * PROJ + 11))
                link(nc.vector.tensor_tensor(v_rem[:, 0, :, 0:HD], CT[0:2 * REM, 0:D].rearrange("p (h d) -> p h d", d=HD), maskr[:], ALU.mult))
                nc.vector.tensor_tensor(v_rem[:, 1, :, 0:HD], CT[0:2 * REM, D:2 * D].rearrange("p (h d) -> p h d", d=HD), maskr[:], ALU.mult).then_inc(proj_dve, 1)

            def latent_attention(n, m):
                e = 0
                for h in range(HEAD_STEPS):
                    if h >= 4 and h % 4 == 0 and h <= HEADS:
                        g = h // 4 - 1
                        dve.wait_ge(prob_ready, at(dve, n * UNITS + h))
                        nc.vector.reciprocal(rsum[:, :, 4 * g:4 * g + 4], sums[:, :, 4 * g:4 * g + 4]).then_inc(rsum_ready, 1)
                    if h < HEADS:
                        scores(n, h)
                    if m is not None and h == 0:
                        feed_forward_gates(m)
                    if m is not None and h == 1:
                        gate_parts()
                    if h == 1:
                        remainder_values(n)
                    if h >= 7 and h % 4 == 3:
                        g = (h - 7) // 4
                        wait_all(dve, (rb_done, n * GROUPS + g + 1), (cts_ready, n * (GROUPS + EA) + g + 1))
                        rb = bass.AP(CT[:, :].tensor, 0, [list(CT[:, :].ap[0]), [IMG1, 2], [1, SEQ]])
                        nc.vector.tensor_tensor(ctn[:, g, :].rearrange("p (a q) -> p a q", a=2), rb,
                                                cts[:, :].rearrange("p (a q) -> p a q", a=2), ALU.mult).then_inc(ctn_ready, 1)
                    if m is not None and h in EXPERT_STEPS:
                        gate_hidden(m, e)
                        e += 1

            def mixture_of_attention(n, m, more):
                e = len(EXPERT_STEPS)
                if m is not None:
                    gate_hidden(m, e)
                    e += 1
                dve.wait_ge(oproj_done, at(dve, n * 1 + 1))
                link(nc.vector.tensor_tensor(h1[:, 0:2, :], S_BANKS[0][0:TT, :].rearrange("p (c d) -> p c d", c=2), h_in[:, 0:2, :], ALU.add))
                nc.vector.tensor_tensor(h1[:, 2, :], S_BANKS[1][0:TT, 0:D], h_in[:, 2, :], ALU.add).then_inc(h_free, 1)
                dve.wait_ge(h_free, at(dve, n * 1 + 1))
                variance(h1, var_ready)
                if m is not None:
                    gate_hidden(m, e)
                    e += 1
                normalized(rstd_ready, n * 3 + 1, h1, src, None)
                linked()
                variance(src, var_ready)
                if m is not None:
                    gate_hidden(m, e)
                    e += 1
                normalized(rstd_ready, n * 3 + 2, src, xn, xn_ready)
                if m is not None:
                    while e < EF:
                        gate_hidden(m, e)
                        e += 1
                    finish(m)
                dve.wait_ge(mk_done, at(dve, n * 4 + 2))
                nc.vector.tensor_copy(glog[:, :, 0:EA], PT[:, 0:3 * EA].rearrange("p (s e) -> p s e", s=3)).then_inc(mk_dve, 1)
                dve.wait_ge(mk_dve, at(dve, n * 3 + 1))
                dve.sem_inc(vector_turn, 1)
                two_largest(128, EA)
                gates_of(n, 0, 128, EA, gates_a).then_inc(gates_ready, 1)
                def clipped(x):
                    dve.wait_ge(rel_mid, at(dve, n * EA + x + 1))
                    rows = spans_of[x % 4]
                    link(nc.vector.tensor_copy(rows[:, :, 0:SIDE], columns(rows[:, :, SIDE], SIDE)))
                    nc.vector.tensor_copy(rows[:, :, SIDE + REL:SPAN], columns(rows[:, :, SIDE + REL - 1], SIDE)).then_inc(rel_ready, 1)

                def weigh(e):
                    dve.wait_ge(prob_ready, at(dve, n * UNITS + HEADS + e + 1))
                    link(nc.vector.reciprocal(mrs[:, e, :], msum[:, e, :]))
                    linked()
                    link(nc.vector.tensor_tensor(mw[:, e, :], mrs[:, e, :], gates_a[:, :, e], ALU.mult))
                    linked()
                    for s in range(3):
                        p = prob[:, e // 2 % 2, s, e % 2 * SEQ:(e % 2 + 1) * SEQ]
                        last = nc.vector.tensor_scalar(p, p, mw[:, e, s:s + 1], None, ALU.mult)
                        if s < 2:
                            link(last)
                    last.then_inc(mw_ready, 1)

                for x in range(EA - 1):
                    clipped(x)
                    if x == 4:
                        dve.wait_ge(gates_tran, at(dve, n * 1 + 1))
                        nc.vector.tensor_copy(gatesT_a[:, :].rearrange("e (a q) -> e a q", a=2),
                                              bass.AP(ACC[1][:, :].tensor, 0, [[ACC[1][:, :].ap[0][0], EA], [IMG1, 2], [1, SEQ]])).then_inc(gatesT_ready, 1)
                    if x >= FIRST_SCORES - 1:
                        scores(n, HEADS + x - FIRST_SCORES + 1)
                weigh(0)
                clipped(EA - 1)
                for x in range(2, EA + 1):
                    if x < EA:
                        scores(n, HEADS + x)
                    if x == 3:
                        dve.wait_ge(mk_done, at(dve, n * 4 + 4))
                        for par in range(2):
                            for a in range(2):
                                last = nc.vector.scalar_tensor_tensor(out=vmr[:, par, a, :], in0=HB[0:2 * REM, a * 128:(a + 1) * 128],
                                                                      scalar=maskc[:, par:par + 1], in1=vbm[:, par, :],
                                                                      op0=ALU.mult, op1=ALU.add)
                                if par + a < 2:
                                    link(last)
                        last.then_inc(mk_dve, 1)
                    weigh(x - 1)
                    if x == 2:
                        dve.wait_ge(mk_done, at(dve, n * 4 + 3))
                        nc.vector.tensor_tensor(vm[:, :, :, :].rearrange("p b a d -> p (b a) d"), GB[:, :].rearrange("p (c d) -> p c d", c=4), spread(vb[:, :], 4), ALU.add).then_inc(mk_dve, 1)
                    if more and x == 4:
                        dve.wait_ge(h_loaded, at(dve, n * LOADS + 2 * LOADS))
                        variance(h_in, avar_ready)
                    if more and x == 5:
                        normalized(arstd_ready, n + 2, h_in, xn, axn_ready)
                dve.wait_ge(moa_done, at(dve, n * 1 + 1))
                link(nc.vector.tensor_tensor(x2[:, 0:2, :], ACC[0][0:TT, :].rearrange("p (c d) -> p c d", c=2), src[:, 0:2, :], ALU.add))
                link(nc.vector.tensor_tensor(x2[:, 2, :], ACC[1][0:TT, 0:D], src[:, 2, :], ALU.add))
                linked()
                variance(x2, var_ready)
                if m is not None:
                    dve.wait_ge(stored, at(dve, m * 16 + 16))
                link(nc.vector.tensor_tensor(resid[:], x2[:], h1[:], ALU.add))
                normalized(rstd_ready, n * 3 + 3, x2, xn, xn_ready)
                dve.wait_ge(fg_done, at(dve, n * 1 + 1))
                link(nc.vector.tensor_copy(glog[0:TT], GB[0:TT, 0:3 * EF].rearrange("p (s e) -> p s e", s=3)))
                linked()
                two_largest(TT, EF)

            dve.wait_ge(h_loaded, LOADS)
            variance(h_in, avar_ready)
            normalized(arstd_ready, 1, h_in, xn, axn_ready)
            latent_attention(0, None)
            mixture_of_attention(0, None, True)
            restart()
            with dve.Fori(0, pairs - 2) as n:
                latent_attention(n + 1, n)
                mixture_of_attention(n + 1, n, True)
                restart()
            latent_attention(pairs - 1, pairs - 2)
            mixture_of_attention(pairs - 1, pairs - 2, False)
            feed_forward_gates(pairs - 1)
            gate_parts()
            for e in range(EF):
                gate_hidden(pairs - 1, e)
            finish(pairs - 1)

        @block.tensor
        def _(pe):
            mm = nc.tensor.matmul
            I = ident

            pe.wait_ge(setup_dve, 1)
            for c in range(HALF):
                for k in range(HALF):
                    nc.tensor.transpose(S_BANKS[c][:, k * 128:(k + 1) * 128], wk_v[:, 0, k, c * 128:(c + 1) * 128], I[:])
            nc.tensor.transpose(PT[:, 0:128], reltab[:], I[:]).then_inc(setup_pe, 1)
            pe.wait_ge(setup_dve, 2)
            for k in range(HALF):
                for c in range(HALF):
                    last = mm(CT[:, k * LAT:(k + 1) * LAT], wkvT[:, c, k * 128:(k + 1) * 128], wdown[:, c, :], start=c == 0, stop=c == HALF - 1)
            last.then_inc(setup_pe, 1)
            pe.wait_ge(setup_dve, 3)
            pe.wait_ge(wpad_in, 16 * (HALF + 1 + 4))

            columns_ = patch_steps * GRID

            def embed(u):
                pe.wait_ge(pfeat, 2 * u + 2)
                if u >= 2:
                    pe.wait_ge(padd, u - 1)
                for k in range(PC):
                    last = mm((CT, PT)[u % 2][0:PR, 0:D], xpT[:, u % 2, k, :], wt[:, k, :], start=k == 0, stop=k == PC - 1)
                last.then_inc(pmm, 1)

            for u in range(columns_):
                if u and u % GRID == 0:
                    embed(u - 1)
                pe.wait_ge(pnorm, u + 1)
                for half in range(2):
                    if u:
                        pe.wait_ge(pfeat, 2 * (u - 1) + half + 1)
                    for c in range(3):
                        k = 3 * half + c
                        last = nc.tensor.transpose(S_BANKS[half][:, c * PR:(c + 1) * PR], xpn[:, u % 2, k * 128:(k + 1) * 128], I[0:PR, 0:PR])
                    last.then_inc(ptran, 1)
                if u % GRID:
                    embed(u - 1)
            embed(columns_ - 1)

            def transposes(n, k):
                pe.wait_ge(xn_ready, at(pe, n * XN + k + 1))
                for c in range(HALF):
                    for j in range(3):
                        last = nc.tensor.transpose(S_BANKS[c][:, j * TT:(j + 1) * TT], xn[:, j, c * 128:(c + 1) * 128], I[0:TT, 0:TT])
                    last.then_inc(xn_tran, 1)

            def early_transposes(p, c):
                pe.wait_ge(axn_ready, at(pe, p + 1)) if c == 0 else pe.wait_ge(afeat_ready, at(pe, p * 2 + 1))
                for j in range(3):
                    last = nc.tensor.transpose(GB[:, j * TT:(j + 1) * TT], xn[:, j, c * 128:(c + 1) * 128], I[0:TT, 0:TT])
                last.then_inc(axn_tran, 1)

            def gate_logits(n, j):
                if j == 0:
                    pe.wait_ge(feat_ready, at(pe, n * FEAT + 4))
                for k in range(HALF):
                    last = mm(GB[0:TT, j * EF:(j + 1) * EF], x2T[:, k, j * TT:(j + 1) * TT], fgatew[:, k, :], start=k == 0, stop=k == 1)
                if j == 2:
                    last.then_inc(fg_done, 1)

            def project(n, part, logits_of=None):
                def taken(k):
                    pe.wait_ge(proj_act, at(pe, n * PACT + k))

                if part == 0:
                  pe.wait_ge(afeat_ready, at(pe, n * 2 + 2))
                  for g in range(GROUPS):
                    if g >= 2:
                        taken(g - 1)
                    for k in range(HALF):
                        last = mm((CT, PT)[g % 2][:, 0:PAIR], wq[:, k, 4 * g:4 * g + 4, :].rearrange("p h d -> p (h d)"), xaT[:, k, :], start=k == 0, stop=k == 1)
                    last.then_inc(proj_done, 1)
                if part == 1:
                  taken(3)
                  for k in range(HALF):
                    last = mm(CT[0:LAT, 0:PAIR], wlat[:, k, :], xaT[:, k, :], start=k == 0, stop=k == 1)
                  last.then_inc(proj_done, 1)
                if part == 2:
                    taken(6)
                    for g in range(GROUPS):
                        if g >= 2:
                            taken(5 + g)
                        mm((PT, CT)[g % 2][:, 0:PAIR], wupk[:, 4 * g:4 * g + 4, :].rearrange("p h d -> p (h d)"), latT[:, :], start=True, stop=True).then_inc(proj_done, 1)
                        if g >= 1 and logits_of is not None:
                            gate_logits(logits_of, g - 1)

            def latent_values(n, part):
                if part == 0:
                    pe.wait_ge(proj_act, at(pe, n * PACT + 9))
                    halves = wupv[:, :].rearrange("l (h b d) -> l b h d", b=2, d=HD)
                    places = PT[:, :].rearrange("p (a h b d) -> p a b h d", a=2, b=2, d=HD)
                    for a in range(2):
                        for b in range(2):
                            k0 = a * SEQ + b * REM
                            last = mm(places[:, a, b], latT[:, k0:k0 + 128], halves[:, b], start=True, stop=True, skip_group_check=True)
                else:
                    pe.wait_ge(proj_act, at(pe, n * PACT + 10))
                    for a in range(2):
                        last = mm(CT[0:2 * REM, a * D:(a + 1) * D], latR[:, a, :], wupv[:, :], start=True, stop=True)
                last.then_inc(proj_done, 1)

            def head_scores(n, h):
                g, j = divmod(h, 4)
                if h == 0:
                    pe.wait_ge(proj_act, at(pe, n * PACT + 10))
                if h >= 2:
                    pe.wait_ge(sc_taken, at(pe, n * UNITS + h - 1))
                for s, row, col, rows, a in SLOTS:
                    last = mm(S_BANKS[h % 2][row:row + rows, s * SEQ:(s + 1) * SEQ], qT[32 * j:32 * j + HD, g, col:col + rows],
                              kT[32 * j:32 * j + HD, g, a * SEQ:(a + 1) * SEQ], start=True, stop=True, tile_position=(32 * j, row))
                last.then_inc(sc_done, 1)

            def tran_main(n, u):
                p, h = divmod(u, 2)
                k = n * (3 * UNITS // 2) + 3 * p + h
                ready = prob_ready if u < HEADS else mw_ready
                value = n * UNITS + u + 1 if u < HEADS else n * EA + (u - HEADS) + 1
                if u == 0:
                    wait_all(pe, (ready, value), (proj_act, n * PACT + 11))
                else:
                    wait_all(pe, (ready, value), (pt_taken, k))
                for s in range(3):
                    last = nc.tensor.transpose(PT[:, s * 128:(s + 1) * 128], prob[:, p % 2, s, (SEQ + REM) * h:(SEQ + REM) * h + 128], I[:])
                last.then_inc(pt_done, 1)

            def tran_rem(n, p):
                pe.wait_ge(pt_taken, at(pe, n * (3 * UNITS // 2) + 3 * p + 2))
                for s in range(3):
                    last = nc.tensor.transpose(PT[0:2 * REM, s * 128:(s + 1) * 128], prob[:, p % 2, s, 128:128 + 2 * REM], I[:])
                last.then_inc(pt_done, 1)

            def group_values(n, g):
                value = n * (3 * UNITS // 2) + 6 * g + 6
                if g:
                    wait_all(pe, (pt_taken, value), (ctn_ready, n * GROUPS + g))
                else:
                    wait_all(pe, (pt_taken, value), (proj_dve, n + 1))
                for a in range(2):
                    q0 = a * IMG1
                    for j in range(4):
                        mm(CT[32 * j:32 * j + 32, a * SEQ:(a + 1) * SEQ], v_main[:, a, 4 * g + j, :], ptm[:, j, q0:q0 + SEQ],
                           start=True, stop=False, tile_position=(0, 32 * j))
                    for j in range(4):
                        last = mm(CT[32 * j:32 * j + 32, a * SEQ:(a + 1) * SEQ], v_rem[:, a, 4 * g + j, :], ptr[:, j // 2, q0:q0 + SEQ],
                                  start=False, stop=True, tile_position=(0, 32 * j))
                last.then_inc(pv_done, 1)

            def group_divisors(n, g):
                wait_all(pe, (rsx_ready, n * GROUPS + g + 1), (cts_ready, n * (GROUPS + EA) + g + 1))
                for s in range(3):
                    last = mm(CT[:, s * 128:(s + 1) * 128], rsx[:, s, :], I[:], start=True, stop=True)
                last.then_inc(rb_done, 1)

            def out_project(n):
                pe.wait_ge(ctn_ready, at(pe, n * GROUPS + GROUPS))
                pe.wait_ge(sc_taken, at(pe, n * UNITS + HEADS))
                for j in range(3):
                    for g in range(GROUPS):
                        last = mm(S_BANKS[j // 2][0:TT, (j % 2) * D:(j % 2 + 1) * D], ctn[:, g, j * TT:(j + 1) * TT], wo[:, g, :],
                                  start=g == 0, stop=g == GROUPS - 1)
                last.then_inc(oproj_done, 1)

            def expert_up(m, e):
                if e == 0:
                    wait_all(pe, (fgT_ready, m * 2 + 2))
                else:
                    wait_all(pe, (relu_ready, m * EF + e))
                for k in range(HALF):
                    mm(HB[:, 0:PAIR], w1[:, e, k, :], x2T[:, k, :], start=k == 0, stop=k == 1)
                if e:
                    wait_all(pe, (gated_ready, m * EF + e))
                mm(GB[:, 0:PAIR], pick[:, e, :], partsT[:, :], start=True, stop=True).then_inc(up_done, 1)

            def gate_rows(m):
                pe.wait_ge(fgates_ready, at(pe, m + 1))
                for j in range(3):
                    last = nc.tensor.transpose(HB[0:EF, j * TT:(j + 1) * TT], gates_f[:, j, :], I[0:TT, 0:TT])
                last.then_inc(fg_tran, 1)
                for j in range(3):
                    last = nc.tensor.transpose(GB[0:3 * EF, j * TT:(j + 1) * TT], gparts[:, j, :, :].rearrange("p a e -> p (a e)"), I[0:TT, 0:TT])
                last.then_inc(fg_tran, 1)

            def into_tiles(first, last_, lhs, rhs, seq_start):
                for j in range(3):
                    i = mm(ACC[j // 2][0:TT, (j % 2) * D:(j % 2 + 1) * D], lhs(j), rhs,
                           start=seq_start and j != 1, stop=last_, skip_group_check=True)
                return i

            def expert_down(m, e):
                if e == 0:
                    into_tiles(True, False, lambda j: gatesT_f[:, j * TT:(j + 1) * TT], b2[:, :], True)
                pe.wait_ge(gated_ready, at(pe, m * EF + e + 1))
                into_tiles(False, e == EF - 1, lambda j: hg[:, e % 2, j * TT:(j + 1) * TT], w2[:, e, :], False).then_inc(down_done, 1)

            def latent_attention(n, m):
                e = 0
                for h in range(HEAD_STEPS):
                    if m is not None and h in EXPERT_STEPS and h >= HEADS:
                        expert_up(m, e)
                        if e:
                            expert_down(m, e - 1)
                        e += 1
                    if h % 2 == 0 and h >= 4:
                        tran_rem(n, (h - 4) // 2)
                    if h == 0:
                        latent_values(n, 0)
                    if h < HEADS:
                        head_scores(n, h)
                    if h == 1:
                        latent_values(n, 1)
                    if h >= 7 and h % 4 == 3:
                        group_divisors(n, (h - 7) // 4)
                    if h >= 6 and h % 4 == 2:
                        group_values(n, (h - 6) // 4)
                    if 2 <= h < HEADS + 2:
                        tran_main(n, h - 2)
                    if h == GATE_STEP and m is not None:
                        gate_rows(m)
                    if m is not None and h in EXPERT_STEPS and h < HEADS:
                        expert_up(m, e)
                        if e:
                            expert_down(m, e - 1)
                        e += 1
                if m is not None:
                    expert_up(m, e)
                    expert_down(m, e - 1)
                out_project(n)
                if m is not None:
                    for e in range(len(EXPERT_STEPS) + 1, EF):
                        expert_up(m, e)
                        expert_down(m, e - 1)

            def expert_scores(n, x):
                for s, row, col, rows, a in SLOTS:
                    last = mm(S_BANKS[x % 2][row:row + rows, s * SEQ:(s + 1) * SEQ], qm[:, x, col:col + rows], kmT[:, a * SEQ:(a + 1) * SEQ],
                              start=True, stop=True, tile_position=(0, row))
                last.then_inc(sc_done, 1)

            def values(n):
                for b in range(2):
                    for a in range(2):
                        k0 = a * SEQ + b * REM
                        for k in range(HALF):
                            last = mm(GB[:, (2 * b + a) * 128:(2 * b + a + 1) * 128], x1T[:, k, k0:k0 + 128], vw[:, k, :], start=k == 0, stop=k == 1)
                last.then_inc(mk_done, 1)
                pe.wait_ge(x1r_ready, at(pe, n * HALF + 2))
                for a in range(2):
                    for k in range(HALF):
                        last = mm(HB[0:2 * REM, a * 128:(a + 1) * 128], x1R[:, k, a, :], vw[:, k, :], start=k == 0, stop=k == 1)
                last.then_inc(mk_done, 1)

            def mixture_of_attention(n, m, more):
                pe.wait_ge(h_free, at(pe, n * 1 + 1))
                transposes(n, 0)
                if m is not None:
                    expert_down(m, EF - 1)
                pe.wait_ge(feat_ready, at(pe, n * FEAT + 2))
                for k in range(HALF):
                    last = mm(HB[:, 0:PAIR], kw[:, k, :], x1T[:, k, :], start=k == 0, stop=k == 1)
                last.then_inc(mk_done, 1)
                for s, row, col, rows, a in SLOTS:
                    for k in range(HALF):
                        last = mm(PT[row:row + rows, s * EA:(s + 1) * EA], x1T[:, k, col:col + rows], gatew[:, k, :], start=k == 0, stop=k == 1, tile_position=(0, row))
                last.then_inc(mk_done, 1)
                for e in range(EA + 1):
                    if e < EA:
                        if e == 0:
                            pe.wait_ge(mk_act, at(pe, n * 1 + 1))
                        elif e >= 2:
                            pe.wait_ge(q_ready, at(pe, n * EA + e - 1))
                        for k in range(HALF):
                            last = mm((HB, GB)[e % 2][:, 0:PAIR], qw[:, e, k, :], x1T[:, k, :], start=k == 0, stop=k == 1)
                        last.then_inc(q_done, 1)
                    if e >= 1:
                        x = e - 1
                        if x >= 2:
                            wait_all(pe, (q_ready, n * EA + x + 1), (rel_mid, n * EA + x - 1))
                        elif x == 1:
                            wait_all(pe, (q_ready, n * EA + x + 1), (mk_dve, n * 3 + 1))
                        else:
                            pe.wait_ge(q_ready, at(pe, n * EA + x + 1))
                        for s, row, col, rows, a in SLOTS:
                            last = mm((CT, PT)[x % 2][row:row + rows, s * REL:(s + 1) * REL], qm[:, x, col:col + rows], relT[:, :],
                                      start=True, stop=True, tile_position=(0, row))
                        last.then_inc(rel_done, 1)
                    if e == 4:
                        if m is not None:
                            wait_all(pe, (gates_ready, n + 1), (y_ready, m + 1))
                        else:
                            pe.wait_ge(gates_ready, at(pe, n + 1))
                        for s in range(3):
                            last = nc.tensor.transpose(ACC[1][0:EA, s * 128:(s + 1) * 128], gates_a[:, s, :], I[:])
                        last.then_inc(gates_tran, 1)
                    if e in (FIRST_SCORES, FIRST_SCORES + 1):
                        expert_scores(n, e - FIRST_SCORES)
                pe.wait_ge(sc_taken, at(pe, n * UNITS + HEADS + 1))
                expert_scores(n, 2)
                values(n)
                pe.wait_ge(sc_taken, at(pe, n * UNITS + HEADS + 2))
                expert_scores(n, 3)
                pe.wait_ge(rel_mid, at(pe, n * EA + EA))
                for x in range(2, EA + 5):
                    if 4 <= x < EA:
                        pe.wait_ge(sc_taken, at(pe, n * UNITS + HEADS + x - 1))
                        expert_scores(n, x)
                    if x == 3:
                        pe.wait_ge(gatesT_ready, at(pe, n + 1))
                        into_tiles(True, False, lambda j: gatesT_a[:, j * TT:(j + 1) * TT], ob[:, :], True)
                    if x % 2 == 0 and 4 <= x < EA + 4:
                        tran_rem(n, (HEADS + x - 4) // 2)
                    if 2 <= x < EA + 2:
                        tran_main(n, HEADS + x - 2)
                    base = n * (GROUPS + EA) + GROUPS
                    if 4 <= x < EA + 4:
                        e = x - 4
                        p = (HEADS + e) // 2
                        if e >= 2:
                            wait_all(pe, (pt_taken, n * (3 * UNITS // 2) + 3 * p + 3), (cts_ready, base + e - 1))
                        else:
                            wait_all(pe, (pt_taken, n * (3 * UNITS // 2) + 3 * p + 3), (mk_dve, n * 3 + 3))
                        for a in range(2):
                            q0 = a * IMG1
                            bank = (CT, HB)[e % 2]
                            mm(bank[:, a * SEQ:(a + 1) * SEQ], vm[:, e % 2, a, :], ptm[:, e % 4, q0:q0 + SEQ], start=True, stop=False)
                            last = mm(bank[:, a * SEQ:(a + 1) * SEQ], vmr[:, e % 2, a, :], ptr[:, p % 2, q0:q0 + SEQ], start=False, stop=True)
                        last.then_inc(pv_done, 1)
                    if more and x in (6, 7):
                        early_transposes(n + 1, x - 6)
                    if x >= 5:
                        e = x - 5
                        pe.wait_ge(cts_ready, at(pe, base + e + 1))
                        last = into_tiles(False, e == EA - 1, lambda j: cm[:, e % 2, j * TT:(j + 1) * TT], ow[:, e, :], False)
                last.then_inc(moa_done, 1)
                if more:
                    project(n + 1, 0)
                    project(n + 1, 1)
                transposes(n, 1)
                if more:
                    project(n + 1, 2, n)
                else:
                    for j in range(3):
                        gate_logits(n, j)

            early_transposes(0, 0)
            early_transposes(0, 1)
            for part in range(3):
                project(0, part)
            latent_attention(0, None)
            mixture_of_attention(0, None, True)
            with pe.Fori(0, pairs - 2) as n:
                latent_attention(n + 1, n)
                mixture_of_attention(n + 1, n, True)
            latent_attention(pairs - 1, pairs - 2)
            mixture_of_attention(pairs - 1, pairs - 2, False)
            gate_rows(pairs - 1)
            expert_up(pairs - 1, 0)
            for e in range(1, EF):
                expert_up(pairs - 1, e)
                expert_down(pairs - 1, e - 1)
            expert_down(pairs - 1, EF - 1)


LOADS = 16 * 8


def constants():
    import numpy as np
    f = np.float32
    c = {"ident": np.eye(128, dtype=f)}
    y, x = np.meshgrid(np.arange(GRID), np.arange(GRID), indexing="ij")
    omega = np.arange(D // 4, dtype=f) / f(D // 4 - 1)
    omega = (f(1.0) / np.power(f(10000.0), omega)).astype(f)
    y = y.reshape(-1)[:, None].astype(f) * omega[None]
    x = x.reshape(-1)[:, None].astype(f) * omega[None]
    pe = np.concatenate((np.sin(x), np.cos(x), np.sin(y), np.cos(y)), axis=1).astype(f)
    c["pe"] = np.ascontiguousarray(np.tile(pe.reshape(GRID, GRID, D), (16, 1, 1)))
    k = np.arange(SEQ, dtype=f)
    dec = np.ones((128, 3, SEQ), f)
    for s, row, col, rows, a in SLOTS:
        q = np.arange(rows) + col - a * SEQ
        q = np.clip(q, 0, SEQ - 1).astype(f)
        dec[row:row + rows, s] = np.exp(f(-0.01) * np.abs(q[:, None] - k[None])) / f(16.0)
    c["decay"] = dec
    top = (np.arange(2 * REM) < REM)
    even = (np.arange(HEADS) % 2 == 0)
    c["mask_rows"] = np.ascontiguousarray(np.repeat((top[:, None] == even[None])[:, :, None], HD, 2).astype(f))
    c["mask_cols"] = np.stack([top, ~top], 1).astype(f)
    c["iota"] = np.tile(np.arange(EF, dtype=f), (128, 1))
    pick = np.zeros((3, EF, EF, 128), f)
    for e in range(EF):
        pick[:, e, e] = 1
    c["pick"] = pick.reshape(3 * EF, EF, 128)
    return c


def kernel(**inputs):
    import numpy as np
    import concourse.bacc as bacc
    from concourse.bass_utils import run_bass_kernel_spmd

    nc = bacc.Bacc("TRN2", target_bir_lowering=False, num_devices=1)
    arrays, aps = {}, {}
    for name, a in {**inputs, **constants()}.items():
        a = np.ascontiguousarray(a)
        arrays[f"in_{name}"] = a
        aps[name] = nc.dram_tensor(f"in_{name}", a.shape, mybir.dt.from_np(a.dtype), kind="ExternalInput").ap()
    shape = (inputs["x"].shape[0], SEQ, D)
    out = nc.dram_tensor("out", shape, F32, kind="ExternalOutput").ap()
    early_fusion(nc, aps, out)
    r = run_bass_kernel_spmd(nc, [arrays], core_ids=[0])
    return r.results[0]["out"]
```

```python
import concourse.bass as bass
from concourse import mybir
from concourse.alu_op_type import AluOpType as ALU
from contextlib import ExitStack

F32 = mybir.dt.float32
BF16 = mybir.dt.bfloat16
U32 = mybir.dt.uint32
ACT = mybir.ActivationFunctionType
AX = mybir.AxisListType

D = 256
HALF = D // 128
PATCH, CH, GRID = 16, 3, 6
NPATCH = GRID * GRID
TXT = 128
SEQ = 1 + NPATCH + TXT
PAIR = 2 * SEQ
TT = PAIR // 3
PF = CH * PATCH * PATCH
PC = PF // 128
HEADS, HD, GROUPS = 16, 16, 4
PACKS = 2
LAT = 64
EA, EF = 8, 16
MAXP = 64
REL = 2 * MAXP + 1
SIDE = SEQ - 1 - MAXP
REM = SEQ - 128
WIDE = 384
IMG1 = WIDE - SEQ
SPAN = 2 * SEQ - 1
EPS = 1e-5
ARENA = 26200
SLOTS = [(0, 0, 0, 128, 0), (1, 0, 128, 64, 0), (1, 64, 138, 64, 1), (2, 0, 202, 128, 1)]

HEAD_STEPS = HEADS + 4
GATE_STEP = 3
EXPERT_STEPS = (4, 5, 7, 9, 11, 13, 14, 15, 16, 17, 18, 19)
FIRST_SCORES = 6


def spread(ap, n):
    return bass.AP(ap.tensor, ap.offset, [list(ap.ap[0]), [0, n], list(ap.ap[-1])])


def columns(ap, n):
    return bass.AP(ap.tensor, ap.offset, [list(x) for x in ap.ap] + [[0, n]])


def ends_of(ap):
    return bass.AP(ap.tensor, ap.offset + 128, [list(ap.ap[0]), [SEQ, 2], [-128, 2], [1, REM]])


def head_places(v, rows, image, packs, sub):
    full = v[:, :, :, :]
    first = full.offset + image * HEADS * 32 + sub * (4 * 32 + HD)
    return bass.AP(full.tensor, first, [[full.ap[0][0], rows], [8 * 32, packs], [32, 4], [1, HD]])


def at(eng, value):
    return value if isinstance(value, int) else eng.to_reg(value)


def wait_all(eng, *pairs):
    found = [(sem, at(eng, value)) for sem, value in pairs]
    for sem, value in found:
        eng.wait_ge(sem, value)


def early_fusion(nc, t, out):
    images = t["x"].shape[0]
    pairs = images // 2
    PI = min(16, images)
    PR = PI * GRID
    patch_steps = images // PI
    SCALE_Q = 128.0 ** -0.5

    ctx = ExitStack()
    with ctx:
        def sb(name, shape, dt=F32):
            return ctx.enter_context(nc.sbuf_tensor(name, shape, dt))

        arena = sb("arena", [128, ARENA])
        ends = {"early": 0, "late": 0}

        def within(when, shape):
            size = 1
            for x in shape[1:]:
                size *= x
            at = ends[when]
            ends[when] = at + size
            assert ends[when] <= ARENA, ends
            v = arena[0:shape[0], at:at + size]
            names = ["a", "b", "c", "d"][:len(shape) - 1]
            if len(names) == 1:
                return v
            return v.rearrange(f"p ({' '.join(names)}) -> p {' '.join(names)}", **dict(zip(names, shape[1:])))

        def sem(name):
            return ctx.enter_context(nc.semaphore(name))

        banks = [ctx.enter_context(nc.psum_tensor(f"bank{b}", [128, 512], F32)) for b in range(8)]
        S_BANKS = banks[0:2]
        PT, CT, HB, GB = banks[2], banks[3], banks[4], banks[5]
        ACC = banks[6:8]

        tokens_dram = nc.dram_tensor("patch_tokens", [images * NPATCH, D], F32)
        cls_dram = nc.dram_tensor("cls_rows", [2, D], F32)
        span_dram = nc.dram_tensor("rel_span", [EA, 3 * 128, SPAN], F32)

        ident = sb("ident", [128, 128])
        wt = within("early", [128, PC, D])
        ln1g = sb("ln1g", [128, PC])
        ln1b = sb("ln1b", [128, PC])
        tbias = within("early", [128, D])
        ln2g = within("early", [128, D])
        peb = within("early", [PR, GRID, D])
        tln2b = within("early", [128, D])
        wq = sb("wq", [128, HALF, HEADS, 32])
        wk_v = within("early", [128, 2, HALF, D])
        wkvT = within("early", [128, HALF, D])
        wdown = sb("wdown", [128, HALF, LAT])
        wlat = sb("wlat", [128, HALF, LAT])
        wupk = sb("wupk", [LAT, HEADS, 32])
        wupv = sb("wupv", [LAT, D])
        wo = sb("wo", [128, PACKS, D])
        decay = sb("decay", [128, 3, SEQ])
        maskr = sb("maskr", [2 * REM, HEADS, HD])
        maskc = sb("maskc", [2 * REM, 2])
        iota = sb("iota", [128, EF])
        lnw = sb("lnw", [128, 4, HALF])
        gatew = sb("gatew", [128, HALF, EA])
        qw = sb("qw", [128, EA, HALF, 128])
        qb = sb("qb", [128, EA])
        qbs = sb("qbs", [128, EA])
        kw = sb("kw", [128, HALF, 128])
        kb = sb("kb", [128, 1])
        vw = sb("vw", [128, HALF, 128])
        vb = sb("vb", [128, 128])
        vbm = sb("vbm", [2 * REM, 2, 128])
        ow = sb("ow", [128, EA, D])
        ob = sb("ob", [EA, D])
        reltab = within("early", [128, 128])
        relT = sb("relT", [128, REL])
        fgatew = sb("fgatew", [128, HALF, EF])
        w1 = sb("w1", [128, EF, HALF, 128])
        b1 = sb("b1", [128, EF])
        w2 = sb("w2", [128, EF, D])
        b2 = sb("b2", [EF, D])
        pick_f = within("early", [3 * EF, EF, 128])
        pick = sb("pick", [3 * EF, EF, 128], BF16)
        neghalf = sb("neghalf", [128, GRID])
        clsr = within("early", [2, D])
        clsp = within("early", [2, D])

        xin = [within("early", [PR, CH * PATCH, GRID * PATCH]) for _ in range(2)]
        xpn = within("early", [PR, 2, PF])
        xpT = within("early", [128, 2, PC, PR])
        ytok = [within("early", [PR, GRID, D]) for _ in range(2)]
        pst = within("early", [PR, GRID, 2, 6])
        pmv = [within("early", [PR, GRID, 2]) for _ in range(2)]
        pve = within("early", [PR, GRID])
        prs = [within("early", [PR, GRID]) for _ in range(2)]
        tst = within("early", [PR, GRID, 6])
        tmv = within("early", [PR, GRID, 2])
        tve = within("early", [PR, GRID])
        trs = within("early", [PR, GRID])

        h_in = sb("h_in", [TT, 3, D])
        h1 = sb("h1", [TT, 3, D])
        src = sb("src", [TT, 3, D])
        x2 = src
        resid = sb("resid", [TT, 3, D])
        xn = sb("xn", [TT, 3, D])
        st = sb("st", [TT, 3, 6])
        mv = sb("mv", [TT, 3, 2])
        ve = sb("ve", [TT, 3])
        rs = sb("rs", [TT, 3])
        xaT = within("late", [128, HALF, PAIR])
        x1T = within("late", [128, HALF, PAIR])
        x2T = within("late", [128, HALF, PAIR])
        qT = within("late", [128, GROUPS, PAIR])
        kT = within("late", [128, GROUPS, PAIR])
        latT = within("late", [LAT, PAIR])
        latR = within("late", [LAT, 2, 2 * REM])
        x1R = within("late", [128, HALF, 2, 2 * REM])
        rsx = within("late", [128, 3, 128])
        v_main = sb("v_main", [128, 2, HEADS, 32])
        v_rem = sb("v_rem", [2 * REM, 2, HEADS, 32])
        sc = within("late", [128, 2, 3, SEQ])
        nmax = sb("nmax", [128, 2, 3])
        prob = within("late", [128, 2, 3, 2 * SEQ])
        pt_area = within("late", [128, 6 * WIDE])
        ptm = pt_area[:, 0:4 * WIDE].rearrange("p (u q) -> p u q", u=4)
        ptr = pt_area[0:2 * REM, 4 * WIDE:6 * WIDE].rearrange("p (u q) -> p u q", u=2)
        sums = sb("sums", [128, 3, HEADS])
        rsum = sb("rsum", [128, 3, HEADS])
        cts = within("late", [128, PAIR])
        ctn = within("late", [128, PACKS, PAIR])
        kmT = within("late", [128, PAIR])
        vm = within("late", [128, 2, 2, 128])
        vmr = within("late", [2 * REM, 2, 2, 128])
        qm = within("late", [128, EA, PAIR])
        span_own = within("late", [128, 2, 3, SPAN])
        span_lent = pt_area[:, 0:6 * SPAN].rearrange("p (u s w) -> p u s w", u=2, s=3)
        spans_of = [span_lent[:, 0], span_lent[:, 1], span_own[:, 0], span_own[:, 1]]
        bias = within("late", [128, EA, 3, SEQ])
        glog = sb("glog", [128, 3, EF])
        gtop = sb("gtop", [128, 3, 8])
        gidx = sb("gidx", [128, 3, 8], U32)
        gidf = sb("gidf", [128, 3, 2])
        gd = sb("gd", [128, 3])
        ge = sb("ge", [128, 3])
        gs = sb("gs", [128, 3])
        g1 = sb("g1", [128, 3])
        g2 = sb("g2", [128, 3])
        ga = sb("ga", [128, 3, EF])
        gb = sb("gb", [128, 3, EF])
        gates_a = sb("gates_a", [128, 3, EA])
        gatesT_a = sb("gatesT_a", [EA, PAIR])
        msum = sb("msum", [128, EA, 3])
        mrs = sb("mrs", [128, EA, 3])
        mw = sb("mw", [128, EA, 3])
        cm = within("late", [128, 2, PAIR])
        gates_f = sb("gates_f", [TT, 3, EF])
        gparts = sb("gparts", [TT, 3, 3, EF])
        gpb = sb("gpb", [TT, 3, 3, EF], BF16)
        grest = sb("grest", [TT, 3, EF])
        gatesT_f = sb("gatesT_f", [EF, PAIR])
        partsT = sb("partsT", [3 * EF, PAIR], BF16)
        hr = within("late", [128, PAIR])
        hg = within("late", [128, 2, PAIR])

        patch_in = sem("patch_in")
        w_in = sem("w_in")
        bias_zero = sem("bias_zero")
        pool_step = sem("pool_step")
        pool_turn = sem("pool_turn")
        vector_turn = sem("vector_turn")
        zeroed = sem("zeroed")
        wpad_in = sem("wpad_in")
        x_in = [sem(f"x_in{b}") for b in range(2)]
        pvar = sem("pvar")
        prstd = sem("prstd")
        tvar = sem("tvar")
        trstd = sem("trstd")
        pnorm = sem("pnorm")
        ptran = sem("ptran")
        pfeat = sem("pfeat")
        pmm = sem("pmm")
        padd = sem("padd")
        ptok = sem("ptok")
        tok_out = [sem(f"tok_out{b}") for b in range(2)]
        dve_step = sem("dve_step")
        cls_sum = sem("cls_sum")
        cls_out = sem("cls_out")
        setup_pe = sem("setup_pe")
        setup_dve = sem("setup_dve")

        h_loaded = sem("h_loaded")
        h_free = sem("h_free")
        var_ready = sem("var_ready")
        rstd_ready = sem("rstd_ready")
        xn_ready = sem("xn_ready")
        xn_tran = sem("xn_tran")
        feat_ready = sem("feat_ready")
        proj_done = sem("proj_done")
        proj_act = sem("proj_act")
        proj_dve = sem("proj_dve")
        avar_ready = sem("avar_ready")
        arstd_ready = sem("arstd_ready")
        axn_ready = sem("axn_ready")
        axn_tran = sem("axn_tran")
        afeat_ready = sem("afeat_ready")
        sc_done = sem("sc_done")
        sc_taken = sem("sc_taken")
        max_ready = sem("max_ready")
        prob_ready = sem("prob_ready")
        pt_done = sem("pt_done")
        pt_taken = sem("pt_taken")
        pv_done = sem("pv_done")
        cts_ready = sem("cts_ready")
        rsum_ready = sem("rsum_ready")
        rsx_ready = sem("rsx_ready")
        x1r_ready = sem("x1r_ready")
        rb_done = sem("rb_done")
        ctn_ready = sem("ctn_ready")
        oproj_done = sem("oproj_done")
        mk_done = sem("mk_done")
        mk_act = sem("mk_act")
        mk_dve = sem("mk_dve")
        top_diff = sem("top_diff")
        top_exp = sem("top_exp")
        gates_ready = sem("gates_ready")
        gates_tran = sem("gates_tran")
        gatesT_ready = sem("gatesT_ready")
        q_done = sem("q_done")
        q_ready = sem("q_ready")
        rel_done = sem("rel_done")
        rel_mid = sem("rel_mid")
        rel_ready = sem("rel_ready")
        span_out = [sem(f"span_out{b}") for b in range(4)]
        bias_in = [sem(f"bias_in{e}") for e in range(EA)]
        mw_ready = sem("mw_ready")
        moa_done = sem("moa_done")
        fg_done = sem("fg_done")
        gates_whole = sem("gates_whole")
        fgates_ready = sem("fgates_ready")
        fg_tran = sem("fg_tran")
        fgT_ready = sem("fgT_ready")
        up_done = sem("up_done")
        relu_ready = sem("relu_ready")
        gated_ready = sem("gated_ready")
        down_done = sem("down_done")
        y_ready = sem("y_ready")
        stored = sem("stored")

        WLOADS = PLOADS = 0

        block = ctx.enter_context(nc.Block())

        XN, TRAN, FEAT = 2, 4, 4
        UNITS = HEADS + EA
        PROJ, PACT = 11, 11

        @block.sync
        def _(sp):
            def image_rows(step):
                for c in range(CH):
                    sp.dma_start(xin[step % 2][:, c * PATCH:(c + 1) * PATCH, :].rearrange("r p w -> r (p w)"),
                                 t["x"][step * PI:(step + 1) * PI, c].rearrange("b (g p) w -> b g (p w)", g=GRID)
                                 ).then_inc(x_in[step % 2], 16)

            def load(dst, source):
                nonlocal WLOADS
                sp.dma_start(dst, source, allow_slow_non_contiguous=True).then_inc(w_in, 16)
                WLOADS += 16

            for step in range(min(2, patch_steps)):
                image_rows(step)
            for r in range(2):
                load(clsr[r:r + 1, :], t["L0_tok_cls_token"].rearrange("a b d -> (a b) d"))
                load(clsp[r:r + 1, :], t["L0_tok_cls_pos_embedding"].rearrange("a b d -> (a b) d"))
            load(wk_v[:, 0], t["L0_attn_W_k"].rearrange("(k p) d -> p k d", p=128))
            load(wk_v[:, 1], t["L0_attn_W_v"].rearrange("(k p) d -> p k d", p=128))
            load(wdown[:], t["L0_attn_W_down_kv"].rearrange("(k p) d -> p k d", p=128))
            load(wupv[:], t["L0_attn_W_up_v"])
            load(decay[:], t["decay"])
            load(maskr[:], t["mask_rows"])
            load(maskc[:], t["mask_cols"])
            load(iota[:], t["iota"])
            for k, name in enumerate(("ln1_w", "ln1_b", "ln2_w", "ln2_b")):
                load(lnw[:, k, :], t["L0_ffn_" + name].rearrange("(k p) -> p k", p=128))
            load(gatew[:], t["L0_ffn_attn_gate_w"].rearrange("(k p) e -> p k e", p=128))
            for k in range(HALF):
                load(qw[:, :, k, :], t["L0_ffn_q_w"][:, k * 128:(k + 1) * 128, :].rearrange("e p h -> p e h"))
                load(w1[:, :, k, :], t["L0_ffn_ff_w1"][:, k * 128:(k + 1) * 128, :].rearrange("e p h -> p e h"))
            load(qb[:], t["L0_ffn_q_b"].rearrange("e h -> h e"))
            load(kw[:], t["L0_ffn_k_w"].rearrange("(k p) d -> p k d", p=128))
            load(kb[:], t["L0_ffn_k_b"].rearrange("(p o) -> p o", o=1))
            load(vw[:], t["L0_ffn_v_w"].rearrange("(k p) d -> p k d", p=128))
            load(vb[:], t["L0_ffn_v_b"].partition_broadcast(128))
            load(ow[:], t["L0_ffn_o_w"].rearrange("e h d -> h e d"))
            load(ob[:], t["L0_ffn_o_b"])
            load(reltab[:], t["L0_ffn_rel_table"][0:128])
            load(relT[:, 128:REL], t["L0_ffn_rel_table"][128:REL].rearrange("r h -> h r"))
            load(fgatew[:], t["L0_ffn_ff_gate_w"].rearrange("(k p) e -> p k e", p=128))
            load(b1[:], t["L0_ffn_ff_b1"].rearrange("e h -> h e"))
            load(w2[:], t["L0_ffn_ff_w2"].rearrange("e h d -> h e d"))
            load(b2[:], t["L0_ffn_ff_b2"])
            load(pick_f[:], t["pick"])
            sp.wait_ge(zeroed, 5)
            for k in range(HALF):
                sp.dma_start(wq[:, k, :, 0:HD], t["L0_attn_W_q"][k * 128:(k + 1) * 128, :].rearrange("p (h d) -> p h d", d=HD)).then_inc(wpad_in, 16)
            sp.dma_start(wupk[:, :, 0:HD], t["L0_attn_W_up_k"].rearrange("l (h d) -> l h d", d=HD)).then_inc(wpad_in, 16)
            rows = t["L0_attn_W_o"].rearrange("(p s j d) n -> j s d p n", p=PACKS, s=2, j=4)
            for j in range(4):
                for sub in range(2):
                    sp.dma_start(wo[32 * j + HD * sub:32 * j + HD * sub + HD, :, :], rows[j, sub]).then_inc(wpad_in, 16)


            for step in range(patch_steps):
                if step + 2 < patch_steps:
                    sp.wait_ge(pnorm, (step + 1) * GRID)
                    image_rows(step + 2)
                sp.wait_ge(ptok, step + 1)
                sp.dma_start(tokens_dram[step * PI * NPATCH:(step + 1) * PI * NPATCH, :].rearrange("(r w) d -> r (w d)", w=GRID),
                             ytok[step % 2][:, :, :].rearrange("r w d -> r (w d)")).then_inc(tok_out[step % 2], 16)
            sp.wait_ge(cls_sum, 1)
            sp.dma_start(cls_dram[:, :], clsr[:, :]).then_inc(cls_out, 16)
            sp.wait_ge(cls_out, 16)
            for b in range(min(2, patch_steps)):
                sp.wait_ge(tok_out[b], 16 * ((patch_steps - b + 1) // 2))

            def load_tokens(n):
                if not (isinstance(n, int) and n == 0):
                    sp.wait_ge(h_free, at(sp, n))
                pieces = []
                for a in range(2):
                    pieces += [("c", a, 0, a * SEQ, 1), ("p", a, 0, a * SEQ + 1, NPATCH), ("t", a, 0, a * SEQ + 1 + NPATCH, TXT)]
                for kind, a, first, row, count in pieces:
                    while count:
                        tile, r = divmod(row, TT)
                        m = min(count, TT - r)
                        if kind == "c":
                            s = cls_dram[a:a + 1, :]
                        elif kind == "p":
                            s = tokens_dram[bass.ds(n * 2 * NPATCH + a * NPATCH + first, m), :]
                        else:
                            s = t["txt"].rearrange("b s d -> (b s) d")[bass.ds(n * 2 * TXT + a * TXT + first, m), :]
                        sp.dma_start(h_in[r:r + m, tile, :], s).then_inc(h_loaded, 16)
                        first, row, count = first + m, row + m, count - m

            def spans(n):
                for e in range(EA):
                    sp.wait_ge(rel_ready, at(sp, n * EA + e + 1))
                    sp.dma_start(span_dram[e].rearrange("(s p) w -> p s w", p=128), spans_of[e % 4]).then_inc(span_out[e % 4], 16)
                    if e >= 1:
                        skew(n, e - 1)
                skew(n, EA - 1)

            def skew(n, e):
                r = at(sp, n * (EA // 4 * 16) + (e // 4 + 1) * 16)
                sp.wait_ge(span_out[e % 4], r)
                base = e * 3 * 128 * SPAN
                T = span_dram[:, :, :].tensor
                for slot, row, rows, q0 in ((0, 0, 128, 0), (2, 0, 128, REM), (1, 0, REM, 128), (1, 128 - REM, REM, 0)):
                    s = bass.AP(T, base + (slot * 128 + row) * SPAN + SEQ - 1 - q0, [[SPAN - 1, rows], [1, SEQ]])
                    sp.dma_start(bias[row:row + rows, e, slot, :], s).then_inc(bias_in[e], 16)

            def store(n):
                rows = out.rearrange("b s d -> (b s) d")
                r = at(sp, n + 1)
                sp.wait_ge(y_ready, r)
                sp.dma_start(rows[bass.ds(n * PAIR, PAIR), :].rearrange("(c p) d -> p c d", p=TT), resid[:, :, :]).then_inc(stored, 16)

            load_tokens(0)
            sp.wait_ge(bias_zero, 1)
            load_tokens(1)
            spans(0)
            with sp.Fori(0, pairs - 2) as n:
                load_tokens(n + 2)
                store(n)
                spans(n + 1)
            store(pairs - 2)
            spans(pairs - 1)
            store(pairs - 1)
            sp.wait_ge(stored, 16 * pairs)

        @block.gpsimd
        def _(pool):
            for z in (wq, wupk, v_main, v_rem):
                pool.memset(z[:], 0.0).then_inc(zeroed, 1)
            pool.memset(neghalf[:], -0.5).then_inc(zeroed, 1)
            pool.wait_ge(zeroed, 5)
            for step in range(patch_steps + 1):
                if step < patch_steps:
                    pool.wait_ge(pvar, step + 1)
                    nc.gpsimd.tensor_tensor(prs[step % 2], pve, neghalf[0:PR, :], ALU.pow).then_inc(prstd, 1)
                if step:
                    pool.wait_ge(tvar, step)
                    nc.gpsimd.tensor_tensor(trs, tve, neghalf[0:PR, :], ALU.pow).then_inc(trstd, 1)

            pool.wait_ge(setup_dve, 3)
            for b in range(min(2, patch_steps)):
                pool.wait_ge(tok_out[b], 16 * ((patch_steps - b + 1) // 2))
            pool.memset(bias[:, :, :, :], 0.0).then_inc(bias_zero, 1)

            def inverse_root(var, rstd, k):
                pool.wait_ge(var, at(pool, k))
                nc.gpsimd.tensor_tensor(rs[:, :], ve[:, :], neghalf[0:TT, 0:3], ALU.pow).then_inc(rstd, 1)

            count = [0]

            def link(i):
                count[0] += 1
                return i.then_inc(pool_step, 1)

            def linked():
                pool.wait_ge(pool_step, count[0])

            def restart():
                linked()
                pool.sem_clear(pool_step)
                count[0] = 0

            def gate_parts(n):
                pool.wait_ge(gates_whole, at(pool, n + 1))
                pool.sem_inc(pool_turn, 1)
                link(nc.gpsimd.tensor_copy(gpb[:, :, 0, :], gates_f[:]))
                linked()
                link(nc.gpsimd.tensor_tensor(grest[:], gates_f[:], gpb[:, :, 0, :], ALU.subtract))
                linked()
                link(nc.gpsimd.tensor_copy(gpb[:, :, 1, :], grest[:]))
                linked()
                link(nc.gpsimd.tensor_tensor(gparts[:, :, 2, :], grest[:], gpb[:, :, 1, :], ALU.subtract))
                nc.gpsimd.tensor_copy(gparts[:, :, 0:2, :].rearrange("p s a e -> p s (a e)"), gpb[:, :, 0:2, :].rearrange("p s a e -> p s (a e)")).then_inc(fgates_ready, 1)

            def pair(n, more):
                for p in range(PACKS):
                    if p:
                        wait_all(pool, (rsum_ready, n * PACKS + p + 1), (rb_done, n * PACKS + p))
                    else:
                        pool.wait_ge(rsum_ready, at(pool, n * PACKS + 1))
                    pool.sem_inc(pool_turn, 1)
                    for sub in range(2):
                        last = nc.gpsimd.tensor_copy(rsx[:, :, :].rearrange("p s (j b d) -> p s j b d", j=4, b=2)[:, :, :, sub],
                                                     columns(rsum[:, :, 8 * p + 4 * sub:8 * p + 4 * sub + 4], HD))
                    last.then_inc(rsx_ready, 1)
                inverse_root(var_ready, rstd_ready, n * 3 + 1)
                inverse_root(var_ready, rstd_ready, n * 3 + 2)
                for k in range(HALF):
                    pool.wait_ge(feat_ready, at(pool, n * FEAT + 1 + k))
                    pool.sem_inc(pool_turn, 1)
                    nc.gpsimd.tensor_copy(x1R[:, k].rearrange("p a (b r) -> p a b r", b=2), ends_of(x1T[:, k, :])).then_inc(x1r_ready, 1)
                if more:
                    inverse_root(avar_ready, arstd_ready, n + 2)
                inverse_root(var_ready, rstd_ready, n * 3 + 3)
                gate_parts(n)

            inverse_root(avar_ready, arstd_ready, 1)
            pair(0, True)
            restart()
            with pool.Fori(0, pairs - 2) as n:
                pair(n + 1, True)
                restart()
            pair(pairs - 1, False)

        @block.scalar
        def _(act):
            def load(dst, source):
                nonlocal PLOADS
                act.dma_start(dst, source, allow_slow_non_contiguous=True).then_inc(patch_in, 16)
                PLOADS += 16

            load(ident[:], t["ident"])
            tw = t["L0_tok_W"].rearrange("(h p c) d -> p c h d", p=128, c=CH)
            for c in range(CH):
                load(wt[:, 2 * c:2 * c + 2, :], tw[:, c])
            for dst, name in ((ln1g, "L0_tok_ln1_g"), (ln1b, "L0_tok_ln1_b")):
                v = t[name].rearrange("(h p c) -> p c h", p=128, c=CH)
                for c in range(CH):
                    load(dst[:, 2 * c:2 * c + 2], v[:, c])
            for dst, name in ((tbias, "L0_tok_bias"), (ln2g, "L0_tok_ln2_g"), (tln2b, "L0_tok_ln2_b")):
                load(dst[:], t[name].partition_broadcast(128))
            load(peb[:], t["pe"][0:PR])
            act.wait_ge(patch_in, PLOADS)
            for step in range(patch_steps):
                for w in range(GRID):
                    u = step * GRID + w
                    if u >= 2:
                        act.wait_ge(pmm, u - 1)
                    for half in range(2):
                        act.wait_ge(ptran, 2 * u + half + 1)
                        for c in range(3):
                            k = 3 * half + c
                            last = nc.scalar.activation(xpT[:, u % 2, k, :], S_BANKS[half][:, c * PR:(c + 1) * PR], ACT.Identity,
                                                        bias=ln1b[:, k:k + 1], scale=ln1g[:, k:k + 1])
                        last.then_inc(pfeat, 1)

            def features(n, k, dst, gain):
                for c in range(HALF):
                    act.wait_ge(xn_tran, at(act, n * TRAN + 2 * k + c + 1))
                    nc.scalar.activation(dst[:, c, :], S_BANKS[c][:, 0:PAIR], ACT.Identity,
                                         bias=lnw[:, gain + 1, c:c + 1], scale=lnw[:, gain, c:c + 1]).then_inc(feat_ready, 1)

            def early_features(p, c):
                act.wait_ge(axn_tran, at(act, p * 2 + c + 1))
                nc.scalar.copy(xaT[:, c, :], GB[:, 0:PAIR]).then_inc(afeat_ready, 1)

            def take_queries(p):
                for g in range(GROUPS):
                    act.wait_ge(proj_done, at(act, p * PROJ + g + 1))
                    nc.scalar.copy(qT[:, g, :], (CT, PT)[g % 2][:, 0:PAIR]).then_inc(proj_act, 1)

            def take_latent(p):
                act.wait_ge(proj_done, at(act, p * PROJ + 5))
                nc.scalar.copy(latT[:, :], CT[0:LAT, 0:PAIR]).then_inc(proj_act, 1)
                nc.scalar.copy(latR[:, :, :].rearrange("p a (b r) -> p a b r", b=2), ends_of(CT[0:LAT, 0:PAIR])).then_inc(proj_act, 1)

            def take_keys(p):
                for g in range(GROUPS):
                    act.wait_ge(proj_done, at(act, p * PROJ + 6 + g))
                    nc.scalar.copy(kT[:, g, :], (PT, CT)[g % 2][:, 0:PAIR]).then_inc(proj_act, 1)

            def take_values(p):
                act.wait_ge(proj_done, at(act, p * PROJ + 10))
                for sub in range(2):
                    last = nc.scalar.copy(head_places(v_main, 128, 0, 2 * PACKS, sub),
                                          PT[:, :].rearrange("p (q s j d) -> p q s j d", s=2, j=4, d=HD)[:, :, sub])
                last.then_inc(proj_act, 1)

            def softmax_row(n, u, parity):
                act.wait_ge(max_ready, at(act, n * UNITS + u + 1))
                for s in range(3):
                    acc = sums[:, s, u:u + 1] if u < HEADS else msum[:, u - HEADS, s:s + 1]
                    last = nc.scalar.activation(prob[:, parity, s, u % 2 * SEQ:(u % 2 + 1) * SEQ], sc[:, u % 2, s, :], ACT.Exp,
                                                bias=nmax[:, u % 2, s:s + 1], scale=1.0, accum_out=acc)
                last.then_inc(prob_ready, 1)

            def take_main(n, u):
                p, h = divmod(u, 2)
                act.wait_ge(pt_done, at(act, n * (3 * UNITS // 2) + 3 * p + h + 1))
                nc.scalar.copy(ptm[:, u % 4, :], PT[:, 0:WIDE]).then_inc(pt_taken, 1)

            def take_rem(n, p):
                act.wait_ge(pt_done, at(act, n * (3 * UNITS // 2) + 3 * p + 3))
                nc.scalar.copy(ptr[:, p % 2, :], PT[0:2 * REM, 0:WIDE]).then_inc(pt_taken, 1)

            def relu(m, e):
                if e == 0:
                    act.wait_ge(up_done, at(act, m * EF + 1))
                else:
                    wait_all(act, (up_done, m * EF + e + 1), (gated_ready, m * EF + e))
                nc.scalar.activation(hr[:, :], HB[:, 0:PAIR], ACT.Relu, bias=b1[:, e:e + 1], scale=1.0).then_inc(relu_ready, 1)

            def top_exp_step(n, k):
                act.wait_ge(top_diff, at(act, n * 2 + k + 1))
                rows = 128 if k == 0 else TT
                nc.scalar.activation(ge[0:rows, :], gd[0:rows, :], ACT.Exp).then_inc(top_exp, 1)

            def gate_rows(m):
                act.wait_ge(fg_tran, at(act, m * 2 + 1))
                nc.scalar.copy(gatesT_f[:, :], HB[0:EF, 0:PAIR]).then_inc(fgT_ready, 1)
                act.wait_ge(fg_tran, at(act, m * 2 + 2))
                nc.scalar.copy(partsT[:, :], GB[0:3 * EF, 0:PAIR]).then_inc(fgT_ready, 1)

            def latent_attention(n, m):
                e = 0
                for h in range(HEAD_STEPS):
                    if m is not None and h in EXPERT_STEPS and h >= HEADS:
                        relu(m, e)
                        e += 1
                    if h % 2 == 0 and h >= 4:
                        take_rem(n, (h - 4) // 2)
                    if h in (10, 18):
                        act.wait_ge(pv_done, at(act, n * (PACKS + EA) + h // 8))
                        nc.scalar.copy(cts[:, :], CT[:, 0:PAIR]).then_inc(cts_ready, 1)
                    if 2 <= h < HEADS + 2:
                        take_main(n, h - 2)
                    if h == GATE_STEP and m is not None:
                        gate_rows(m)
                    if h == 0:
                        take_values(n)
                    if h < HEADS:
                        softmax_row(n, h, (h // 2) % 2)
                    if m is not None and h in EXPERT_STEPS and h < HEADS:
                        relu(m, e)
                        e += 1
                if m is not None:
                    for e in range(len(EXPERT_STEPS), EF):
                        relu(m, e)

            def mixture_of_attention(n, more):
                features(n, 0, x1T, 0)
                act.wait_ge(mk_done, at(act, n * 4 + 1))
                nc.scalar.activation(kmT[:, :], HB[:, 0:PAIR], ACT.Identity, bias=kb[:, 0:1], scale=1.0).then_inc(mk_act, 1)
                top_exp_step(n, 0)
                for e in range(EA + 1):
                    if e < EA:
                        act.wait_ge(q_done, at(act, n * EA + e + 1))
                        nc.scalar.activation(qm[:, e, :], (HB, GB)[e % 2][:, 0:PAIR], ACT.Identity, bias=qbs[:, e:e + 1], scale=SCALE_Q).then_inc(q_ready, 1)
                    if e >= 1:
                        x = e - 1
                        if x >= 4:
                            wait_all(act, (rel_done, n * EA + x + 1), (span_out[x % 4], n * (EA // 4 * 16) + 16))
                        else:
                            act.wait_ge(rel_done, at(act, n * EA + x + 1))
                        nc.scalar.copy(spans_of[x % 4][:, :, SIDE:SIDE + REL],
                                       (CT, PT)[x % 2][:, 0:3 * REL].rearrange("p (s r) -> p s r", s=3)).then_inc(rel_mid, 1)
                    if e >= FIRST_SCORES + 1:
                        softmax_row(n, HEADS + e - FIRST_SCORES - 1, 0)
                softmax_row(n, HEADS + 2, 1)
                wait_all(act, (span_out[0], n * (EA // 4 * 16) + 32), (span_out[1], n * (EA // 4 * 16) + 32))
                for x in range(2, EA + 5):
                    if x % 2 == 0 and 4 <= x < EA + 4:
                        take_rem(n, (HEADS + x - 4) // 2)
                    if 2 <= x < EA + 2:
                        take_main(n, HEADS + x - 2)
                    if 3 <= x < EA:
                        softmax_row(n, HEADS + x, x // 2 % 2)
                    if 4 <= x < EA + 4:
                        e = x - 4
                        act.wait_ge(pv_done, at(act, n * (PACKS + EA) + PACKS + e + 1))
                        nc.scalar.copy(cm[:, e % 2, :], (CT, HB)[e % 2][:, 0:PAIR]).then_inc(cts_ready, 1)
                    if more and x in (6, 7):
                        early_features(n + 1, x - 6)
                if more:
                    take_queries(n + 1)
                    take_latent(n + 1)
                features(n, 1, x2T, 2)
                if more:
                    take_keys(n + 1)
                top_exp_step(n, 1)

            early_features(0, 0)
            early_features(0, 1)
            take_queries(0)
            take_latent(0)
            take_keys(0)
            latent_attention(0, None)
            mixture_of_attention(0, True)
            with act.Fori(0, pairs - 2) as n:
                latent_attention(n + 1, n)
                mixture_of_attention(n + 1, True)
            latent_attention(pairs - 1, pairs - 2)
            mixture_of_attention(pairs - 1, False)
            gate_rows(pairs - 1)
            for e in range(EF):
                relu(pairs - 1, e)

        @block.vector
        def _(dve):
            count = [0]

            def link(i):
                count[0] += 1
                return i.then_inc(dve_step, 1)

            def linked():
                dve.wait_ge(dve_step, count[0])

            def restart():
                linked()
                dve.sem_clear(dve_step)
                count[0] = 0

            dve.wait_ge(patch_in, PLOADS)
            link(nc.vector.tensor_tensor(peb[:], peb[:], spread(tln2b[0:PR, :], GRID), ALU.add))

            def rows_of(step):
                return xin[step % 2].rearrange("r q (g w) -> r g q w", g=GRID)

            def patch_statistics(step, w):
                for half in range(2):
                    link(nc.vector.bn_stats(pst[:, w, half, :], rows_of(step)[:, w, 24 * half:24 * half + 24, :]))

            def patch_variances(step):
                linked()
                for w in range(GRID):
                    link(nc.vector.bn_aggr(pmv[step % 2][:, w, :], pst[:, w, :, :].rearrange("r h s -> r (h s)")))
                linked()
                if step:
                    dve.wait_ge(prstd, step)
                nc.vector.tensor_scalar(pve, pmv[step % 2][:, :, 1], EPS, None, ALU.add).then_inc(pvar, 1)

            def normalize(step, w):
                u = step * GRID + w
                if w == 0:
                    dve.wait_ge(prstd, step + 1)
                if u >= 2:
                    dve.wait_ge(ptran, 2 * (u - 1))
                nc.vector.tensor_scalar(xpn[:, u % 2, :].rearrange("r (q w) -> r q w", w=PATCH), rows_of(step)[:, w],
                                        pmv[step % 2][:, w, 0:1], prs[step % 2][:, w:w + 1], ALU.subtract, ALU.mult).then_inc(pnorm, 1)

            def finish_tokens(step):
                y = ytok[step % 2]
                dve.wait_ge(trstd, step + 1)
                for w in range(GRID):
                    link(nc.vector.tensor_scalar(y[:, w, :], y[:, w, :], tmv[:, w, 0:1], trs[:, w:w + 1], ALU.subtract, ALU.mult))
                linked()
                link(nc.vector.tensor_tensor(y, y, spread(ln2g[0:PR, :], GRID), ALU.mult))
                linked()
                nc.vector.tensor_tensor(y, y, peb[:], ALU.add).then_inc(ptok, 1)

            dve.wait_ge(x_in[0], 16 * CH)
            for w in range(GRID):
                patch_statistics(0, w)
            patch_variances(0)
            for step in range(patch_steps):
                normalize(step, 0)
                normalize(step, 1)
                if step:
                    finish_tokens(step - 1)
                if step >= 2:
                    dve.wait_ge(tok_out[step % 2], 16 * (step // 2))
                if step + 1 < patch_steps:
                    dve.wait_ge(x_in[(step + 1) % 2], 16 * CH * ((step + 1) // 2 + 1))
                for w in range(GRID):
                    u = step * GRID + w
                    dve.wait_ge(pmm, u + 1)
                    nc.vector.tensor_tensor(ytok[step % 2][:, w, :], (CT, PT)[u % 2][0:PR, 0:D], tbias[0:PR, :], ALU.add).then_inc(padd, 1)
                    if w + 2 < GRID:
                        normalize(step, w + 2)
                    dve.wait_ge(padd, u + 1)
                    link(nc.vector.bn_stats(tst[:, w, :], ytok[step % 2][:, w, :]))
                    if step + 1 < patch_steps:
                        patch_statistics(step + 1, w)
                if step + 1 < patch_steps:
                    patch_variances(step + 1)
                linked()
                for w in range(GRID):
                    link(nc.vector.bn_aggr(tmv[:, w, :], tst[:, w, :]))
                linked()
                nc.vector.tensor_scalar(tve, tmv[:, :, 1], EPS, None, ALU.add).then_inc(tvar, 1)
            finish_tokens(patch_steps - 1)

            dve.wait_ge(w_in, WLOADS)
            nc.vector.tensor_tensor(clsr[:], clsr[:], clsp[:], ALU.add).then_inc(cls_sum, 1)
            link(nc.vector.tensor_tensor(wk_v[:, 0], wk_v[:, 0], wk_v[:, 1], ALU.add))
            link(nc.vector.tensor_copy(pick[:], pick_f[:]))
            link(nc.vector.tensor_scalar(qbs[:], qb[:], SCALE_Q, None, ALU.mult))
            link(nc.vector.tensor_scalar(vbm[:, 0, :], vb[0:2 * REM, :], maskc[:, 0:1], None, ALU.mult))
            nc.vector.tensor_scalar(vbm[:, 1, :], vb[0:2 * REM, :], maskc[:, 1:2], None, ALU.mult).then_inc(setup_dve, 1)
            dve.wait_ge(setup_pe, 1)
            for k in range(HALF):
                link(nc.vector.tensor_copy(wkvT[:, k, :], S_BANKS[k][:, 0:D]))
            nc.vector.tensor_copy(relT[:, 0:128], PT[:, 0:128]).then_inc(setup_dve, 1)
            dve.wait_ge(setup_pe, 2)
            nc.vector.tensor_copy(wlat[:, :, :], CT[:, 0:HALF * LAT].rearrange("p (k l) -> p k l", k=HALF)).then_inc(setup_dve, 1)

            def variance(x, var):
                for j in range(3):
                    link(nc.vector.bn_stats(st[:, j, :], x[:, j, :]))
                linked()
                for j in range(3):
                    link(nc.vector.bn_aggr(mv[:, j, :], st[:, j, :]))
                linked()
                nc.vector.tensor_scalar(ve[:, :], mv[:, :, 1], EPS, None, ALU.add).then_inc(var, 1)

            def normalized(rstd, k, x, dst, done):
                dve.wait_ge(rstd, at(dve, k))
                for j in range(3):
                    last = nc.vector.tensor_scalar(dst[:, j, :], x[:, j, :], mv[:, j, 0:1], rs[:, j:j + 1], ALU.subtract, ALU.mult)
                    if j < 2 or done is None:
                        link(last)
                if done is not None:
                    last.then_inc(done, 1)

            def two_largest(rows, experts):
                for s in range(3):
                    link(nc.vector.max(gtop[0:rows, s, :], glog[0:rows, s, 0:experts]))
                linked()
                for s in range(3):
                    link(nc.vector.max_index(gidx[0:rows, s, :], gtop[0:rows, s, :], glog[0:rows, s, 0:experts]))
                nc.vector.tensor_tensor(gd[0:rows, :], gtop[0:rows, :, 1], gtop[0:rows, :, 0], ALU.subtract).then_inc(top_diff, 1)
                linked()
                link(nc.vector.tensor_copy(gidf[0:rows], gidx[0:rows, :, 0:2]))

            def gates_of(n, k, rows, experts, dst):
                dve.wait_ge(top_exp, at(dve, n * 2 + k + 1))
                link(nc.vector.tensor_scalar(gs[0:rows], ge[0:rows], 1.0, None, ALU.add))
                linked()
                link(nc.vector.reciprocal(g1[0:rows], gs[0:rows]))
                linked()
                link(nc.vector.tensor_tensor(g2[0:rows], ge[0:rows], g1[0:rows], ALU.mult))
                linked()
                for s in range(3):
                    link(nc.vector.tensor_scalar(ga[0:rows, s, 0:experts], iota[0:rows, 0:experts], gidf[0:rows, s, 0:1], g1[0:rows, s:s + 1], ALU.is_equal, ALU.mult))
                    link(nc.vector.tensor_scalar(gb[0:rows, s, 0:experts], iota[0:rows, 0:experts], gidf[0:rows, s, 1:2], g2[0:rows, s:s + 1], ALU.is_equal, ALU.mult))
                linked()
                return nc.vector.tensor_tensor(dst[0:rows], ga[0:rows, :, 0:experts], gb[0:rows, :, 0:experts], ALU.add)

            def scores(n, u):
                if u < 2:
                    dve.wait_ge(sc_done, at(dve, n * UNITS + u + 1))
                    if not (isinstance(n, int) and n == 0):
                        dve.wait_ge(prob_ready, at(dve, n * UNITS + u - 1))
                else:
                    wait_all(dve, (sc_done, n * UNITS + u + 1), (prob_ready, n * UNITS + u - 1))
                s = S_BANKS[u % 2][:, 0:3 * SEQ].rearrange("p (s k) -> p s k", s=3)
                if u < HEADS:
                    i = nc.vector.tensor_tensor(sc[:, u % 2], s, decay[:], ALU.mult)
                else:
                    e = u - HEADS
                    dve.wait_ge(bias_in[e], at(dve, n * 64 + 64))
                    i = nc.vector.tensor_tensor(sc[:, u % 2], s, bias[:, e], ALU.add)
                i.then_inc(sc_taken, 1)
                dve.wait_ge(sc_taken, at(dve, n * UNITS + u + 1))
                nc.vector.tensor_reduce(nmax[:, u % 2, :], sc[:, u % 2], AX.X, ALU.max, negate=True).then_inc(max_ready, 1)

            def gate_hidden(m, e):
                if e >= 2:
                    wait_all(dve, (relu_ready, m * EF + e + 1), (down_done, m * EF + e - 1))
                else:
                    dve.wait_ge(relu_ready, at(dve, m * EF + e + 1))
                nc.vector.tensor_tensor(hg[:, e % 2, :], GB[:, 0:PAIR], hr[:, :], ALU.mult).then_inc(gated_ready, 1)

            def finish(m):
                dve.wait_ge(down_done, at(dve, m * EF + EF))
                link(nc.vector.tensor_tensor(resid[:, 0:2, :], ACC[0][0:TT, :].rearrange("p (c d) -> p c d", c=2), resid[:, 0:2, :], ALU.add))
                nc.vector.tensor_tensor(resid[:, 2, :], ACC[1][0:TT, 0:D], resid[:, 2, :], ALU.add).then_inc(y_ready, 1)

            def remainder_values(p):
                dve.wait_ge(proj_done, at(dve, p * PROJ + 11))
                for a in range(2):
                    for sub in range(2):
                        last = nc.vector.tensor_tensor(head_places(v_rem, 2 * REM, a, PACKS, sub),
                                                       CT[0:2 * REM, a * D:(a + 1) * D].rearrange("p (q s j d) -> p q s j d", s=2, j=4, d=HD)[:, :, sub],
                                                       maskr[:].rearrange("p (q s j) d -> p q s j d", s=2, j=4)[:, :, sub], ALU.mult)
                        if a + sub < 2:
                            link(last)
                last.then_inc(proj_dve, 1)

            def latent_attention(n, m):
                e = 0
                for h in range(HEAD_STEPS):
                    if h in (8, 16):
                        dve.wait_ge(prob_ready, at(dve, n * UNITS + h))
                        nc.vector.reciprocal(rsum[:, :, h - 8:h], sums[:, :, h - 8:h]).then_inc(rsum_ready, 1)
                    if h < HEADS:
                        scores(n, h)
                    if m is not None and h == 0:
                        gates_of(m, 1, TT, EF, gates_f).then_inc(gates_whole, 1)
                    if h == 1:
                        remainder_values(n)
                    if h in (11, 19):
                        g = h // 8 - 1
                        wait_all(dve, (rb_done, n * PACKS + g + 1), (cts_ready, n * (PACKS + EA) + g + 1))
                        rb = bass.AP(CT[:, :].tensor, 0, [list(CT[:, :].ap[0]), [IMG1, 2], [1, SEQ]])
                        nc.vector.tensor_tensor(ctn[:, g, :].rearrange("p (a q) -> p a q", a=2), rb,
                                                cts[:, :].rearrange("p (a q) -> p a q", a=2), ALU.mult).then_inc(ctn_ready, 1)
                    if m is not None and h in EXPERT_STEPS:
                        gate_hidden(m, e)
                        e += 1

            def mixture_of_attention(n, m, more):
                e = len(EXPERT_STEPS)
                if m is not None:
                    gate_hidden(m, e)
                    e += 1
                dve.wait_ge(oproj_done, at(dve, n + 1))
                link(nc.vector.tensor_tensor(h1[:, 0:2, :], S_BANKS[0][0:TT, :].rearrange("p (c d) -> p c d", c=2), h_in[:, 0:2, :], ALU.add))
                nc.vector.tensor_tensor(h1[:, 2, :], S_BANKS[1][0:TT, 0:D], h_in[:, 2, :], ALU.add).then_inc(h_free, 1)
                dve.wait_ge(h_free, at(dve, n + 1))
                variance(h1, var_ready)
                if m is not None:
                    gate_hidden(m, e)
                    e += 1
                normalized(rstd_ready, n * 3 + 1, h1, src, None)
                linked()
                variance(src, var_ready)
                if m is not None:
                    gate_hidden(m, e)
                    e += 1
                normalized(rstd_ready, n * 3 + 2, src, xn, xn_ready)
                if m is not None:
                    while e < EF:
                        gate_hidden(m, e)
                        e += 1
                    finish(m)
                dve.wait_ge(mk_done, at(dve, n * 4 + 2))
                nc.vector.tensor_copy(glog[:, :, 0:EA], PT[:, 0:3 * EA].rearrange("p (s e) -> p s e", s=3)).then_inc(mk_dve, 1)
                dve.wait_ge(mk_dve, at(dve, n * 3 + 1))
                dve.sem_inc(vector_turn, 1)
                two_largest(128, EA)
                gates_of(n, 0, 128, EA, gates_a).then_inc(gates_ready, 1)
                def clipped(x):
                    dve.wait_ge(rel_mid, at(dve, n * EA + x + 1))
                    rows = spans_of[x % 4]
                    link(nc.vector.tensor_copy(rows[:, :, 0:SIDE], columns(rows[:, :, SIDE], SIDE)))
                    nc.vector.tensor_copy(rows[:, :, SIDE + REL:SPAN], columns(rows[:, :, SIDE + REL - 1], SIDE)).then_inc(rel_ready, 1)

                def weigh(e):
                    dve.wait_ge(prob_ready, at(dve, n * UNITS + HEADS + e + 1))
                    link(nc.vector.reciprocal(mrs[:, e, :], msum[:, e, :]))
                    linked()
                    link(nc.vector.tensor_tensor(mw[:, e, :], mrs[:, e, :], gates_a[:, :, e], ALU.mult))
                    linked()
                    for s in range(3):
                        p = prob[:, e // 2 % 2, s, e % 2 * SEQ:(e % 2 + 1) * SEQ]
                        last = nc.vector.tensor_scalar(p, p, mw[:, e, s:s + 1], None, ALU.mult)
                        if s < 2:
                            link(last)
                    last.then_inc(mw_ready, 1)

                for x in range(EA - 1):
                    clipped(x)
                    if x == 4:
                        dve.wait_ge(gates_tran, at(dve, n + 1))
                        nc.vector.tensor_copy(gatesT_a[:, :].rearrange("e (a q) -> e a q", a=2),
                                              bass.AP(ACC[1][:, :].tensor, 0, [[ACC[1][:, :].ap[0][0], EA], [IMG1, 2], [1, SEQ]])).then_inc(gatesT_ready, 1)
                    if x >= FIRST_SCORES - 1:
                        scores(n, HEADS + x - FIRST_SCORES + 1)
                weigh(0)
                clipped(EA - 1)
                for x in range(2, EA + 1):
                    if x < EA:
                        scores(n, HEADS + x)
                    if x == 3:
                        dve.wait_ge(mk_done, at(dve, n * 4 + 4))
                        for par in range(2):
                            for a in range(2):
                                last = nc.vector.scalar_tensor_tensor(out=vmr[:, par, a, :], in0=HB[0:2 * REM, a * 128:(a + 1) * 128],
                                                                      scalar=maskc[:, par:par + 1], in1=vbm[:, par, :],
                                                                      op0=ALU.mult, op1=ALU.add)
                                if par + a < 2:
                                    link(last)
                        last.then_inc(mk_dve, 1)
                    weigh(x - 1)
                    if x == 2:
                        dve.wait_ge(mk_done, at(dve, n * 4 + 3))
                        nc.vector.tensor_tensor(vm[:, :, :, :].rearrange("p b a d -> p (b a) d"), GB[:, :].rearrange("p (c d) -> p c d", c=4), spread(vb[:, :], 4), ALU.add).then_inc(mk_dve, 1)
                    if more and x == 4:
                        dve.wait_ge(h_loaded, at(dve, n * LOADS + 2 * LOADS))
                        variance(h_in, avar_ready)
                    if more and x == 5:
                        normalized(arstd_ready, n + 2, h_in, xn, axn_ready)
                dve.wait_ge(moa_done, at(dve, n + 1))
                link(nc.vector.tensor_tensor(x2[:, 0:2, :], ACC[0][0:TT, :].rearrange("p (c d) -> p c d", c=2), src[:, 0:2, :], ALU.add))
                link(nc.vector.tensor_tensor(x2[:, 2, :], ACC[1][0:TT, 0:D], src[:, 2, :], ALU.add))
                linked()
                variance(x2, var_ready)
                if m is not None:
                    dve.wait_ge(stored, at(dve, m * 16 + 16))
                link(nc.vector.tensor_tensor(resid[:], x2[:], h1[:], ALU.add))
                normalized(rstd_ready, n * 3 + 3, x2, xn, xn_ready)
                dve.wait_ge(fg_done, at(dve, n + 1))
                link(nc.vector.tensor_copy(glog[0:TT], GB[0:TT, 0:3 * EF].rearrange("p (s e) -> p s e", s=3)))
                linked()
                two_largest(TT, EF)

            dve.wait_ge(h_loaded, LOADS)
            variance(h_in, avar_ready)
            normalized(arstd_ready, 1, h_in, xn, axn_ready)
            latent_attention(0, None)
            mixture_of_attention(0, None, True)
            restart()
            with dve.Fori(0, pairs - 2) as n:
                latent_attention(n + 1, n)
                mixture_of_attention(n + 1, n, True)
                restart()
            latent_attention(pairs - 1, pairs - 2)
            mixture_of_attention(pairs - 1, pairs - 2, False)
            gates_of(pairs - 1, 1, TT, EF, gates_f).then_inc(gates_whole, 1)
            for e in range(EF):
                gate_hidden(pairs - 1, e)
            finish(pairs - 1)

        @block.tensor
        def _(pe):
            mm = nc.tensor.matmul
            I = ident

            columns_ = patch_steps * GRID
            pe.wait_ge(patch_in, PLOADS)

            def embed(u):
                pe.wait_ge(pfeat, 2 * u + 2)
                if u >= 2:
                    pe.wait_ge(padd, u - 1)
                for k in range(PC):
                    last = mm((CT, PT)[u % 2][0:PR, 0:D], xpT[:, u % 2, k, :], wt[:, k, :], start=k == 0, stop=k == PC - 1)
                last.then_inc(pmm, 1)

            for u in range(columns_):
                pe.wait_ge(pnorm, u + 1)
                for half in range(2):
                    if u:
                        pe.wait_ge(pfeat, 2 * (u - 1) + half + 1)
                    for c in range(3):
                        k = 3 * half + c
                        last = nc.tensor.transpose(S_BANKS[half][:, c * PR:(c + 1) * PR], xpn[:, u % 2, k * 128:(k + 1) * 128], I[0:PR, 0:PR])
                    last.then_inc(ptran, 1)
                if u % GRID:
                    embed(u - 1)
                if u % GRID == GRID - 1:
                    embed(u)


            pe.wait_ge(setup_dve, 1)
            pe.wait_ge(padd, patch_steps * GRID)
            for c in range(HALF):
                for k in range(HALF):
                    nc.tensor.transpose(S_BANKS[c][:, k * 128:(k + 1) * 128], wk_v[:, 0, k, c * 128:(c + 1) * 128], I[:])
            nc.tensor.transpose(PT[:, 0:128], reltab[:], I[:]).then_inc(setup_pe, 1)
            pe.wait_ge(setup_dve, 2)
            for k in range(HALF):
                for c in range(HALF):
                    last = mm(CT[:, k * LAT:(k + 1) * LAT], wkvT[:, c, k * 128:(k + 1) * 128], wdown[:, c, :], start=c == 0, stop=c == HALF - 1)
            last.then_inc(setup_pe, 1)
            pe.wait_ge(setup_dve, 3)
            pe.wait_ge(wpad_in, 16 * (HALF + 1 + 8))

            def transposes(n, k):
                pe.wait_ge(xn_ready, at(pe, n * XN + k + 1))
                for c in range(HALF):
                    for j in range(3):
                        last = nc.tensor.transpose(S_BANKS[c][:, j * TT:(j + 1) * TT], xn[:, j, c * 128:(c + 1) * 128], I[0:TT, 0:TT])
                    last.then_inc(xn_tran, 1)

            def early_transposes(p, c):
                pe.wait_ge(axn_ready, at(pe, p + 1)) if c == 0 else pe.wait_ge(afeat_ready, at(pe, p * 2 + 1))
                for j in range(3):
                    last = nc.tensor.transpose(GB[:, j * TT:(j + 1) * TT], xn[:, j, c * 128:(c + 1) * 128], I[0:TT, 0:TT])
                last.then_inc(axn_tran, 1)

            def gate_logits(n, j):
                if j == 0:
                    pe.wait_ge(feat_ready, at(pe, n * FEAT + 4))
                for k in range(HALF):
                    last = mm(GB[0:TT, j * EF:(j + 1) * EF], x2T[:, k, j * TT:(j + 1) * TT], fgatew[:, k, :], start=k == 0, stop=k == 1)
                if j == 2:
                    last.then_inc(fg_done, 1)

            def project(n, part, logits_of=None):
                def taken(k):
                    pe.wait_ge(proj_act, at(pe, n * PACT + k))

                if part == 0:
                    pe.wait_ge(afeat_ready, at(pe, n * 2 + 2))
                    for g in range(GROUPS):
                        if g >= 2:
                            taken(g - 1)
                        for k in range(HALF):
                            last = mm((CT, PT)[g % 2][:, 0:PAIR], wq[:, k, 4 * g:4 * g + 4, :].rearrange("p h d -> p (h d)"), xaT[:, k, :], start=k == 0, stop=k == 1)
                        last.then_inc(proj_done, 1)
                if part == 1:
                    taken(3)
                    for k in range(HALF):
                        last = mm(CT[0:LAT, 0:PAIR], wlat[:, k, :], xaT[:, k, :], start=k == 0, stop=k == 1)
                    last.then_inc(proj_done, 1)
                if part == 2:
                    taken(6)
                    for g in range(GROUPS):
                        if g >= 2:
                            taken(5 + g)
                        mm((PT, CT)[g % 2][:, 0:PAIR], wupk[:, 4 * g:4 * g + 4, :].rearrange("p h d -> p (h d)"), latT[:, :], start=True, stop=True).then_inc(proj_done, 1)
                        if g >= 1 and logits_of is not None:
                            gate_logits(logits_of, g - 1)

            def latent_values(n, part):
                if part == 0:
                    pe.wait_ge(proj_act, at(pe, n * PACT + 9))
                    halves = wupv[:, :].rearrange("l (h b d) -> l b h d", b=2, d=HD)
                    places = PT[:, :].rearrange("p (a h b d) -> p a b h d", a=2, b=2, d=HD)
                    for a in range(2):
                        for b in range(2):
                            k0 = a * SEQ + b * REM
                            last = mm(places[:, a, b], latT[:, k0:k0 + 128], halves[:, b], start=True, stop=True, skip_group_check=True)
                else:
                    pe.wait_ge(proj_act, at(pe, n * PACT + 10))
                    for a in range(2):
                        last = mm(CT[0:2 * REM, a * D:(a + 1) * D], latR[:, a, :], wupv[:, :], start=True, stop=True)
                last.then_inc(proj_done, 1)

            def head_scores(n, h):
                g, j = divmod(h, 4)
                if h == 0:
                    pe.wait_ge(proj_act, at(pe, n * PACT + 10))
                if h >= 2:
                    pe.wait_ge(sc_taken, at(pe, n * UNITS + h - 1))
                for s, row, col, rows, a in SLOTS:
                    last = mm(S_BANKS[h % 2][row:row + rows, s * SEQ:(s + 1) * SEQ], qT[32 * j:32 * j + HD, g, col:col + rows],
                              kT[32 * j:32 * j + HD, g, a * SEQ:(a + 1) * SEQ], start=True, stop=True, tile_position=(32 * j, row))
                last.then_inc(sc_done, 1)

            def tran_main(n, u):
                p, h = divmod(u, 2)
                k = n * (3 * UNITS // 2) + 3 * p + h
                ready = prob_ready if u < HEADS else mw_ready
                value = n * UNITS + u + 1 if u < HEADS else n * EA + (u - HEADS) + 1
                if u == 0:
                    wait_all(pe, (ready, value), (proj_act, n * PACT + 11))
                else:
                    wait_all(pe, (ready, value), (pt_taken, k))
                for s in range(3):
                    last = nc.tensor.transpose(PT[:, s * 128:(s + 1) * 128], prob[:, p % 2, s, (SEQ + REM) * h:(SEQ + REM) * h + 128], I[:])
                last.then_inc(pt_done, 1)

            def tran_rem(n, p):
                pe.wait_ge(pt_taken, at(pe, n * (3 * UNITS // 2) + 3 * p + 2))
                for s in range(3):
                    last = nc.tensor.transpose(PT[0:2 * REM, s * 128:(s + 1) * 128], prob[:, p % 2, s, 128:128 + 2 * REM], I[:])
                last.then_inc(pt_done, 1)

            def group_values(n, g):
                value = n * (3 * UNITS // 2) + 6 * g + 6
                if g == 0:
                    wait_all(pe, (pt_taken, value), (proj_dve, n + 1))
                elif g == 2:
                    wait_all(pe, (pt_taken, value), (ctn_ready, n * PACKS + 1))
                else:
                    wait_all(pe, (pt_taken, value))
                for a in range(2):
                    q0 = a * IMG1
                    for j in range(4):
                        mm(CT[32 * j:32 * j + 32, a * SEQ:(a + 1) * SEQ], v_main[:, a, 4 * g + j, :], ptm[:, j, q0:q0 + SEQ],
                           start=g % 2 == 0 and a == 0, stop=False, tile_position=(0, 32 * j), skip_group_check=True)
                    for j in range(4):
                        last = mm(CT[32 * j:32 * j + 32, a * SEQ:(a + 1) * SEQ], v_rem[:, a, 4 * g + j, :], ptr[:, j // 2, q0:q0 + SEQ],
                                  start=False, stop=g % 2 == 1, tile_position=(0, 32 * j), skip_group_check=True)
                if g % 2:
                    last.then_inc(pv_done, 1)

            def group_divisors(n, g):
                wait_all(pe, (rsx_ready, n * PACKS + g + 1), (cts_ready, n * (PACKS + EA) + g + 1))
                for s in range(3):
                    last = mm(CT[:, s * 128:(s + 1) * 128], rsx[:, s, :], I[:], start=True, stop=True)
                last.then_inc(rb_done, 1)

            def out_project(n):
                pe.wait_ge(ctn_ready, at(pe, n * PACKS + PACKS))
                pe.wait_ge(sc_taken, at(pe, n * UNITS + HEADS))
                for j in range(3):
                    for g in range(PACKS):
                        last = mm(S_BANKS[j // 2][0:TT, (j % 2) * D:(j % 2 + 1) * D], ctn[:, g, j * TT:(j + 1) * TT], wo[:, g, :],
                                  start=g == 0, stop=g == PACKS - 1)
                last.then_inc(oproj_done, 1)

            def expert_up(m, e):
                if e == 0:
                    wait_all(pe, (fgT_ready, m * 2 + 2))
                else:
                    wait_all(pe, (relu_ready, m * EF + e))
                for k in range(HALF):
                    mm(HB[:, 0:PAIR], w1[:, e, k, :], x2T[:, k, :], start=k == 0, stop=k == 1)
                if e:
                    wait_all(pe, (gated_ready, m * EF + e))
                mm(GB[:, 0:PAIR], pick[:, e, :], partsT[:, :], start=True, stop=True).then_inc(up_done, 1)

            def gate_rows(m):
                pe.wait_ge(fgates_ready, at(pe, m + 1))
                for j in range(3):
                    last = nc.tensor.transpose(HB[0:EF, j * TT:(j + 1) * TT], gates_f[:, j, :], I[0:TT, 0:TT])
                last.then_inc(fg_tran, 1)
                for j in range(3):
                    last = nc.tensor.transpose(GB[0:3 * EF, j * TT:(j + 1) * TT], gparts[:, j, :, :].rearrange("p a e -> p (a e)"), I[0:TT, 0:TT])
                last.then_inc(fg_tran, 1)

            def into_tiles(first, last_, lhs, rhs, seq_start):
                for j in range(3):
                    i = mm(ACC[j // 2][0:TT, (j % 2) * D:(j % 2 + 1) * D], lhs(j), rhs,
                           start=seq_start and j != 1, stop=last_, skip_group_check=True)
                return i

            def expert_down(m, e):
                if e == 0:
                    into_tiles(True, False, lambda j: gatesT_f[:, j * TT:(j + 1) * TT], b2[:, :], True)
                pe.wait_ge(gated_ready, at(pe, m * EF + e + 1))
                into_tiles(False, e == EF - 1, lambda j: hg[:, e % 2, j * TT:(j + 1) * TT], w2[:, e, :], False).then_inc(down_done, 1)

            def latent_attention(n, m):
                e = 0
                for h in range(HEAD_STEPS):
                    if m is not None and h in EXPERT_STEPS and h >= HEADS:
                        expert_up(m, e)
                        if e:
                            expert_down(m, e - 1)
                        e += 1
                    if h % 2 == 0 and h >= 4:
                        tran_rem(n, (h - 4) // 2)
                    if h == 0:
                        latent_values(n, 0)
                    if h < HEADS:
                        head_scores(n, h)
                    if h == 1:
                        latent_values(n, 1)
                    if h in (11, 19):
                        group_divisors(n, h // 8 - 1)
                    if h >= 6 and h % 4 == 2:
                        group_values(n, (h - 6) // 4)
                    if 2 <= h < HEADS + 2:
                        tran_main(n, h - 2)
                    if h == GATE_STEP and m is not None:
                        gate_rows(m)
                    if m is not None and h in EXPERT_STEPS and h < HEADS:
                        expert_up(m, e)
                        if e:
                            expert_down(m, e - 1)
                        e += 1
                if m is not None:
                    expert_up(m, e)
                    expert_down(m, e - 1)
                out_project(n)
                if m is not None:
                    for e in range(len(EXPERT_STEPS) + 1, EF):
                        expert_up(m, e)
                        expert_down(m, e - 1)

            def expert_scores(n, x):
                for s, row, col, rows, a in SLOTS:
                    last = mm(S_BANKS[x % 2][row:row + rows, s * SEQ:(s + 1) * SEQ], qm[:, x, col:col + rows], kmT[:, a * SEQ:(a + 1) * SEQ],
                              start=True, stop=True, tile_position=(0, row))
                last.then_inc(sc_done, 1)

            def values(n):
                for b in range(2):
                    for a in range(2):
                        k0 = a * SEQ + b * REM
                        for k in range(HALF):
                            last = mm(GB[:, (2 * b + a) * 128:(2 * b + a + 1) * 128], x1T[:, k, k0:k0 + 128], vw[:, k, :], start=k == 0, stop=k == 1)
                last.then_inc(mk_done, 1)
                pe.wait_ge(x1r_ready, at(pe, n * HALF + 2))
                for a in range(2):
                    for k in range(HALF):
                        last = mm(HB[0:2 * REM, a * 128:(a + 1) * 128], x1R[:, k, a, :], vw[:, k, :], start=k == 0, stop=k == 1)
                last.then_inc(mk_done, 1)

            def mixture_of_attention(n, m, more):
                pe.wait_ge(h_free, at(pe, n + 1))
                transposes(n, 0)
                if m is not None:
                    expert_down(m, EF - 1)
                pe.wait_ge(feat_ready, at(pe, n * FEAT + 2))
                for k in range(HALF):
                    last = mm(HB[:, 0:PAIR], kw[:, k, :], x1T[:, k, :], start=k == 0, stop=k == 1)
                last.then_inc(mk_done, 1)
                for s, row, col, rows, a in SLOTS:
                    for k in range(HALF):
                        last = mm(PT[row:row + rows, s * EA:(s + 1) * EA], x1T[:, k, col:col + rows], gatew[:, k, :], start=k == 0, stop=k == 1, tile_position=(0, row))
                last.then_inc(mk_done, 1)
                for e in range(EA + 1):
                    if e < EA:
                        if e == 0:
                            pe.wait_ge(mk_act, at(pe, n + 1))
                        elif e >= 2:
                            pe.wait_ge(q_ready, at(pe, n * EA + e - 1))
                        for k in range(HALF):
                            last = mm((HB, GB)[e % 2][:, 0:PAIR], qw[:, e, k, :], x1T[:, k, :], start=k == 0, stop=k == 1)
                        last.then_inc(q_done, 1)
                    if e >= 1:
                        x = e - 1
                        if x >= 2:
                            wait_all(pe, (q_ready, n * EA + x + 1), (rel_mid, n * EA + x - 1))
                        elif x == 1:
                            wait_all(pe, (q_ready, n * EA + x + 1), (mk_dve, n * 3 + 1))
                        else:
                            pe.wait_ge(q_ready, at(pe, n * EA + x + 1))
                        for s, row, col, rows, a in SLOTS:
                            last = mm((CT, PT)[x % 2][row:row + rows, s * REL:(s + 1) * REL], qm[:, x, col:col + rows], relT[:, :],
                                      start=True, stop=True, tile_position=(0, row))
                        last.then_inc(rel_done, 1)
                    if e == 4:
                        if m is not None:
                            wait_all(pe, (gates_ready, n + 1), (y_ready, m + 1))
                        else:
                            pe.wait_ge(gates_ready, at(pe, n + 1))
                        for s in range(3):
                            last = nc.tensor.transpose(ACC[1][0:EA, s * 128:(s + 1) * 128], gates_a[:, s, :], I[:])
                        last.then_inc(gates_tran, 1)
                    if e in (FIRST_SCORES, FIRST_SCORES + 1):
                        expert_scores(n, e - FIRST_SCORES)
                pe.wait_ge(sc_taken, at(pe, n * UNITS + HEADS + 1))
                expert_scores(n, 2)
                values(n)
                pe.wait_ge(sc_taken, at(pe, n * UNITS + HEADS + 2))
                expert_scores(n, 3)
                pe.wait_ge(rel_mid, at(pe, n * EA + EA))
                for x in range(2, EA + 5):
                    if 4 <= x < EA:
                        pe.wait_ge(sc_taken, at(pe, n * UNITS + HEADS + x - 1))
                        expert_scores(n, x)
                    if x == 3:
                        pe.wait_ge(gatesT_ready, at(pe, n + 1))
                        into_tiles(True, False, lambda j: gatesT_a[:, j * TT:(j + 1) * TT], ob[:, :], True)
                    if x % 2 == 0 and 4 <= x < EA + 4:
                        tran_rem(n, (HEADS + x - 4) // 2)
                    if 2 <= x < EA + 2:
                        tran_main(n, HEADS + x - 2)
                    base = n * (PACKS + EA) + PACKS
                    if 4 <= x < EA + 4:
                        e = x - 4
                        p = (HEADS + e) // 2
                        if e >= 2:
                            wait_all(pe, (pt_taken, n * (3 * UNITS // 2) + 3 * p + 3), (cts_ready, base + e - 1))
                        else:
                            wait_all(pe, (pt_taken, n * (3 * UNITS // 2) + 3 * p + 3), (mk_dve, n * 3 + 3))
                        for a in range(2):
                            q0 = a * IMG1
                            bank = (CT, HB)[e % 2]
                            mm(bank[:, a * SEQ:(a + 1) * SEQ], vm[:, e % 2, a, :], ptm[:, e % 4, q0:q0 + SEQ], start=True, stop=False)
                            last = mm(bank[:, a * SEQ:(a + 1) * SEQ], vmr[:, e % 2, a, :], ptr[:, p % 2, q0:q0 + SEQ], start=False, stop=True)
                        last.then_inc(pv_done, 1)
                    if more and x in (6, 7):
                        early_transposes(n + 1, x - 6)
                    if x >= 5:
                        e = x - 5
                        pe.wait_ge(cts_ready, at(pe, base + e + 1))
                        last = into_tiles(False, e == EA - 1, lambda j: cm[:, e % 2, j * TT:(j + 1) * TT], ow[:, e, :], False)
                last.then_inc(moa_done, 1)
                if more:
                    project(n + 1, 0)
                    project(n + 1, 1)
                transposes(n, 1)
                if more:
                    project(n + 1, 2, n)
                else:
                    for j in range(3):
                        gate_logits(n, j)

            early_transposes(0, 0)
            early_transposes(0, 1)
            for part in range(3):
                project(0, part)
            latent_attention(0, None)
            mixture_of_attention(0, None, True)
            with pe.Fori(0, pairs - 2) as n:
                latent_attention(n + 1, n)
                mixture_of_attention(n + 1, n, True)
            latent_attention(pairs - 1, pairs - 2)
            mixture_of_attention(pairs - 1, pairs - 2, False)
            gate_rows(pairs - 1)
            expert_up(pairs - 1, 0)
            for e in range(1, EF):
                expert_up(pairs - 1, e)
                expert_down(pairs - 1, e - 1)
            expert_down(pairs - 1, EF - 1)


LOADS = 16 * 8


def constants():
    import numpy as np
    f = np.float32
    c = {"ident": np.eye(128, dtype=f)}
    y, x = np.meshgrid(np.arange(GRID), np.arange(GRID), indexing="ij")
    omega = np.arange(D // 4, dtype=f) / f(D // 4 - 1)
    omega = (f(1.0) / np.power(f(10000.0), omega)).astype(f)
    y = y.reshape(-1)[:, None].astype(f) * omega[None]
    x = x.reshape(-1)[:, None].astype(f) * omega[None]
    pe = np.concatenate((np.sin(x), np.cos(x), np.sin(y), np.cos(y)), axis=1).astype(f)
    c["pe"] = np.ascontiguousarray(np.tile(pe.reshape(GRID, GRID, D), (16, 1, 1)))
    k = np.arange(SEQ, dtype=f)
    dec = np.ones((128, 3, SEQ), f)
    for s, row, col, rows, a in SLOTS:
        q = np.arange(rows) + col - a * SEQ
        q = np.clip(q, 0, SEQ - 1).astype(f)
        dec[row:row + rows, s] = np.exp(f(-0.01) * np.abs(q[:, None] - k[None])) / f(16.0)
    c["decay"] = dec
    top = (np.arange(2 * REM) < REM)
    even = (np.arange(HEADS) % 2 == 0)
    c["mask_rows"] = np.ascontiguousarray(np.repeat((top[:, None] == even[None])[:, :, None], HD, 2).astype(f))
    c["mask_cols"] = np.stack([top, ~top], 1).astype(f)
    c["iota"] = np.tile(np.arange(EF, dtype=f), (128, 1))
    pick = np.zeros((3, EF, EF, 128), f)
    for e in range(EF):
        pick[:, e, e] = 1
    c["pick"] = pick.reshape(3 * EF, EF, 128)
    return c


def kernel(**inputs):
    import numpy as np
    import concourse.bacc as bacc
    from concourse.bass_utils import run_bass_kernel_spmd

    nc = bacc.Bacc("TRN2", target_bir_lowering=False, num_devices=1)
    arrays, aps = {}, {}
    for name, a in {**inputs, **constants()}.items():
        a = np.ascontiguousarray(a)
        arrays[f"in_{name}"] = a
        aps[name] = nc.dram_tensor(f"in_{name}", a.shape, mybir.dt.from_np(a.dtype), kind="ExternalInput").ap()
    shape = (inputs["x"].shape[0], SEQ, D)
    out = nc.dram_tensor("out", shape, F32, kind="ExternalOutput").ap()
    early_fusion(nc, aps, out)
    r = run_bass_kernel_spmd(nc, [arrays], core_ids=[0])
    return r.results[0]["out"]
```
